# Optimizing a Trainium2 kernel written in Bass

```python
import numpy as np
import jax
import jax.numpy as jnp

def _softmax(x, axis=-1):
    return jax.nn.softmax(x, axis=axis)

def _gelu(x):
    return jax.nn.gelu(x, approximate=True)

def _silu(x):
    return jax.nn.silu(x)

def _sigmoid(x):
    return jax.nn.sigmoid(x)

def _layernorm(x, axis=-1, eps=1e-05):
    m = jnp.mean(x, axis=axis, keepdims=True)
    v = jnp.var(x, axis=axis, keepdims=True)
    return (x - m) / jnp.sqrt(v + eps)

def _scatter_add(tgt, idx, src, axis=0):
    return tgt.at[idx].add(src)

def _segment_sum(src, seg, n):
    return jax.ops.segment_sum(src, seg, n)
kernel_name = 'mk_perceiver_d2_seqx_r2_6d8007'

def setup_inputs(seed: int=0):
    np.random.seed(seed)
    _w = jnp.asarray

    def _rec_inputs():
        import jax
        import jax.numpy as jnp
        _rk = jax.random.key(seed)
        x = -0.0003929 + 0.9999 * jax.random.normal(jax.random.fold_in(_rk, 1), (32, 32, 512), jnp.float32)
        _lenS = 32 - jax.random.randint(jax.random.fold_in(_rk, 7), (32,), 0, max(1, 32 // 4) + 1, jnp.int32)
        _lenS2 = 257 - jax.random.randint(jax.random.fold_in(_rk, 8), (32,), 0, max(1, 257 // 4) + 1, jnp.int32)
        _ctx_1024P = jax.random.normal(jax.random.fold_in(_rk, 11), (32, 16, 512), jnp.float32)
        _ctx_1024c = jax.random.dirichlet(jax.random.fold_in(_rk, 511), 0.3 * jnp.ones((16,), jnp.float32), (32, 257))
        _ctx_1024t = jnp.einsum('bsk,bkd->bsd', _ctx_1024c, _ctx_1024P)
        _ctx_1024t = _ctx_1024t * jax.lax.rsqrt(jnp.mean(jnp.square(_ctx_1024t)) + 1e-12) * 0.953939
        ctx_1024 = 2.81802e-05 + 1.00001 * (_ctx_1024t + 0.3 * jax.random.normal(jax.random.fold_in(_rk, 611), (32, 257, 512), jnp.float32))
        return (x, ctx_1024)
    x, ctx_1024 = _rec_inputs()

    def _L0_xattn_setup():
        import jax, jax.numpy as jnp
        import numpy as np
        EMBED = 512
        B, I, J = (8, 1024, 1024)
        SCALE = EMBED ** (-0.5)
        key = jax.random.key(seed)
        ks = jax.random.split(key, 5)
        s = EMBED ** (-0.5)
        return {'q_in': jax.random.normal(ks[0], (B, I, EMBED), dtype=jnp.float32), 'k_v': jax.random.normal(ks[1], (B, J, EMBED), dtype=jnp.float32), 'Wq': jax.random.normal(ks[2], (EMBED, EMBED), dtype=jnp.float32) * s, 'bq': jnp.zeros((EMBED,), dtype=jnp.float32), 'Wk': jax.random.normal(ks[3], (EMBED, EMBED), dtype=jnp.float32) * s, 'bk': jnp.zeros((EMBED,), dtype=jnp.float32), 'Wv': jax.random.normal(ks[4], (EMBED, EMBED), dtype=jnp.float32) * s, 'bv': jnp.zeros((EMBED,), dtype=jnp.float32)}
    _L0_xattn_all = _L0_xattn_setup()
    _L0_xattn_in = {k: v for k, v in _L0_xattn_all.items() if k in ('Wq', 'bq', 'Wk', 'bk', 'Wv', 'bv')}
    del _L0_xattn_all

    def _L0_attn_setup():
        import jax, jax.numpy as jnp
        import numpy as np
        DIM = 512
        HEADS = 16
        DIM_HEAD = 64
        INNER = HEADS * DIM_HEAD

        def _attention(x, ln_gamma, ln_beta, w_qkv, w_out, b_out):
            b, n, _ = x.shape
            scale = DIM_HEAD ** (-0.5)
            mu = jnp.mean(x, axis=-1, keepdims=True)
            var = jnp.var(x, axis=-1, keepdims=True)
            xn = (x - mu) / jnp.sqrt(var + 1e-05) * ln_gamma + ln_beta
            qkv = jnp.einsum('bnd,ed->bne', xn, w_qkv)
            q, k, v = jnp.split(qkv, 3, axis=-1)
            reshape = lambda t: t.reshape(b, n, HEADS, DIM_HEAD).transpose(0, 2, 1, 3)
            q, k, v = (reshape(q) * scale, reshape(k), reshape(v))
            sim = jnp.einsum('bhid,bhjd->bhij', q, k)
            mask_value = -jnp.finfo(sim.dtype).max
            causal = jnp.triu(jnp.ones((n, n), dtype=bool), k=1)
            sim = jnp.where(causal, mask_value, sim)
            sim = sim - jax.lax.stop_gradient(jnp.max(sim, axis=-1, keepdims=True))
            attn = jax.nn.softmax(sim, axis=-1)
            out = jnp.einsum('bhij,bhjd->bhid', attn, v)
            out = out.transpose(0, 2, 1, 3).reshape(b, n, INNER)
            return jnp.einsum('bne,de->bnd', out, w_out) + b_out
        key = jax.random.key(seed)
        ks = jax.random.split(key, 6)
        x = jax.random.normal(ks[0], (2, 1024, DIM), dtype=jnp.float32)
        ln_gamma = jnp.ones((DIM,), dtype=jnp.float32)
        ln_beta = jnp.zeros((DIM,), dtype=jnp.float32)
        w_qkv = jax.random.normal(ks[1], (3 * INNER, DIM), dtype=jnp.float32) * DIM ** (-0.5)
        w_out = jax.random.normal(ks[2], (DIM, INNER), dtype=jnp.float32) * INNER ** (-0.5)
        b_out = jax.random.normal(ks[3], (DIM,), dtype=jnp.float32) * 0.02
        return {'x': x, 'ln_gamma': ln_gamma, 'ln_beta': ln_beta, 'w_qkv': w_qkv, 'w_out': w_out, 'b_out': b_out}
    _L0_attn_all = _L0_attn_setup()
    _L0_attn_in = {k: v for k, v in _L0_attn_all.items() if k in ('ln_gamma', 'ln_beta', 'w_qkv', 'w_out', 'b_out')}
    del _L0_attn_all

    def _L0_ffn_setup():
        import jax, jax.numpy as jnp
        import numpy as np
        DIM = 512
        INTER = 256
        E = 16
        TOPK = 4
        N_GROUPS = 4
        TOPK_GROUPS = 2
        ROUTE_SCALE = 1.0
        INIT_STD = 0.02
        B, S = (2, 512)
        key = jax.random.key(seed)
        ks = jax.random.split(key, 8)
        return {'x': jax.random.normal(ks[0], (B, S, DIM), jnp.float32), 'gate_w': jax.random.normal(ks[1], (E, DIM), jnp.float32) * INIT_STD, 'gate_bias': jnp.zeros((E,), jnp.float32), 'w1': jax.random.normal(ks[2], (E, INTER, DIM), jnp.float32) * INIT_STD, 'w2': jax.random.normal(ks[3], (E, DIM, INTER), jnp.float32) * INIT_STD, 'w3': jax.random.normal(ks[4], (E, INTER, DIM), jnp.float32) * INIT_STD, 'ws1': jax.random.normal(ks[5], (INTER, DIM), jnp.float32) * INIT_STD, 'ws2': jax.random.normal(ks[6], (DIM, INTER), jnp.float32) * INIT_STD, 'ws3': jax.random.normal(ks[7], (INTER, DIM), jnp.float32) * INIT_STD}
    _L0_ffn_all = _L0_ffn_setup()
    _L0_ffn_in = {k: v for k, v in _L0_ffn_all.items() if k in ('gate_w', 'gate_bias', 'w1', 'w2', 'w3', 'ws1', 'ws2', 'ws3')}
    del _L0_ffn_all

    def _L1_xattn_setup():
        import jax, jax.numpy as jnp
        import numpy as np
        D_MODEL = 512
        N_HEADS = 16
        D_K = D_MODEL // N_HEADS
        key = jax.random.key(seed)
        ks = jax.random.split(key, 11)
        B, L, S = (2, 1024, 1024)
        scale = 1.0 / np.sqrt(D_MODEL)
        return {'x_q': jax.random.normal(ks[0], (B, L, D_MODEL), jnp.float32), 'x_k': jax.random.normal(ks[1], (B, S, D_MODEL), jnp.float32), 'x_v': jax.random.normal(ks[2], (B, S, D_MODEL), jnp.float32), 'W_Q': jax.random.normal(ks[3], (D_MODEL, D_MODEL), jnp.float32) * scale, 'b_Q': jax.random.normal(ks[4], (D_MODEL,), jnp.float32) * 0.01, 'W_K': jax.random.normal(ks[5], (D_MODEL, D_MODEL), jnp.float32) * scale, 'b_K': jax.random.normal(ks[6], (D_MODEL,), jnp.float32) * 0.01, 'W_V': jax.random.normal(ks[7], (D_MODEL, D_MODEL), jnp.float32) * scale, 'b_V': jax.random.normal(ks[8], (D_MODEL,), jnp.float32) * 0.01, 'W_O': jax.random.normal(ks[9], (D_MODEL, D_MODEL), jnp.float32) * scale, 'b_O': jax.random.normal(ks[10], (D_MODEL,), jnp.float32) * 0.01}
    _L1_xattn_all = _L1_xattn_setup()
    _L1_xattn_in = {k: v for k, v in _L1_xattn_all.items() if k in ('W_Q', 'b_Q', 'W_K', 'b_K', 'W_V', 'b_V', 'W_O', 'b_O')}
    del _L1_xattn_all

    def _L1_attn_setup():
        import jax, jax.numpy as jnp
        import numpy as np
        N_HEAD = 16
        D_K = 64
        D_V = 64
        EMBED = 512
        BATCH = 4
        SEQ = 1024
        key = jax.random.key(seed)
        ks = jax.random.split(key, 12)
        s = lambda d: 1.0 / np.sqrt(d)
        u = lambda k, shape, d: jax.random.uniform(k, shape, jnp.float32, -s(d), s(d))
        return {'z': jax.random.normal(ks[0], (BATCH, SEQ, EMBED), jnp.float32), 'wq': u(ks[1], (EMBED, D_K), D_K), 'wk': u(ks[2], (EMBED, D_K), D_K), 'wv': u(ks[3], (EMBED, D_V), D_V), 'fcq_w': u(ks[4], (D_K, N_HEAD * D_K), D_K), 'fcq_b': u(ks[5], (N_HEAD * D_K,), N_HEAD * D_K), 'fck_w': u(ks[6], (D_K, N_HEAD * D_K), D_K), 'fck_b': u(ks[7], (N_HEAD * D_K,), N_HEAD * D_K), 'fcv_w': u(ks[8], (D_V, N_HEAD * D_V), D_V), 'fcv_b': u(ks[9], (N_HEAD * D_V,), N_HEAD * D_V), 'fco_w': u(ks[10], (N_HEAD * D_V, EMBED), EMBED), 'fco_b': u(ks[11], (EMBED,), EMBED)}
    _L1_attn_all = _L1_attn_setup()
    _L1_attn_in = {k: v for k, v in _L1_attn_all.items() if k in ('wq', 'wk', 'wv', 'fcq_w', 'fcq_b', 'fck_w', 'fck_b', 'fcv_w', 'fcv_b', 'fco_w', 'fco_b')}
    del _L1_attn_all

    def _L1_ffn_setup():
        import jax, jax.numpy as jnp
        import numpy as np
        TOP_K = 2
        key = jax.random.key(seed)
        k1, k2, k3, k4 = jax.random.split(key, 4)
        B, T, D, H, E = (2, 1024, 512, 1024, 8)
        x = jax.random.normal(k1, (B, T, D), dtype=jnp.float32)
        w12 = jax.random.normal(k2, (E, 2 * H, D), dtype=jnp.float32) * D ** (-0.5)
        w3 = jax.random.normal(k3, (E, D, H), dtype=jnp.float32) * H ** (-0.5)
        gate_w = jax.random.normal(k4, (E, D), dtype=jnp.float32) * D ** (-0.5)
        return {'x': x, 'w12': w12, 'w3': w3, 'gate_w': gate_w}
    _L1_ffn_all = _L1_ffn_setup()
    _L1_ffn_in = {k: v for k, v in _L1_ffn_all.items() if k in ('w12', 'w3', 'gate_w')}
    del _L1_ffn_all
    return {'x': x, 'ctx_1024': ctx_1024, 'L0_xattn_Wq': _L0_xattn_in['Wq'], 'L0_xattn_bq': _L0_xattn_in['bq'], 'L0_xattn_Wk': _L0_xattn_in['Wk'], 'L0_xattn_bk': _L0_xattn_in['bk'], 'L0_xattn_Wv': _L0_xattn_in['Wv'], 'L0_xattn_bv': _L0_xattn_in['bv'], 'L0_attn_ln_gamma': _L0_attn_in['ln_gamma'], 'L0_attn_ln_beta': _L0_attn_in['ln_beta'], 'L0_attn_w_qkv': _L0_attn_in['w_qkv'], 'L0_attn_w_out': _L0_attn_in['w_out'], 'L0_attn_b_out': _L0_attn_in['b_out'], 'L0_ffn_gate_w': _L0_ffn_in['gate_w'], 'L0_ffn_gate_bias': _L0_ffn_in['gate_bias'], 'L0_ffn_w1': _L0_ffn_in['w1'], 'L0_ffn_w2': _L0_ffn_in['w2'], 'L0_ffn_w3': _L0_ffn_in['w3'], 'L0_ffn_ws1': _L0_ffn_in['ws1'], 'L0_ffn_ws2': _L0_ffn_in['ws2'], 'L0_ffn_ws3': _L0_ffn_in['ws3'], 'L1_xattn_W_Q': _L1_xattn_in['W_Q'], 'L1_xattn_b_Q': _L1_xattn_in['b_Q'], 'L1_xattn_W_K': _L1_xattn_in['W_K'], 'L1_xattn_b_K': _L1_xattn_in['b_K'], 'L1_xattn_W_V': _L1_xattn_in['W_V'], 'L1_xattn_b_V': _L1_xattn_in['b_V'], 'L1_xattn_W_O': _L1_xattn_in['W_O'], 'L1_xattn_b_O': _L1_xattn_in['b_O'], 'L1_attn_wq': _L1_attn_in['wq'], 'L1_attn_wk': _L1_attn_in['wk'], 'L1_attn_wv': _L1_attn_in['wv'], 'L1_attn_fcq_w': _L1_attn_in['fcq_w'], 'L1_attn_fcq_b': _L1_attn_in['fcq_b'], 'L1_attn_fck_w': _L1_attn_in['fck_w'], 'L1_attn_fck_b': _L1_attn_in['fck_b'], 'L1_attn_fcv_w': _L1_attn_in['fcv_w'], 'L1_attn_fcv_b': _L1_attn_in['fcv_b'], 'L1_attn_fco_w': _L1_attn_in['fco_w'], 'L1_attn_fco_b': _L1_attn_in['fco_b'], 'L1_ffn_w12': _L1_ffn_in['w12'], 'L1_ffn_w3': _L1_ffn_in['w3'], 'L1_ffn_gate_w': _L1_ffn_in['gate_w']}

def reference(x, ctx_1024, L0_xattn_Wq, L0_xattn_bq, L0_xattn_Wk, L0_xattn_bk, L0_xattn_Wv, L0_xattn_bv, L0_attn_ln_gamma, L0_attn_ln_beta, L0_attn_w_qkv, L0_attn_w_out, L0_attn_b_out, L0_ffn_gate_w, L0_ffn_gate_bias, L0_ffn_w1, L0_ffn_w2, L0_ffn_w3, L0_ffn_ws1, L0_ffn_ws2, L0_ffn_ws3, L1_xattn_W_Q, L1_xattn_b_Q, L1_xattn_W_K, L1_xattn_b_K, L1_xattn_W_V, L1_xattn_b_V, L1_xattn_W_O, L1_xattn_b_O, L1_attn_wq, L1_attn_wk, L1_attn_wv, L1_attn_fcq_w, L1_attn_fcq_b, L1_attn_fck_w, L1_attn_fck_b, L1_attn_fcv_w, L1_attn_fcv_b, L1_attn_fco_w, L1_attn_fco_b, L1_ffn_w12, L1_ffn_w3, L1_ffn_gate_w):
    import jax
    import jax.numpy as jnp

    def _L0_xattn_ref(q_in, k_v, Wq, bq, Wk, bk, Wv, bv):
        import jax, jax.numpy as jnp
        import numpy as np
        EMBED = 512
        B, I, J = (8, 1024, 1024)
        SCALE = EMBED ** (-0.5)
        q = q_in @ Wq + bq
        k = k_v @ Wk + bk
        v = k_v @ Wv + bv
        sim = jnp.einsum('bid,bjd->bij', q, k) * SCALE
        attn = jax.nn.softmax(sim, axis=-1)
        out = jnp.einsum('bij,bjd->bid', attn, v)
        return out

    def _L0_attn_ref(x, ln_gamma, ln_beta, w_qkv, w_out, b_out):
        import jax, jax.numpy as jnp
        import numpy as np
        DIM = 512
        HEADS = 16
        DIM_HEAD = 64
        INNER = HEADS * DIM_HEAD

        def _attention(x, ln_gamma, ln_beta, w_qkv, w_out, b_out):
            b, n, _ = x.shape
            scale = DIM_HEAD ** (-0.5)
            mu = jnp.mean(x, axis=-1, keepdims=True)
            var = jnp.var(x, axis=-1, keepdims=True)
            xn = (x - mu) / jnp.sqrt(var + 1e-05) * ln_gamma + ln_beta
            qkv = jnp.einsum('bnd,ed->bne', xn, w_qkv)
            q, k, v = jnp.split(qkv, 3, axis=-1)
            reshape = lambda t: t.reshape(b, n, HEADS, DIM_HEAD).transpose(0, 2, 1, 3)
            q, k, v = (reshape(q) * scale, reshape(k), reshape(v))
            sim = jnp.einsum('bhid,bhjd->bhij', q, k)
            mask_value = -jnp.finfo(sim.dtype).max
            causal = jnp.triu(jnp.ones((n, n), dtype=bool), k=1)
            sim = jnp.where(causal, mask_value, sim)
            sim = sim - jax.lax.stop_gradient(jnp.max(sim, axis=-1, keepdims=True))
            attn = jax.nn.softmax(sim, axis=-1)
            out = jnp.einsum('bhij,bhjd->bhid', attn, v)
            out = out.transpose(0, 2, 1, 3).reshape(b, n, INNER)
            return jnp.einsum('bne,de->bnd', out, w_out) + b_out
        return _attention(x, ln_gamma, ln_beta, w_qkv, w_out, b_out)

    def _L0_ffn_ref(x, gate_w, gate_bias, w1, w2, w3, ws1, ws2, ws3):
        import jax, jax.numpy as jnp
        import numpy as np
        DIM = 512
        INTER = 256
        E = 16
        TOPK = 4
        N_GROUPS = 4
        TOPK_GROUPS = 2
        ROUTE_SCALE = 1.0
        INIT_STD = 0.02
        B, S = (2, 512)
        Bx, Sx, D = x.shape
        T = Bx * Sx
        xf = x.reshape(T, D)
        scores = jax.nn.sigmoid(xf @ gate_w.T)
        original_scores = scores
        s = scores + gate_bias
        sg = s.reshape(T, N_GROUPS, E // N_GROUPS)
        group_scores = sg.max(axis=-1)
        _, gidx = jax.lax.top_k(group_scores, TOPK_GROUPS)
        keep = jnp.zeros((T, N_GROUPS), bool).at[jnp.arange(T)[:, None], gidx].set(True)
        s_masked = jnp.where(keep[:, :, None], sg, -jnp.inf).reshape(T, E)
        _, idx = jax.lax.top_k(s_masked, TOPK)
        weights = jnp.take_along_axis(original_scores, idx, axis=1) * ROUTE_SCALE
        comb = jnp.zeros((T, E), x.dtype).at[jnp.arange(T)[:, None], idx].add(weights)
        h1 = jnp.einsum('td,eid->tei', xf, w1)
        h3 = jnp.einsum('td,eid->tei', xf, w3)
        h = jax.nn.silu(h1) * h3
        y = jnp.einsum('tei,edi,te->td', h, w2, comb)
        z = jax.nn.silu(xf @ ws1.T) * (xf @ ws3.T) @ ws2.T
        return (y + z).reshape(Bx, Sx, D)

    def _L1_xattn_ref(x_q, x_k, x_v, W_Q, b_Q, W_K, b_K, W_V, b_V, W_O, b_O):
        import jax, jax.numpy as jnp
        import numpy as np
        D_MODEL = 512
        N_HEADS = 16
        D_K = D_MODEL // N_HEADS
        B, L, _ = x_q.shape
        S = x_k.shape[1]
        H, dk = (N_HEADS, D_K)
        Q = (x_q @ W_Q + b_Q).reshape(B, L, H, dk).transpose(0, 2, 1, 3)
        K = (x_k @ W_K + b_K).reshape(B, S, H, dk).transpose(0, 2, 1, 3)
        V = (x_v @ W_V + b_V).reshape(B, S, H, dk).transpose(0, 2, 1, 3)
        scores = jnp.einsum('bhld,bhsd->bhls', Q, K) / jnp.sqrt(jnp.float32(dk))
        attn = jax.nn.softmax(scores, axis=-1)
        ctx = jnp.einsum('bhls,bhsd->bhld', attn, V)
        ctx = ctx.transpose(0, 2, 1, 3).reshape(B, L, H * dk)
        out = ctx @ W_O + b_O
        return out

    def _L1_attn_ref(z, wq, wk, wv, fcq_w, fcq_b, fck_w, fck_b, fcv_w, fcv_b, fco_w, fco_b):
        import jax, jax.numpy as jnp
        import numpy as np
        N_HEAD = 16
        D_K = 64
        D_V = 64
        EMBED = 512
        BATCH = 4
        SEQ = 1024
        b, n, _ = z.shape
        scale = jnp.sqrt(jnp.float32(D_K))
        q = z @ wq @ fcq_w + fcq_b
        k = z @ wk @ fck_w + fck_b
        v = z @ wv @ fcv_w + fcv_b
        q = q.reshape(b, n, N_HEAD, D_K)
        k = k.reshape(b, n, N_HEAD, D_K)
        v = v.reshape(b, n, N_HEAD, D_V)
        scores = jnp.einsum('bihd,bjhd->bhij', q, k) / scale
        attn = jax.nn.softmax(scores, axis=-1)
        out = jnp.einsum('bhij,bjhd->bihd', attn, v)
        out = out.reshape(b, n, N_HEAD * D_V)
        return out @ fco_w + fco_b

    def _L1_ffn_ref(x, w12, w3, gate_w):
        import jax, jax.numpy as jnp
        import numpy as np
        TOP_K = 2
        E = gate_w.shape[0]
        H = w3.shape[-1]
        scores = jnp.einsum('btd,ed->bte', x, gate_w)
        topk_scores, topk_idx = jax.lax.top_k(scores, TOP_K)
        topk_probs = jax.nn.softmax(topk_scores, axis=-1)
        total_probs = jnp.sum(jax.nn.one_hot(topk_idx, E, dtype=topk_probs.dtype) * topk_probs[..., None], axis=-2)
        h12 = jnp.einsum('btd,ehd->bteh', x, w12)
        h1, h2 = (h12[..., :H], h12[..., H:])
        hidden = jax.nn.silu(h1) * h2
        expert_out = jnp.einsum('bteh,edh->bted', hidden, w3)
        y = jnp.sum(total_probs[..., None] * expert_out, axis=-2)
        return y
    x = x + _L0_xattn_ref(_layernorm(x, axis=-1), ctx_1024, L0_xattn_Wq, L0_xattn_bq, L0_xattn_Wk, L0_xattn_bk, L0_xattn_Wv, L0_xattn_bv)
    x = x + _L0_attn_ref(_layernorm(x, axis=-1), L0_attn_ln_gamma, L0_attn_ln_beta, L0_attn_w_qkv, L0_attn_w_out, L0_attn_b_out)
    x = x + _L0_ffn_ref(_layernorm(x, axis=-1), L0_ffn_gate_w, L0_ffn_gate_bias, L0_ffn_w1, L0_ffn_w2, L0_ffn_w3, L0_ffn_ws1, L0_ffn_ws2, L0_ffn_ws3)
    x = x + _L1_xattn_ref(_layernorm(x, axis=-1), ctx_1024, ctx_1024, L1_xattn_W_Q, L1_xattn_b_Q, L1_xattn_W_K, L1_xattn_b_K, L1_xattn_W_V, L1_xattn_b_V, L1_xattn_W_O, L1_xattn_b_O)
    x = x + _L1_attn_ref(_layernorm(x, axis=-1), L1_attn_wq, L1_attn_wk, L1_attn_wv, L1_attn_fcq_w, L1_attn_fcq_b, L1_attn_fck_w, L1_attn_fck_b, L1_attn_fcv_w, L1_attn_fcv_b, L1_attn_fco_w, L1_attn_fco_b)
    x = x + _L1_ffn_ref(_layernorm(x, axis=-1), L1_ffn_w12, L1_ffn_w3, L1_ffn_gate_w)
    return x

_drawn_inputs = setup_inputs


def setup_inputs(seed=0):
    import zlib

    import numpy as np

    out = dict(_drawn_inputs(seed))
    spreads = {'L0_xattn_bq': (0.0, 0.1),
     'L0_xattn_bk': (0.0, 0.8),
     'L0_xattn_bv': (0.0, 0.1),
     'L0_attn_ln_gamma': (1.0, 0.2),
     'L0_attn_ln_beta': (0.0, 0.1),
     'L0_ffn_gate_bias': (0.0, 0.1)}
    factors = {'L1_xattn_b_Q': 6.214,
     'L1_xattn_b_K': 8.0,
     'L1_xattn_b_V': 2.874,
     'L1_xattn_b_O': 3.547,
     'L1_attn_fcq_b': 8.0,
     'L1_attn_fck_b': 8.0,
     'L1_attn_fcv_b': 3.399}
    for name, (base, spread) in spreads.items():
        noise = np.random.default_rng([zlib.crc32(name.encode()), seed]).standard_normal(out[name].shape)
        drawn = base * np.exp(spread * noise) if base else spread * noise
        out[name] = jnp.asarray(drawn.astype(out[name].dtype))
    for name, factor in factors.items():
        out[name] = (out[name] * factor).astype(out[name].dtype)
    return out
```

```python
from contextlib import ExitStack

import numpy as np
import concourse.bass as bass
from concourse import mybir

F32 = mybir.dt.float32
F32R = mybir.dt.float32r
U32 = mybir.dt.uint32
ALU = mybir.AluOpType
ACT = mybir.ActivationFunctionType
AX_X = mybir.AxisListType.X

P = 128
B, NQ, D = 32, 32, 512
S = 257
SE = 258
T = B * NQ
NT = T // P
SEQ = P // NQ
DC = D // P
HALF = 512
NHALF = T // HALF
DH = 64
HH = 8
E0, I0, K0 = 16, 256, 4
G0, GK0 = 4, 2
E1, I1, K1 = 8, 1024, 2
XH, XD = 16, 32
UNITS0 = (E0 + 1) * I0 // P
UNITS1 = E1 * I1 // P
PAIRS = 32
LEAD = 2
FAR = 1e30
MASKED = -3.4028234663852886e38
LN_EPS = 1e-5
F_SIZE, R_SIZE = 74 * 256, 69 * 256
N_SIZE = 2304


class Links:

    def __init__(self, engine, sem):
        self.engine, self.sem, self.done, self.turn, self.k, self.per = engine, sem, 0, 0, 0, 0

    def enter(self, turn, per):
        self.turn, self.per, self.k = turn * per, per, 0

    def leave(self, turns):
        assert self.k == self.per, (self.k, self.per)
        self.done, self.turn, self.k, self.per = self.done + turns * self.per, 0, 0, 0

    def link(self, instruction):
        instruction.then_inc(self.sem, 1)
        self.k += 1
        self.engine.wait_ge(self.sem, self.turn + (self.done + self.k))
        if not self.per:
            self.done, self.k = self.done + 1, 0


class Area:

    def __init__(self, tensor, size, at=0):
        self.tensor, self.size, self.at = tensor, size, at

    def take(self, *shape):
        n = int(np.prod(shape))
        at, self.at = self.at, self.at + n + n % 2
        assert self.at <= self.size, ("arena", self.at, self.size)
        ap = self.tensor[:, at:at + n]
        if len(shape) > 1:
            names = "abcd"[:len(shape)]
            ap = ap.rearrange(f"p ({' '.join(names)}) -> p {' '.join(names)}", **dict(zip(names, shape)))
        return ap


def build(nc, d, out):
    with ExitStack() as ctx:
        def sb(name, shape, dt=F32):
            return ctx.enter_context(nc.sbuf_tensor(name, shape, dt))

        layer_sems = []

        def sem(name):
            layer_sems.append(nc.alloc_semaphore(name=name))
            return layer_sems[-1]

        def free_semaphores():
            with nc.Block() as block:
                @block.sync
                def _(eng):
                    for s in layer_sems:
                        eng.sem_clear(s)
            for s in layer_sems:
                nc.release_semaphore(s)
            layer_sems.clear()

        pe, act, dve, pool = nc.tensor, nc.scalar, nc.vector, nc.gpsimd
        x = sb("x", [P, NT, D])
        xh = sb("xh", [P, DC, T], F32R)
        xl = sb("xl", [P, DC, T], F32R)
        ident = sb("ident", [P, P])
        epst = sb("epst", [P, 1])
        stats = sb("stats", [P, NT, 6])
        moments = sb("moments", [P, NT, 2])
        rstd = sb("rstd", [P, NT])
        comb = sb("comb", [P, NT, PAIRS])
        fa = sb("fa", [P, F_SIZE])
        ra = sb("ra", [P, R_SIZE], F32R)
        na = sb("na", [P, N_SIZE])
        banks = ctx.enter_context(nc.psum_tensor("banks", [P, 8, 512], F32))
        vlast_dram = nc.dram_tensor("vlast_scratch", [B, D], F32, kind="Internal").ap()

        def mm3(psum, lh, ll, rh, rl, first=True, last=True):
            pe.matmul(psum, lh, rh, start=first, stop=False)
            pe.matmul(psum, lh, rl, start=False, stop=False)
            return pe.matmul(psum, ll, rh, start=False, stop=last)

        def chunks(ap):
            return ap.rearrange("p (c t) -> p c t", c=DC)

        s_x, s_id = sem("x_loaded"), sem("ident_made")
        with nc.Block() as block:
            @block.sync
            def _(eng):
                eng.dma_start(x[:], d["x"].rearrange("(t p) d -> p t d", p=P)).then_inc(s_x, 16)
                eng.wait_ge(s_x, 16)

            @block.gpsimd
            def _(eng):
                pool.memset(ident[:], 0.0).then_inc(s_id, 1)
                pool.memset(epst[:], LN_EPS)
                eng.wait_ge(s_id, 1)
                pool.affine_select(out=ident[:], in_=ident[:], compare_op=ALU.not_equal, fill=1.0,
                                   base=0, pattern=[[-1, P]], channel_multiplier=1)

        def layer_norm(tag, affine=None, ahead=()):
            f = Area(na, N_SIZE)
            xn = [f.take(D) for _ in range(LEAD)]
            gain, shift = f.take(D), f.take(D)
            root = f.take(NT)
            first = Area(fa, F_SIZE).take(NT, D)
            s_gain, s_stats, s_mom, s_root = (sem(f"{tag}_{n}") for n in ("gain", "statistics", "moments", "root"))
            s_xn, s_turned, s_hi, s_lo, s_links = (sem(f"{tag}_{n}") for n in ("normed", "turned", "high", "low", "links"))

            with nc.Block() as block:
                @block.sync
                def _(eng):
                    if affine:
                        eng.dma_start(gain, affine[0].partition_broadcast(P)).then_inc(s_gain, 16)
                        eng.dma_start(shift, affine[1].partition_broadcast(P)).then_inc(s_gain, 16)
                    for load, _, _ in ahead:
                        load(eng)

                @block.gpsimd
                def _(eng):
                    for _, _, low in ahead:
                        low(eng, pool, (0, 2))

                @block.vector
                def _(eng):
                    links = Links(eng, s_links)

                    def moments_of(source, k):
                        with dve.Fori(0, NT) as t:
                            dve.bn_stats(stats[:, t, :], source[:, t, :]).then_inc(s_stats, 1)
                        for t in range(NT):
                            eng.wait_ge(s_stats, NT * k + t + 1)
                            dve.bn_aggr(moments[:, t, :], stats[:, t, :]).then_inc(s_mom, 1)
                        eng.wait_ge(s_root, k + 1)
                        links.link(dve.reciprocal(rstd[:], root))

                    source = x
                    moments_of(x, 0)
                    if affine:
                        for t in range(NT):
                            ins = dve.tensor_scalar(first[:, t, :], x[:, t, :], moments[:, t, 0:1], rstd[:, t:t + 1],
                                                    ALU.subtract, ALU.mult)
                        links.link(ins)
                        source = first
                        moments_of(first, 1)
                        eng.wait_ge(s_gain, 32)

                    def normalise(n, u):
                        eng.wait_ge(s_turned, n + 1)
                        mean, r = moments[:, n, 0:1], rstd[:, bass.ds(n, 1)]
                        if affine:
                            links.link(dve.scalar_tensor_tensor(xn[u], source[:, n, :], mean, gain, ALU.subtract,
                                                                ALU.mult))
                            ins = dve.scalar_tensor_tensor(xn[u], xn[u], r, shift, ALU.mult, ALU.add)
                        else:
                            ins = dve.tensor_scalar(xn[u], source[:, n, :], mean, r, ALU.subtract, ALU.mult)
                        ins.then_inc(s_xn, 1)

                    def low_part(n, u):
                        eng.wait_ge(s_hi, n + 1)
                        dve.tensor_tensor(xl[:, :, bass.ts(n, P)], chunks(banks[:, u, :]),
                                          xh[:, :, bass.ts(n, P)].bitcast(F32), ALU.subtract).then_inc(s_lo, 1)

                    eng.sem_inc(s_lo, LEAD)
                    links.enter(0, 1 if affine else 0)
                    normalise(0, 0)
                    links.leave(1)
                    with dve.Fori(0, NT // 2 - 1) as i:
                        links.enter(i, 2 if affine else 0)
                        for u in range(2):
                            normalise(2 * i + u + 1, 1 - u)
                            low_part(2 * i + u, u)
                        links.leave(NT // 2 - 1)
                    normalise(NT - 1, 1)
                    low_part(NT - 2, 0)
                    low_part(NT - 1, 1)
                    for _, _, low in ahead:
                        low(eng, dve, (1, 3))

                @block.scalar
                def _(eng):
                    for k in range(2 if affine else 1):
                        eng.wait_ge(s_mom, NT * k + NT)
                        act.activation(root, moments[:, :, 1], ACT.Sqrt, bias=epst[:]).then_inc(s_root, 1)
                    with act.Fori(0, NT // 2) as i:
                        for u in range(LEAD):
                            n = 2 * i + u
                            eng.wait_ge(s_turned, n + 1 + LEAD)
                            act.activation(xh[:, :, bass.ts(n, P)], chunks(banks[:, u, :]),
                                           ACT.Copy).then_inc(s_hi, 1)
                    for _, high, _ in ahead:
                        high(eng)

                @block.tensor
                def _(eng):
                    eng.sem_inc(s_turned, LEAD)
                    with pe.Fori(0, NT // 2) as i:
                        for u in range(LEAD):
                            n = 2 * i + u
                            eng.wait_ge(s_xn, n + 1)
                            eng.wait_ge(s_lo, n + 1)
                            for c in range(DC):
                                ins = pe.transpose(banks[:, u, c * P:(c + 1) * P],
                                                   xn[u][:, c * P:(c + 1) * P], ident[:])
                            ins.then_inc(s_turned, 1)

        def split_programs(tag, weights, staging):
            s_ld = [sem(f"{tag}_weight{k}") for k in range(len(weights))]
            s_hi = [sem(f"{tag}_high{k}") for k in range(len(weights))]
            s_w = [sem(f"{tag}_split{k}") for k in range(len(weights))]
            slots = len(staging)

            def load(eng):
                for k, (_, _, src) in enumerate(weights):
                    if k >= slots:
                        eng.wait_ge(s_w[k - slots], 1)
                    eng.dma_start(staging[k % slots], src).then_inc(s_ld[k], 16)

            def high(eng):
                for k, (hi, _, _) in enumerate(weights):
                    eng.wait_ge(s_ld[k], 16)
                    act.activation(hi, staging[k % slots], ACT.Copy).then_inc(s_hi[k], 1)

            def low(eng, unit, which):
                for k in which:
                    if k < len(weights):
                        hi, lo, _ = weights[k]
                        eng.wait_ge(s_hi[k], 1)
                        unit.tensor_tensor(lo, staging[k % slots], hi.bitcast(F32), ALU.subtract).then_inc(s_w[k], 1)
            return load, high, low, s_w

        def columns(w):
            return w.rearrange("(c p) n -> p c n", p=P)

        def cross_one_head():
            scale = float(D) ** -0.5
            f, r = Area(fa, F_SIZE), Area(ra, R_SIZE)
            qp, bv, bk, bq, shift = f.take(DC, T), f.take(D), f.take(DC), f.take(DC), f.take(NT)
            f2 = f.at
            staging = [f.take(DC, D) for _ in range(3)]
            wv = r.take(DC, D), r.take(DC, D)
            r2 = r.at
            wq, wk = (r.take(DC, D), r.take(DC, D)), (r.take(DC, D), r.take(DC, D))
            q = [r.take(DC, HALF) for _ in range(2)]
            load, high, low, s_w = split_programs("xa", [
                (*wq, columns(d["L0_xattn_Wq"])), (*wk, columns(d["L0_xattn_WkT"])),
                (*wv, columns(d["L0_xattn_Wv"]))], staging)
            layer_norm("na", ahead=[(load, high, low)])
            s_b, s_mm, s_hi, s_out = sem("xa_biases"), sem("xa_product"), sem("xa_high"), sem("xa_taken")
            jobs = [(h, kind, c) for h in range(NHALF) for kind, c in
                    [("q", c) for c in range(DC)] + [("k", c) for c in range(DC)] + [("shift", 0)]]
            NB = 4

            with nc.Block() as block:
                @block.sync
                def _(eng):
                    eng.dma_start(bq, d["L0_xattn_bq"]).then_inc(s_b, 16)
                    eng.dma_start(bk, d["L0_xattn_bk"]).then_inc(s_b, 16)
                    eng.dma_start(bv, d["L0_xattn_bv"].partition_broadcast(P)).then_inc(s_b, 16)

                @block.scalar
                def _(eng):
                    eng.wait_ge(s_b, 48)
                    for j, (h, kind, c) in enumerate(jobs):
                        if kind != "q":
                            continue
                        eng.wait_ge(s_mm, j + 1)
                        if h:
                            eng.wait_ge(s_mm, len(jobs) // 2)
                        act.activation(q[0][:, c, :], banks[:, j % NB, :], ACT.Identity,
                                       bias=bq[:, c:c + 1]).then_inc(s_hi, 1)

                @block.vector
                def _(eng):
                    eng.wait_ge(s_b, 48)
                    highs = 0
                    for j, (h, kind, c) in enumerate(jobs):
                        bank = banks[:, j % NB, :]
                        eng.wait_ge(s_mm, j + 1)
                        if kind == "q":
                            highs += 1
                            eng.wait_ge(s_hi, highs)
                            ins = dve.scalar_tensor_tensor(q[1][:, c, :], bank, bq[:, c:c + 1],
                                                           q[0][:, c, :].bitcast(F32), ALU.add, ALU.subtract)
                        elif kind == "k":
                            ins = dve.tensor_copy(qp[:, c, h * HALF:(h + 1) * HALF], bank)
                        else:
                            ins = dve.tensor_copy(shift[:, 4 * h:4 * h + 4], bank[:, 0:4])
                        ins.then_inc(s_out, 1)

                @block.tensor
                def _(eng):
                    for j, (h, kind, c) in enumerate(jobs):
                        bank = banks[:, j % NB, :]
                        if j >= NB:
                            eng.wait_ge(s_out, j - NB + 1)
                        cols = slice(c * P, (c + 1) * P)
                        tok = slice(h * HALF, (h + 1) * HALF)
                        if kind == "q":
                            eng.wait_ge(s_w[0], 1)
                            for k in range(DC):
                                ins = mm3(bank, wq[0][:, k, cols], wq[1][:, k, cols], xh[:, k, tok],
                                          xl[:, k, tok], k == 0, k == DC - 1)
                        elif kind == "k":
                            eng.wait_ge(s_w[1], 1)
                            eng.wait_ge(s_out, j - c)
                            for k in range(DC):
                                ins = mm3(bank, wk[0][:, k, cols], wk[1][:, k, cols], q[0][:, k, :],
                                          q[1][:, k, :], k == 0, k == DC - 1)
                        else:
                            for t in range(4):
                                for k in range(DC):
                                    for part in range(2):
                                        ins = pe.matmul(bank[:, t:t + 1],
                                                        q[part][:, k, t * P:(t + 1) * P].bitcast(F32),
                                                        bk[:, k:k + 1], start=(k + part == 0),
                                                        stop=(k == DC - 1 and part == 1))
                        ins.then_inc(s_mm, 1)

            f = Area(fa, F_SIZE, f2)
            r = Area(ra, R_SIZE, r2)
            qg = [f.take(DC, P) for _ in range(2)]
            ct = [f.take(DC, S) for _ in range(SEQ)]
            cn = [f.take(3, D) for _ in range(SEQ)]
            pr = [f.take(S) for _ in range(2)]
            pt = [f.take(3, P) for _ in range(2)]
            a = [f.take(D) for _ in range(2)]
            mx, top, bias, rs, rinv = (f.take(2) for _ in range(5))
            at = [(r.take(DC, P), r.take(DC, P)) for _ in range(2)]
            s_ctxT = [sem(f"xa_ctxT{j}") for j in range(SEQ)]
            s_ctx = [sem(f"xa_ctx{j}") for j in range(SEQ)]
            (s_qg, s_sc, s_bias, s_exp, s_tp, s_pt, s_pv, s_a, s_at, s_ah, s_al, s_o, s_x, s_links) = (
                sem(f"xa_{n}") for n in ("q_tile", "scores", "bias", "exp", "p_turned", "p_kept", "pv", "a_kept",
                                         "a_turned", "a_high", "a_low", "out", "x_added", "links"))

            with nc.Block() as block:
                @block.sync
                def _(eng):
                    with eng.Fori(0, NT) as n:
                        eng.wait_ge(s_sc, n + LEAD)
                        for j in range(SEQ):
                            eng.dma_start(ct[j], d["ctxT"][SEQ * n + j]).then_inc(s_ctxT[j], 16)
                        for j in range(SEQ):
                            eng.wait_ge(s_pv, SEQ * n + j + 1)
                            eng.dma_start(cn[j][:, 0:2, :], d["ctx"][SEQ * n + j, 0:2 * P, :]
                                          .rearrange("(k p) e -> p k e", p=P)).then_inc(s_ctx[j], 16)
                            eng.dma_start(cn[j][0:1, 2, :], d["ctx"][SEQ * n + j, 2 * P:S, :]).then_inc(s_ctx[j], 16)

                @block.gpsimd
                def _(eng):
                    with pool.Fori(0, NT // 2) as i:
                        for u in range(2):
                            n = 2 * i + u
                            eng.wait_ge(s_sc, n + 1)
                            eng.wait_ge(s_w[2], 1)
                            pool.tensor_copy(qg[u], qp[:, :, bass.ts(n, P)]).then_inc(s_qg, 1)

                @block.scalar
                def _(eng):
                    eng.sem_inc(s_exp, LEAD)
                    with act.Fori(0, NT // 2) as i:
                        for u in range(2):
                            n = 2 * i + u
                            eng.wait_ge(s_bias, n + 1)
                            act.activation(pr[u], banks[:, u, 0:S], ACT.Exp, bias=bias[:, u:u + 1], scale=scale,
                                           accum_out=rs[:, u:u + 1]).then_inc(s_exp, 1)
                            eng.wait_ge(s_at, n + 1 + LEAD)
                            act.activation(at[u][0], chunks(banks[:, 6, :]), ACT.Copy).then_inc(s_ah, 1)

                @block.vector
                def _(eng):
                    links = Links(eng, s_links)
                    eng.sem_inc(s_pt, LEAD)
                    eng.sem_inc(s_a, LEAD)
                    eng.sem_inc(s_al, 1)
                    eng.sem_inc(s_x, 1)

                    def softmax_top(n, u):
                        eng.wait_ge(s_sc, n + 1 + LEAD)
                        links.link(dve.reduce_max(mx[:, u:u + 1], banks[:, u, 0:S], AX_X))
                        sh = shift[:, bass.ds(n, 1)]
                        links.link(dve.tensor_tensor(top[:, u:u + 1], mx[:, u:u + 1], sh, ALU.add))
                        dve.tensor_scalar(bias[:, u:u + 1], top[:, u:u + 1], sh, -scale, ALU.subtract,
                                          ALU.mult).then_inc(s_bias, 1)

                    def rest(n, u):
                        eng.wait_ge(s_exp, n + 1 + LEAD)
                        dve.reciprocal(rinv[:, u:u + 1], rs[:, u:u + 1])
                        eng.wait_ge(s_tp, n + 1)
                        dve.tensor_copy(pt[u][:, 0:2, :], banks[:, 2 + u, 0:2 * P].rearrange("p (k t) -> p k t", k=2))
                        dve.tensor_copy(pt[u][0:1, 2, :], banks[0:1, 2 + u, 2 * P:3 * P]).then_inc(s_pt, 1)
                        eng.wait_ge(s_pv, SEQ * n + 2 * SEQ)
                        dve.tensor_scalar(a[u], banks[:, 4 + u, :], rinv[:, u:u + 1], None, ALU.mult).then_inc(s_a, 1)
                        eng.wait_ge(s_ah, n + 1)
                        dve.tensor_tensor(at[u][1], chunks(banks[:, 6, :]), at[u][0].bitcast(F32),
                                          ALU.subtract).then_inc(s_al, 1)
                        eng.wait_ge(s_o, n + 1)
                        links.link(dve.tensor_tensor(a[u], banks[:, 7, :], bv, ALU.add))
                        dve.tensor_tensor(x[:, n, :], x[:, n, :], a[u], ALU.add).then_inc(s_x, 1)

                    links.enter(0, 2)
                    softmax_top(0, 0)
                    links.leave(1)
                    with dve.Fori(0, NT // 2 - 1) as i:
                        links.enter(i, 6)
                        for u in range(2):
                            softmax_top(2 * i + u + 1, 1 - u)
                            rest(2 * i + u, u)
                        links.leave(NT // 2 - 1)
                    softmax_top(NT - 1, 1)
                    rest(NT - 2, 0)
                    rest(NT - 1, 1)

                @block.tensor
                def _(eng):
                    eng.sem_inc(s_sc, LEAD)
                    eng.sem_inc(s_pv, SEQ)
                    eng.sem_inc(s_at, LEAD)

                    def scores(n, u):
                        eng.wait_ge(s_qg, n + 1)
                        eng.wait_ge(s_exp, n + 1)
                        for j in range(SEQ):
                            eng.wait_ge(s_ctxT[j], 16 * n + 16)
                            for c in range(DC):
                                ins = pe.matmul(banks[NQ * j:NQ * j + NQ, u, 0:S], qg[u][:, c, NQ * j:NQ * j + NQ],
                                                ct[j][:, c, :], start=c == 0, stop=c == DC - 1)
                        ins.then_inc(s_sc, 1)

                    def rest(n, u):
                        eng.wait_ge(s_exp, n + 1 + LEAD)
                        eng.wait_ge(s_pt, n + 1)
                        for k in range(3):
                            rows = P if k < 2 else 1
                            ins = pe.transpose(banks[0:rows, 2 + u, k * P:(k + 1) * P],
                                               pr[u][:, k * P:k * P + rows], ident[:])
                        ins.then_inc(s_tp, 1)
                        eng.wait_ge(s_pt, n + 1 + LEAD)
                        eng.wait_ge(s_a, n + 1)
                        for j in range(SEQ):
                            eng.wait_ge(s_ctx[j], 32 * n + 32)
                            for k in range(3):
                                rows = P if k < 2 else 1
                                ins = pe.matmul(banks[NQ * j:NQ * j + NQ, 4 + u, :],
                                                pt[u][0:rows, k, NQ * j:NQ * j + NQ], cn[j][0:rows, k, :],
                                                start=k == 0, stop=k == 2)
                            ins.then_inc(s_pv, 1)
                        eng.wait_ge(s_a, n + 1 + LEAD)
                        eng.wait_ge(s_al, n + 1)
                        for c in range(DC):
                            ins = pe.transpose(banks[:, 6, c * P:(c + 1) * P], a[u][:, c * P:(c + 1) * P], ident[:])
                        ins.then_inc(s_at, 1)
                        eng.wait_ge(s_al, n + 2)
                        eng.wait_ge(s_x, n + 1)
                        for c in range(DC):
                            ins = mm3(banks[:, 7, :], at[u][0][:, c, :], at[u][1][:, c, :], wv[0][:, c, :],
                                      wv[1][:, c, :], c == 0, c == DC - 1)
                        ins.then_inc(s_o, 1)

                    scores(0, 0)
                    with pe.Fori(0, NT // 2 - 1) as i:
                        for u in range(2):
                            scores(2 * i + u + 1, 1 - u)
                            rest(2 * i + u, u)
                    scores(NT - 1, 1)
                    rest(NT - 2, 0)
                    rest(NT - 1, 1)

        def self_attention(tag, low_rank):
            scale = float(DH) ** -0.5
            HD = HH * DH
            EC = HD // P
            f, r = Area(fa, F_SIZE), Area(ra, R_SIZE)
            bo = f.take(D)
            zero_off = [f.take(HH, P) for _ in range(2)]
            mask, ss = f.take(HH, NQ), [f.take(HH, NQ) for _ in range(2)]
            bqc, bkc, bvb = f.take(2 * EC), f.take(2 * EC), f.take(2 * HD)
            f1 = f.at
            rqk = rv = None
            if low_rank:
                rqk, rv = (r.take(T), r.take(T)), (r.take(T), r.take(T))
            r1 = r.at
            s_c = sem(f"{tag}_constants")
            s_cl = sem(f"{tag}_constant_loads")
            pb = zero_off

            first_half = half_weights(tag, low_rank, 0, HD, EC, f1, r1, rqk, rv)
            if low_rank:
                fw, rw = Area(fa, F_SIZE, f1), Area(ra, R_SIZE, R_SIZE - 4 * DC * P)
                staging = [fw.take(DC, 2 * P)]
                w64 = rw.take(DC, 2 * P), rw.take(DC, 2 * P)
                load, high, low, s_w = split_programs(f"{tag}0", [(*w64, columns(d["L1_attn_w64"]))], staging)
                layer_norm("ne", ahead=[(load, high, low)])
                s_mm, s_hi, s_lo = sem(f"{tag}0_product"), sem(f"{tag}0_high"), sem(f"{tag}0_low")
                jobs = [(h, k) for h in range(NHALF) for k in range(2)]
            else:
                layer_norm("nb", (d["L0_attn_ln_gamma"], d["L0_attn_ln_beta"]), ahead=[first_half[1][:3]])
            with nc.Block() as block:
                @block.sync
                def _(eng):
                    loads = [(bo, d["L1_attn_fco_b" if low_rank else "L0_attn_b_out"].partition_broadcast(P))]
                    if low_rank:
                        loads += [(bqc, d["L1_attn_fcq_b"]),
                                  (bkc, d["L1_attn_fck_b"]),
                                  (bvb, d["L1_attn_fcv_b"].partition_broadcast(P))]
                    for dst, src in loads:
                        eng.dma_start(dst, src).then_inc(s_cl, 16)
                    if low_rank:
                        first_half[1][0](eng)
                    eng.wait_ge(s_cl, 16 * len(loads))

                @block.gpsimd
                def _(eng):
                    if low_rank:
                        first_half[1][2](eng, pool, range(3))
                    for u in range(2):
                        pool.memset(pb[u], 0.0)
                    if not low_rank:
                        for u in range(2):
                            pool.memset(ss[u], MASKED)
                        pool.memset(mask, 1.0).then_inc(s_c, 1)
                        for j in range(SEQ):
                            eng.wait_ge(s_c, j + 1)
                            m = mask[NQ * j:NQ * j + NQ]
                            pool.affine_select(out=m, in_=m, compare_op=ALU.is_ge, fill=0.0, base=0,
                                               pattern=[[0, HH], [-1, NQ]], channel_multiplier=1).then_inc(s_c, 1)

                @block.scalar
                def _(eng):
                    if low_rank:
                        for j, (h, k) in enumerate(jobs):
                            eng.wait_ge(s_mm, j + 1)
                            act.activation((rqk, rv)[k][0][:, h * HALF:(h + 1) * HALF], banks[:, j, :],
                                           ACT.Copy).then_inc(s_hi, 1)
                        first_half[1][1](eng)

                @block.vector
                def _(eng):
                    if low_rank:
                        for j, (h, k) in enumerate(jobs):
                            eng.wait_ge(s_hi, j + 1)
                            tok = slice(h * HALF, (h + 1) * HALF)
                            dve.tensor_tensor((rqk, rv)[k][1][:, tok], banks[:, j, :],
                                              (rqk, rv)[k][0][:, tok].bitcast(F32), ALU.subtract)

                @block.tensor
                def _(eng):
                    if low_rank:
                        eng.wait_ge(s_w[0], 1)
                        for j, (h, k) in enumerate(jobs):
                            tok = slice(h * HALF, (h + 1) * HALF)
                            for c in range(DC):
                                ins = mm3(banks[:, j, :], w64[0][:, c, k * P:(k + 1) * P], w64[1][:, c, k * P:(k + 1) * P],
                                          xh[:, c, tok], xl[:, c, tok], c == 0, c == DC - 1)
                            ins.then_inc(s_mm, 1)

            second_half = half_weights(tag, low_rank, 1, HD, EC, f1, r1, rqk, rv)
            for hh, (buffers, programs) in enumerate((first_half, second_half)):
                half_of_heads(tag, low_rank, hh, scale, HD, EC, bo, pb, mask, ss, bqc, bkc, bvb, rqk, rv, buffers,
                              programs, second_half[1] if hh == 0 else None)

        def half_weights(tag, low_rank, hh, HD, EC, f1, r1, rqk, rv):
            name = f"{tag}{hh + 1}"
            f, r = Area(fa, F_SIZE, f1), Area(ra, R_SIZE, r1)
            qt, kt = f.take(EC, T), f.take(EC, T)
            f2 = f.at
            heads = slice(hh * HD, (hh + 1) * HD)
            wo = r.take(EC, D), r.take(EC, D)
            tail = Area(fa, F_SIZE, F_SIZE - 4 * HD).take(4, HD)
            staging = [tail, f.take(4, HD), tail]
            if low_rank:
                wv, r2 = (r.take(HD), r.take(HD)), r.at
                r.at += 4096
                wqk = (r.take(HD), r.take(HD))
                weights = [(*wqk, d["L1_attn_fcqk"][:, heads]), (*wv, d["L1_attn_fcvv"][:, heads]),
                           (*wo, d["L1_attn_fco_w"][heads, :].rearrange("(c p) n -> p c n", p=P))]
                staging = [tail[:, 0, :], tail[:, 1, :], staging[1]]
                w = (wqk, wqk, wv, wo)
            else:
                wv, r2 = (r.take(DC, HD), r.take(DC, HD)), r.at
                wk, wq = ((r.take(DC, HD), r.take(DC, HD)) for _ in range(2))
                qkv, inner = d["L0_attn_w_qkvT"], 2 * HD

                def part(k):
                    return qkv[:, k * inner + hh * HD:k * inner + (hh + 1) * HD].rearrange("(c p) n -> p c n", p=P)
                weights = [(*wq, part(0)), (*wk, part(1)), (*wv, part(2)),
                           (*wo, d["L0_attn_w_outT"][heads, :].rearrange("(c p) n -> p c n", p=P))]
                w = (wq, wk, wv, wo)
            if hh == 0:
                programs = split_programs(name, weights, staging if low_rank else staging[:2])
            else:
                programs = (split_programs(name, weights[:1], staging[:1]),
                            split_programs(name + "r", weights[1:], staging[1:]))
            return (qt, kt, f2, r2, w), programs

        def half_of_heads(tag, low_rank, hh, scale, HD, EC, bo, pb, mask, ss, bqc, bkc, bvb, rqk, rv, buffers, programs,
                          following):
            name = f"{tag}{hh + 1}"
            heads = slice(hh * HD, (hh + 1) * HD)
            qt, kt, f2, r2, (wq, wk, wv, wo) = buffers
            wqk = wq
            s_w = programs[3] if hh == 0 else programs[0][3] + programs[1][3]
            s_mm, s_out = sem(f"{name}_qk_product"), sem(f"{name}_qk_taken")
            jobs = [(k, e, h) for k in range(2) for e in range(EC) for h in range(NHALF)]
            NB = 4

            with nc.Block() as block:
                if hh == 1:
                    @block.sync
                    def _(eng):
                        programs[1][0](eng)

                    @block.gpsimd
                    def _(eng):
                        programs[1][2](eng, pool, range(3))

                    @block.scalar
                    def _(eng):
                        programs[1][1](eng)

                @block.vector
                def _(eng):
                    for j, (k, e, h) in enumerate(jobs):
                        eng.wait_ge(s_mm, j + 1)
                        dst = (qt, kt)[k][:, e, h * HALF:(h + 1) * HALF]
                        if low_rank:
                            b = (bqc, bkc)[k][:, hh * EC + e:hh * EC + e + 1]
                            ins = dve.tensor_scalar(dst, banks[:, j % NB, :], b, None, ALU.add)
                        else:
                            ins = dve.tensor_copy(dst, banks[:, j % NB, :])
                        ins.then_inc(s_out, 1)

                @block.tensor
                def _(eng):
                    for j, (k, e, h) in enumerate(jobs):
                        if j >= NB:
                            eng.wait_ge(s_out, j - NB + 1)
                        cols, tok = slice(e * P, (e + 1) * P), slice(h * HALF, (h + 1) * HALF)
                        eng.wait_ge(s_w[0 if low_rank else k], 1)
                        if low_rank:
                            rows = slice(DH * k, DH * k + DH)
                            ins = mm3(banks[:, j % NB, :], wqk[0][rows, cols], wqk[1][rows, cols],
                                      rqk[0][rows, tok], rqk[1][rows, tok])
                        else:
                            w = (wq, wk)[k]
                            for c in range(DC):
                                ins = mm3(banks[:, j % NB, :], w[0][:, c, cols], w[1][:, c, cols], xh[:, c, tok],
                                          xl[:, c, tok], c == 0, c == DC - 1)
                        ins.then_inc(s_mm, 1)

            f, r = Area(fa, F_SIZE, f2), Area(ra, R_SIZE, r2)
            qg, kg, vg = ([f.take(EC, P) for _ in range(2)] for _ in range(3))
            sh, ex = ([f.take(HH, NQ) for _ in range(2)] for _ in range(2))
            mx, sums, rinv = (f.take(2, HH) for _ in range(3))
            xg = [(r.take(P), r.take(P)) if low_rank else (r.take(DC, P), r.take(DC, P)) for _ in range(2)]
            ot = [(r.take(EC, P), r.take(EC, P)) for _ in range(2)]
            (s_g, s_v, s_vg, s_s, s_sh, s_ex, s_pb, s_o, s_oh, s_ol, s_y, s_xa, s_links) = (
                sem(f"{name}_{n}") for n in ("tile", "v", "v_kept", "scores", "shifted", "exp", "p_turned", "o",
                                             "o_high", "o_low", "out", "x_added", "links"))
            s_passed = sem(f"{name}_passed")
            src = rv if low_rank else (xh, xl)

            with nc.Block() as block:
                if hh == 0:
                    @block.sync
                    def _(eng):
                        following[0][0](eng)

                @block.gpsimd
                def _(eng):
                    with pool.Fori(0, NT // 2) as i:
                        for u in range(2):
                            n = 2 * i + u
                            eng.wait_ge(s_s, n + 1)
                            eng.wait_ge(s_w[0], 1)
                            for part in range(2):
                                if low_rank:
                                    pool.tensor_copy(xg[u][part], src[part][:, bass.ts(n, P)])
                                else:
                                    pool.tensor_copy(xg[u][part], src[part][:, :, bass.ts(n, P)])
                            pool.tensor_copy(qg[u], qt[:, :, bass.ts(n, P)])
                            pool.tensor_copy(kg[u], kt[:, :, bass.ts(n, P)]).then_inc(s_g, 1)

                @block.scalar
                def _(eng):
                    def keep_v(n, u):
                        eng.wait_ge(s_v, n + 1)
                        eng.wait_ge(s_o, n + 1)
                        act.activation(vg[u], chunks(banks[:, 4 * u, :]), ACT.Copy).then_inc(s_vg, 1)

                    def rest(n, u):
                        eng.wait_ge(s_sh, n + 1)
                        act.activation(ex[u], sh[u], ACT.Exp, scale=scale).then_inc(s_ex, 1)
                        eng.wait_ge(s_o, n + 1 + LEAD)
                        act.activation(ot[u][0], chunks(banks[:, 4 * u + 3, :]), ACT.Copy).then_inc(s_oh, 1)

                    keep_v(0, 0)
                    if hh == 0:
                        following[0][1](eng)
                    with act.Fori(0, NT // 2 - 1) as i:
                        for u in range(2):
                            keep_v(2 * i + u + 1, 1 - u)
                            rest(2 * i + u, u)
                    keep_v(NT - 1, 1)
                    rest(NT - 2, 0)
                    rest(NT - 1, 1)

                @block.vector
                def _(eng):
                    links = Links(eng, s_links)
                    eng.sem_inc(s_xa, LEAD)
                    if hh == 0:
                        following[0][2](eng, dve, range(1))
                    steps = 5 + (1 if low_rank else 0) + (1 if hh == 0 else 0)
                    with dve.Fori(0, NT // 2) as i:
                        links.enter(i, 2 * steps)
                        for u in range(2):
                            n = 2 * i + u
                            bs = banks[:, 4 * u + 1:4 * u + 3, :].rearrange("p k (h t) -> p (k h) t", h=4)
                            if low_rank:
                                eng.wait_ge(s_vg, n + 1)
                                v = vg[u].rearrange("p c t -> p (c t)")
                                links.link(dve.tensor_tensor(v, v, bvb[:, heads], ALU.add))
                            eng.wait_ge(s_s, n + 1 + LEAD)
                            eng.sem_inc(s_passed, 1)
                            for j in range(SEQ):
                                rows = slice(NQ * j, NQ * j + NQ)
                                if low_rank:
                                    ins = dve.tensor_copy(ss[u][rows], bs[rows, :, rows])
                                else:
                                    ins = dve.copy_predicated(ss[u][rows], mask[rows].bitcast(U32), bs[rows, :, rows])
                            links.link(ins)
                            links.link(dve.reduce_max(mx[:, u, :], ss[u], AX_X))
                            dve.tensor_tensor(sh[u], ss[u], mx[:, u, :].unsqueeze(2).to_broadcast([P, HH, NQ]),
                                              ALU.subtract).then_inc(s_sh, 1)
                            eng.wait_ge(s_ex, n + 1)
                            links.link(dve.reduce_sum(sums[:, u, :], ex[u], AX_X))
                            links.link(dve.reciprocal(rinv[:, u, :], sums[:, u, :]))
                            links.link(dve.tensor_tensor(ex[u], ex[u], rinv[:, u, :].unsqueeze(2).to_broadcast([P, HH, NQ]),
                                                         ALU.mult))
                            for j in range(SEQ):
                                rows = slice(NQ * j, NQ * j + NQ)
                                ins = dve.transpose(pb[u][rows, :, rows], ex[u][rows])
                            ins.then_inc(s_pb, 1)
                            eng.wait_ge(s_oh, n + 1)
                            dve.tensor_tensor(ot[u][1], chunks(banks[:, 4 * u + 3, :]), ot[u][0].bitcast(F32),
                                              ALU.subtract).then_inc(s_ol, 1)
                            if hh == 0:
                                links.link(dve.tensor_tensor(x[:, n, :], x[:, n, :], bo, ALU.add))
                            eng.wait_ge(s_y, n + 1)
                            dve.tensor_tensor(x[:, n, :], banks[:, 4 * u, :], x[:, n, :], ALU.add).then_inc(s_xa, 1)
                        links.leave(NT // 2)

                @block.tensor
                def _(eng):
                    eng.sem_inc(s_s, LEAD)
                    eng.sem_inc(s_o, LEAD)

                    def v_and_scores(n, u):
                        eng.wait_ge(s_g, n + 1)
                        eng.wait_ge(s_xa, n + 1)
                        if low_rank:
                            ins = mm3(banks[:, 4 * u, :], xg[u][0][0:DH], xg[u][1][0:DH], wv[0][0:DH], wv[1][0:DH])
                        else:
                            for c in range(DC):
                                ins = mm3(banks[:, 4 * u, :], xg[u][0][:, c, :], xg[u][1][:, c, :], wv[0][:, c, :],
                                          wv[1][:, c, :], c == 0, c == DC - 1)
                        ins.then_inc(s_v, 1)
                        for h in range(HH):
                            rows = slice(DH * (h % 2), DH * (h % 2) + DH)
                            ins = pe.matmul(banks[:, 4 * u + 1 + h % 2, (h // 2) * P:(h // 2 + 1) * P],
                                            qg[u][rows, h // 2, :], kg[u][rows, h // 2, :], start=True, stop=True)
                        ins.then_inc(s_s, 1)

                    def rest(n, u):
                        eng.wait_ge(s_vg, n + 1)
                        eng.wait_ge(s_pb, n + 1)
                        for h in range(HH):
                            rows = slice(DH * (h % 2), DH * (h % 2) + DH)
                            v = vg[u].rearrange("p c t -> p (c t)")
                            ins = pe.matmul(banks[rows, 4 * u + 3, (h // 2) * P:(h // 2 + 1) * P],
                                            v[:, h * DH:(h + 1) * DH], pb[u][:, (h % 2) * 4 + h // 2, :],
                                            start=True, stop=True)
                        ins.then_inc(s_o, 1)
                        eng.wait_ge(s_ol, n + 1)
                        for c in range(EC):
                            ins = mm3(banks[:, 4 * u, :], ot[u][0][:, c, :], ot[u][1][:, c, :], wo[0][:, c, :],
                                      wo[1][:, c, :], c == 0, c == EC - 1)
                        ins.then_inc(s_y, 1)

                    v_and_scores(0, 0)
                    with pe.Fori(0, NT // 2 - 1) as i:
                        for u in range(2):
                            v_and_scores(2 * i + u + 1, 1 - u)
                            rest(2 * i + u, u)
                    v_and_scores(NT - 1, 1)
                    rest(NT - 2, 0)
                    rest(NT - 1, 1)

        def routing(tag, layer):
            E, K = (E0, K0) if layer == 0 else (E1, K1)
            f = Area(fa, F_SIZE)
            gate, gbias = f.take(DC, E), f.take(E)
            lg, sc, sel, t1 = (f.take(NT, E) for _ in range(4))
            gt, eq = f.take(NT, E, E), f.take(NT, E, E)
            tri = f.take(E, E)
            gm, gk = f.take(NT, G0), f.take(NT, G0)
            mx, sm, rank = f.take(NT), f.take(NT), f.take(NT, E)
            s_ld, s_tri, s_mm, s_act, s_in, s_links = (
                sem(f"{tag}_{n}") for n in ("gate", "earlier", "logits", "activated", "shifted", "links"))

            def compare(links, v, n, dst, size):
                a4, b4 = gt[:, :, 0:n, 0:n], eq[:, :, 0:n, 0:n]
                if n == E:
                    a4, b4 = gt, eq
                other = v.unsqueeze(2).to_broadcast([P, NT, n, n])
                own = v.unsqueeze(3).to_broadcast([P, NT, n, n])
                dve.tensor_tensor(a4, other, own, ALU.is_gt)
                links.link(dve.tensor_tensor(b4, other, own, ALU.is_equal))
                links.link(dve.tensor_tensor(b4, b4, tri[:, 0:n, 0:n].unsqueeze(1).to_broadcast([P, NT, n, n]),
                                             ALU.mult))
                links.link(dve.tensor_tensor(a4, a4, b4, ALU.add))
                links.link(dve.reduce_sum(dst, a4, AX_X))

            with nc.Block() as block:
                @block.sync
                def _(eng):
                    eng.dma_start(gate, d["L0_ffn_gateT" if layer == 0 else "L1_ffn_gateT"]
                                  .rearrange("(c p) e -> p c e", p=P)).then_inc(s_ld, 16)
                    if layer == 0:
                        eng.dma_start(gbias, d["L0_ffn_gate_bias"].partition_broadcast(P)).then_inc(s_ld, 16)

                @block.gpsimd
                def _(eng):
                    pool.memset(tri, 1.0).then_inc(s_tri, 1)
                    eng.wait_ge(s_tri, 1)
                    pool.affine_select(out=tri, in_=tri, compare_op=ALU.is_gt, fill=0.0, base=0,
                                       pattern=[[1, E], [-1, E]], channel_multiplier=0).then_inc(s_tri, 1)

                @block.scalar
                def _(eng):
                    if layer == 0:
                        eng.wait_ge(s_mm, 1)
                        act.activation(sc.rearrange("p t e -> p (t e)"), banks[:, 0, 0:NT * E],
                                       ACT.Sigmoid).then_inc(s_act, 1)
                    else:
                        eng.wait_ge(s_in, 1)
                        act.activation(sc, t1, ACT.Exp).then_inc(s_act, 1)

                @block.vector
                def _(eng):
                    links = Links(eng, s_links)
                    eng.wait_ge(s_tri, 2)
                    if layer == 0:
                        eng.wait_ge(s_act, 1)
                        eng.wait_ge(s_ld, 32)
                        links.link(dve.tensor_tensor(sel, sc, gbias.unsqueeze(1).to_broadcast([P, NT, E]), ALU.add))
                        links.link(dve.reduce_max(gm, sel.rearrange("p t (g e) -> p t g e", g=G0), AX_X))
                        compare(links, gm, G0, gk, 0)
                        links.link(dve.tensor_scalar(gm, gk, float(GK0), None, ALU.is_lt))
                        links.link(dve.tensor_scalar(gk, gm, -1.0, FAR, ALU.add, ALU.mult))
                        s4 = sel.rearrange("p t (g e) -> p t g e", g=G0)
                        shape = [P, NT, G0, E // G0]
                        links.link(dve.tensor_tensor(s4, s4, gm.unsqueeze(3).to_broadcast(shape), ALU.mult))
                        links.link(dve.tensor_tensor(s4, s4, gk.unsqueeze(3).to_broadcast(shape), ALU.add))
                    else:
                        eng.wait_ge(s_mm, 1)
                        links.link(dve.tensor_copy(sel.rearrange("p t e -> p (t e)"), banks[:, 0, 0:NT * E]))
                        links.link(dve.reduce_max(mx, sel, AX_X))
                        dve.tensor_tensor(t1, sel, mx.unsqueeze(2).to_broadcast([P, NT, E]),
                                          ALU.subtract).then_inc(s_in, 1)
                        eng.wait_ge(s_act, 1)
                    compare(links, sel, E, rank, 1)
                    links.link(dve.tensor_scalar(rank, rank, float(K), None, ALU.is_lt))
                    if layer == 0:
                        dve.tensor_tensor(comb[:, :, 0:E], rank, sc, ALU.mult)
                        dve.memset(comb[:, :, E:E + 1], 1.0)
                    else:
                        links.link(dve.tensor_tensor(lg, rank, sc, ALU.mult))
                        links.link(dve.reduce_sum(sm, lg, AX_X))
                        links.link(dve.reciprocal(mx, sm))
                        links.link(dve.tensor_tensor(t1, lg, mx.unsqueeze(2).to_broadcast([P, NT, E]), ALU.mult))
                        pairs = PAIRS // E
                        dve.tensor_copy(comb[:].rearrange("p t (e k) -> p t e k", e=E),
                                        t1.unsqueeze(3).to_broadcast([P, NT, E, pairs]))

                @block.tensor
                def _(eng):
                    eng.wait_ge(s_ld, 32 if layer == 0 else 16)
                    for t in range(NT):
                        for c in range(DC):
                            for part, xp in enumerate((xh, xl)):
                                ins = pe.matmul(banks[:, 0, t * E:(t + 1) * E], xp[:, c, t * P:(t + 1) * P].bitcast(F32),
                                                gate[:, c, :], start=(c + part == 0), stop=(c == DC - 1 and part == 1))
                    ins.then_inc(s_mm, 1)

        def experts(tag, units, w):
            f, r = Area(fa, F_SIZE), Area(ra, R_SIZE)
            st = [f.take(3, D) for _ in range(2)]
            wh, wl = ([r.take(3, D) for _ in range(2)] for _ in range(2))
            sg, hf = ([f.take(HALF) for _ in range(NHALF)] for _ in range(2))
            hh_, hl = ([r.take(HALF) for _ in range(NHALF)] for _ in range(2))
            s_ld = [sem(f"{tag}_loaded{u}") for u in range(2)]
            (s_wh, s_w, s_h, s_sg, s_hf, s_hh, s_hl, s_y, s_add) = (
                sem(f"{tag}_{n}") for n in ("w_high", "w_split", "h_products", "silu", "h", "h_high", "h_low", "y",
                                            "added"))
            TH = NT // NHALF
            N = units // 2

            with nc.Block() as block:
                @block.sync
                def _(eng):
                    with eng.Fori(0, N) as i:
                        for u in range(2):
                            n = 2 * i + u
                            eng.wait_ge(s_w, n + 1)
                            eng.dma_start(st[u], w[n]).then_inc(s_ld[u], 16)

                @block.gpsimd
                def _(eng):
                    eng.sem_inc(s_w, LEAD)
                    with pool.Fori(0, N) as i:
                        for u in range(2):
                            n = 2 * i + u
                            eng.wait_ge(s_wh, n + 1)
                            pool.tensor_tensor(wl[u], st[u], wh[u].bitcast(F32), ALU.subtract).then_inc(s_w, 1)

                @block.scalar
                def _(eng):
                    def weights_high(k, n, u):
                        eng.wait_ge(s_ld[u], 16 * k + 16)
                        if not (isinstance(n, int) and n == 0):
                            eng.wait_ge(s_y, 2 * TH * n)
                        act.activation(wh[u], st[u], ACT.Copy).then_inc(s_wh, 1)

                    def hidden(m, h):
                        eng.wait_ge(s_h, m + 1)
                        act.activation(sg[h], banks[:, 2 * h, :], ACT.Silu).then_inc(s_sg, 1)
                        eng.wait_ge(s_hf, m + 1 + LEAD)
                        eng.wait_ge(s_y, TH * m + TH)
                        act.activation(hh_[h], hf[h], ACT.Copy).then_inc(s_hh, 1)

                    def unit_pair(i, last):
                        for u in range(2):
                            m = 4 * i + 2 * u
                            hidden(m, 0)
                            if not (last and u):
                                weights_high(i + u, 2 * i + u + 1, 1 - u)
                            hidden(m + 1, 1)

                    weights_high(0, 0, 0)
                    with act.Fori(0, N - 1) as i:
                        unit_pair(i, False)
                    unit_pair(N - 1, True)

                @block.vector
                def _(eng):
                    eng.sem_inc(s_hf, LEAD)
                    eng.sem_inc(s_add, TH)

                    def hidden(m, h):
                        eng.wait_ge(s_sg, m + 1)
                        dve.tensor_tensor(hf[h], banks[:, 2 * h + 1, :], sg[h], ALU.mult).then_inc(s_hf, 1)
                        eng.wait_ge(s_hh, m + 1)
                        dve.tensor_tensor(hl[h], hf[h], hh_[h].bitcast(F32), ALU.subtract).then_inc(s_hl, 1)

                    def add(i, m, h):
                        for t in range(TH):
                            tile = TH * h + t
                            eng.wait_ge(s_y, TH * m + (t + 1 + 2 * TH))
                            dve.scalar_tensor_tensor(x[:, tile, :], banks[:, 4 + t, :], comb[:, tile, bass.ds(i, 1)],
                                                     x[:, tile, :], ALU.mult, ALU.add).then_inc(s_add, 1)

                    with dve.Fori(0, N) as i:
                        for u in range(2):
                            m = 4 * i + 2 * u
                            hidden(m, 0)
                            hidden(m + 1, 1)
                            add(i, m, 0)
                            add(i, m + 1, 1)

                @block.tensor
                def _(eng):
                    eng.sem_inc(s_y, 2 * TH)

                    def up(n, u, h):
                        if h == 0:
                            eng.wait_ge(s_w, n + 1 + LEAD)
                        eng.wait_ge(s_hf, 2 * n + h + 1)
                        for k in range(2):
                            for c in range(DC):
                                cols = slice(c * P, (c + 1) * P)
                                ins = mm3(banks[:, 2 * h + k, :], wh[u][:, k, cols], wl[u][:, k, cols],
                                          xh[:, c, h * HALF:(h + 1) * HALF], xl[:, c, h * HALF:(h + 1) * HALF],
                                          c == 0, c == DC - 1)
                        ins.then_inc(s_h, 1)

                    def down(n, u, h):
                        m = 2 * n + h
                        eng.wait_ge(s_hl, m + 1)
                        for t in range(TH):
                            eng.wait_ge(s_add, TH * m + (t + 1))
                            cols = slice(t * P, (t + 1) * P)
                            ins = mm3(banks[:, 4 + t, :], hh_[h][:, cols], hl[h][:, cols], wh[u][:, 2, :], wl[u][:, 2, :])
                            ins.then_inc(s_y, 1)

                    def unit_pair(i, last):
                        n = 2 * i
                        up(n, 0, 1)
                        down(n, 0, 0)
                        up(n + 1, 1, 0)
                        down(n, 0, 1)
                        up(n + 1, 1, 1)
                        down(n + 1, 1, 0)
                        if not last:
                            up(n + 2, 0, 0)
                        down(n + 1, 1, 1)

                    up(0, 0, 0)
                    with pe.Fori(0, N - 1) as i:
                        unit_pair(i, False)
                    unit_pair(N - 1, True)

        def cross_heads():
            scale = float(XD) ** -0.5
            f, r = Area(fa, F_SIZE), Area(ra, R_SIZE)
            qt, bvb, bob = f.take(DC, T), f.take(D), f.take(D)
            bqc, bkc, own = f.take(DC), f.take(DC), f.take(4)
            qblk = [f.take(DC, P) for _ in range(2)]
            stg = [f.take(DC, SE) for _ in range(2)]
            f2 = f.at
            staging = [f.take(DC, D) for _ in range(3)]
            lastT, vl = f.take(DC, B), f.take(D)
            wk, wv, wo = ((r.take(DC, D), r.take(DC, D)) for _ in range(3))
            r2 = r.at
            wq = r.take(DC, D), r.take(DC, D)
            load, high, low, s_w = split_programs("xb", [
                (*wv, columns(d["L1_xattn_W_V"])), (*wq, columns(d["L1_xattn_W_Q"])),
                (*wk, columns(d["L1_xattn_W_K"])), (*wo, columns(d["L1_xattn_W_O"]))], staging)
            layer_norm("nd", ahead=[(load, high, low)])
            s_b, s_mm, s_out, s_vl = sem("xb_biases"), sem("xb_product"), sem("xb_taken"), sem("xb_last_v")
            s_own = sem("xb_own_heads")
            jobs = [(e, h) for e in range(DC) for h in range(NHALF)]
            NB = 4

            with nc.Block() as block:
                @block.sync
                def _(eng):
                    for dst, src in ((bqc, d["L1_xattn_b_Q"]),
                                     (bkc, d["L1_xattn_b_K"]),
                                     (bvb, d["L1_xattn_b_V"].partition_broadcast(P)),
                                     (bob, d["L1_xattn_b_O"].partition_broadcast(P)),
                                     (lastT, d["ctxLastT"])):
                        eng.dma_start(dst, src).then_inc(s_b, 16)
                    eng.wait_ge(s_out, 1)
                    eng.dma_start(vlast_dram, vl[0:B, :]).then_inc(s_vl, 16)
                    eng.wait_ge(s_vl, 16)
                    eng.wait_ge(s_b, 80)

                @block.gpsimd
                def _(eng):
                    for u in range(2):
                        pool.memset(stg[u][:, :, S:SE], 0.0)
                    pool.memset(own, 1.0).then_inc(s_own, 1)
                    eng.wait_ge(s_own, 1)
                    pool.affine_select(out=own, in_=own, compare_op=ALU.is_ge, fill=0.0, base=0,
                                       pattern=[[-XD, 4]], channel_multiplier=1).then_inc(s_own, 1)
                    eng.wait_ge(s_own, 2)
                    pool.affine_select(out=own, in_=own, compare_op=ALU.is_gt, fill=0.0, base=XD,
                                       pattern=[[XD, 4]], channel_multiplier=-1)

                @block.vector
                def _(eng):
                    eng.wait_ge(s_b, 80)
                    eng.wait_ge(s_mm, 1)
                    dve.tensor_tensor(vl[0:B, :], banks[0:B, 7, :], bvb[0:B, :], ALU.add).then_inc(s_out, 1)
                    for j, (e, h) in enumerate(jobs):
                        eng.wait_ge(s_mm, j + 2)
                        dve.tensor_scalar(qt[:, e, h * HALF:(h + 1) * HALF], banks[:, j % NB, :], bqc[:, e:e + 1],
                                          None, ALU.add).then_inc(s_out, 1)

                @block.tensor
                def _(eng):
                    eng.wait_ge(s_b, 80)
                    eng.wait_ge(s_w[0], 1)
                    for c in range(DC):
                        for part in range(2):
                            ins = pe.matmul(banks[0:B, 7, :], lastT[:, c, :], wv[part][:, c, :].bitcast(F32),
                                            start=c + part == 0, stop=c == DC - 1 and part == 1)
                    ins.then_inc(s_mm, 1)
                    eng.wait_ge(s_w[1], 1)
                    for j, (e, h) in enumerate(jobs):
                        if j >= NB:
                            eng.wait_ge(s_out, j - NB + 2)
                        cols, tok = slice(e * P, (e + 1) * P), slice(h * HALF, (h + 1) * HALF)
                        for c in range(DC):
                            ins = mm3(banks[:, j % NB, :], wq[0][:, c, cols], wq[1][:, c, cols], xh[:, c, tok],
                                      xl[:, c, tok], c == 0, c == DC - 1)
                        ins.then_inc(s_mm, 1)

            f, r = Area(fa, F_SIZE, f2), Area(ra, R_SIZE, r2)
            kt = [f.take(DC, SE) for _ in range(2)]
            v = [f.take(2, D) for _ in range(2)]
            vlast = [f.take(D) for _ in range(2)]
            pr = [f.take(DC, SE) for _ in range(2)]
            pt, ot = f.take(3, D), f.take(DC, P)
            mx, bias, rs, rinv = (f.take(2, DC) for _ in range(4))
            cx = [(r.take(DC, SE), r.take(DC, SE)) for _ in range(2)]
            oh, ol = r.take(DC, P), r.take(DC, P)
            s_ld = [sem(f"xb_ctx{u}") for u in range(2)]
            s_vld = [sem(f"xb_vlast{u}") for u in range(2)]
            (s_ch, s_cl, s_kp, s_vp, s_k, s_v, s_qb, s_sc, s_bias, s_ex, s_rinv, s_pn, s_t, s_ta, s_td, s_pv,
             s_o, s_oh, s_ol, s_y, s_x, s_links) = (
                sem(f"xb_{n}") for n in (
                    "ctx_high", "ctx_low", "k_product", "v_product", "k_kept", "v_kept", "q_block", "scores", "bias",
                    "exp", "sums", "p_normed", "p_turned", "p_kept_a", "p_kept_d", "pv", "o_kept", "o_high", "o_low",
                    "out", "x_added", "links"))
            SC = 2
            T0, T1 = 6, 7

            with nc.Block() as block:
                @block.sync
                def _(eng):
                    with eng.Fori(0, B // 2) as i:
                        for u in range(2):
                            n = 2 * i + u
                            eng.wait_ge(s_cl, n + 1)
                            eng.dma_start(stg[u][:, :, 0:S], d["ctxT"][n]).then_inc(s_ld[u], 16)
                            eng.wait_ge(s_pv, n + 1)
                            eng.dma_start(vlast[u][0:1, :], vlast_dram[bass.ds(n, 1), :]).then_inc(s_vld[u], 16)

                @block.gpsimd
                def _(eng):
                    eng.sem_inc(s_cl, LEAD)

                    def ctx_low(n, u):
                        eng.wait_ge(s_ch, n + 1)
                        pool.tensor_tensor(cx[u][1], stg[u], cx[u][0].bitcast(F32), ALU.subtract).then_inc(s_cl, 1)

                    def step(m, u, after):
                        eng.wait_ge(s_sc, m + 1)
                        shape = [P, DC, 4, NQ]
                        pool.tensor_tensor(qblk[u].rearrange("p c (h q) -> p c h q", h=4),
                                           qt[:, :, bass.ts(m, NQ)].unsqueeze(2).to_broadcast(shape),
                                           own.unsqueeze(1).unsqueeze(3).to_broadcast(shape), ALU.mult).then_inc(s_qb, 1)
                        if after:
                            ctx_low(m + 1, 1 - u)
                        eng.wait_ge(s_rinv, m + 1)
                        pool.tensor_tensor(pr[u][:, :, 0:S], pr[u][:, :, 0:S],
                                           rinv[:, u, :].unsqueeze(2).to_broadcast([P, DC, S]),
                                           ALU.mult).then_inc(s_pn, 1)

                    ctx_low(0, 0)
                    step(0, 0, True)
                    with pool.Fori(0, NT - 1) as g:
                        for j in range(SEQ):
                            step(SEQ * g + j + 1, (j + 1) % 2, True)
                    for m in range(B - SEQ + 1, B):
                        step(m, m % 2, m + 1 < B)

                @block.scalar
                def _(eng):
                    def ctx_high(half, n, u):
                        eng.wait_ge(s_ld[u], 16 * half + 16)
                        if not (isinstance(n, int) and n < LEAD):
                            eng.wait_ge(s_vp, 2 * n)
                        act.activation(cx[u][0], stg[u], ACT.Copy).then_inc(s_ch, 1)

                    def keep_k(m, u):
                        for e in range(DC):
                            eng.wait_ge(s_kp, DC * m + (e + 1))
                            if e == 0:
                                eng.wait_ge(s_sc, m + 1)
                            act.activation(kt[u][:, e, :], banks[:, e % 2, 0:SE], ACT.Identity,
                                           bias=bkc[:, e:e + 1]).then_inc(s_k, 1)

                    def exps(m, u):
                        eng.wait_ge(s_bias, m + 1)
                        for c in range(DC):
                            ins = act.activation(pr[u][:, c, 0:S], banks[:, SC + c, 0:S], ACT.Exp,
                                                 bias=bias[:, u, c:c + 1], scale=scale, accum_out=rs[:, u, c:c + 1])
                        ins.then_inc(s_ex, 1)

                    def keep_p(n):
                        eng.wait_ge(s_t, 3 * n + 1)
                        act.activation(pt[:, 0, :], banks[:, T0, :], ACT.Copy).then_inc(s_ta, 1)
                        eng.wait_ge(s_t, 3 * n + 3)
                        act.activation(pt[0:1, 2, :], banks[0:1, 0, :], ACT.Copy).then_inc(s_ta, 1)

                    def step(g, j, after, after2):
                        n = SEQ * g + j
                        if after:
                            keep_k(n + 1, (j + 1) % 2)
                        if after2:
                            ctx_high(2 * g + (j + 2) // 2, n + 2, j % 2)
                        keep_p(n)
                        if after:
                            exps(n + 1, (j + 1) % 2)

                    def tile_out(g):
                        eng.wait_ge(s_o, SEQ * g + (SEQ + 1))
                        eng.wait_ge(s_y, g + 1)
                        act.activation(oh, ot, ACT.Copy).then_inc(s_oh, 1)

                    eng.sem_inc(s_ta, LEAD)
                    ctx_high(0, 0, 0)
                    keep_k(0, 0)
                    ctx_high(0, 1, 1)
                    exps(0, 0)
                    with act.Fori(0, NT - 1) as g:
                        for j in range(SEQ):
                            step(g, j, True, True)
                        tile_out(g)
                    for j in range(SEQ):
                        step(NT - 1, j, j < SEQ - 1, j < SEQ - 2)
                    tile_out(NT - 1)

                @block.vector
                def _(eng):
                    links = Links(eng, s_links)

                    def keep_v(m, u):
                        for k in range(2):
                            eng.wait_ge(s_vp, 2 * m + (k + 1 + LEAD))
                            if k == 0:
                                eng.wait_ge(s_pv, m + 1)
                            dve.tensor_tensor(v[u][:, k, :], banks[:, k, :], bvb, ALU.add).then_inc(s_v, 1)

                    def tops(m, u):
                        eng.wait_ge(s_sc, m + 1 + LEAD)
                        links.link(dve.reduce_max(mx[:, u, :], banks[:, SC:SC + DC, 0:S], AX_X))
                        dve.tensor_scalar(bias[:, u, :], mx[:, u, :], -scale, None, ALU.mult).then_inc(s_bias, 1)

                    def sums(m, u):
                        eng.wait_ge(s_ex, m + 1)
                        dve.reciprocal(rinv[:, u, :], rs[:, u, :]).then_inc(s_rinv, 1)

                    def step(g, j, after):
                        n = SEQ * g + j
                        if after:
                            keep_v(n + 1, (j + 1) % 2)
                        eng.wait_ge(s_t, 3 * n + 2)
                        dve.tensor_copy(pt[:, 1, :], banks[:, T1, :]).then_inc(s_td, 1)
                        if after:
                            tops(n + 1, (j + 1) % 2)
                            sums(n + 1, (j + 1) % 2)
                        eng.wait_ge(s_pv, n + 1 + LEAD)
                        o = chunks(banks[:, T1, :])
                        for h in range(4):
                            rows = slice(XD * h, XD * h + XD)
                            ins = dve.tensor_copy(ot[rows, :, NQ * j:NQ * j + NQ], o[rows, :, rows])
                        ins.then_inc(s_o, 1)

                    def tile_out(g):
                        eng.wait_ge(s_oh, g + 1)
                        dve.tensor_tensor(ol, ot, oh.bitcast(F32), ALU.subtract).then_inc(s_ol, 1)
                        links.link(dve.tensor_tensor(x[:, g, :], x[:, g, :], bob, ALU.add))
                        eng.wait_ge(s_y, g + 2)
                        dve.tensor_tensor(x[:, g, :], banks[:, T0, :], x[:, g, :], ALU.add).then_inc(s_x, 1)

                    eng.sem_inc(s_x, 1)
                    eng.sem_inc(s_o, 1)
                    keep_v(0, 0)
                    tops(0, 0)
                    sums(0, 0)
                    with dve.Fori(0, NT - 1) as g:
                        links.enter(g, SEQ + 1)
                        for j in range(SEQ):
                            step(g, j, True)
                        tile_out(g)
                        links.leave(NT - 1)
                    for j in range(SEQ):
                        step(NT - 1, j, j < SEQ - 1)
                    tile_out(NT - 1)

                @block.tensor
                def _(eng):
                    eng.sem_inc(s_vp, 2)
                    eng.sem_inc(s_y, 1)
                    eng.sem_inc(s_sc, LEAD)
                    eng.sem_inc(s_pv, LEAD)

                    def keys_values(m, u):
                        eng.wait_ge(s_cl, m + 1 + LEAD)
                        if not (isinstance(m, int) and m == 0):
                            eng.wait_ge(s_v, 2 * m)
                            eng.wait_ge(s_ta, 2 * m)
                        for e in range(DC):
                            if e >= 2:
                                eng.wait_ge(s_k, DC * m + (e - 1))
                            cols = slice(e * P, (e + 1) * P)
                            for c in range(DC):
                                ins = mm3(banks[:, e % 2, 0:SE], wk[0][:, c, cols], wk[1][:, c, cols], cx[u][0][:, c, :],
                                          cx[u][1][:, c, :], c == 0, c == DC - 1)
                            ins.then_inc(s_kp, 1)
                        for k in range(2):
                            eng.wait_ge(s_k, DC * m + (k + 3))
                            for c in range(DC):
                                rows = slice(k * P, (k + 1) * P)
                                ins = mm3(banks[:, k, :], cx[u][0][:, c, rows], cx[u][1][:, c, rows], wv[0][:, c, :],
                                          wv[1][:, c, :], c == 0, c == DC - 1)
                            ins.then_inc(s_vp, 1)

                    def scores(m, u):
                        eng.wait_ge(s_qb, m + 1)
                        eng.wait_ge(s_k, DC * m + DC)
                        if not (isinstance(m, int) and m == 0):
                            eng.wait_ge(s_ex, m)
                        for c in range(DC):
                            ins = pe.matmul(banks[:, SC + c, 0:S], qblk[u][:, c, :], kt[u][:, c, 0:S], start=True, stop=True)
                        ins.then_inc(s_sc, 1)

                    def turn(g, j, after):
                        n, u = SEQ * g + j, j % 2
                        eng.wait_ge(s_pn, n + 1)
                        eng.wait_ge(s_ta, 2 * n + 1)
                        eng.wait_ge(s_x, g + 1)
                        eng.wait_ge(s_o, n + 1)
                        for k in range(3):
                            rows = P if k < 2 else 1
                            if k == 2 and after:
                                eng.wait_ge(s_v, 2 * n + 3)
                            for c in range(DC):
                                ins = pe.transpose(banks[0:rows, (T0, T1, 0)[k], c * P:(c + 1) * P],
                                                   pr[u][:, c, k * P:k * P + rows], ident[:])
                            ins.then_inc(s_t, 1)

                    def p_v(g, j):
                        n, u = SEQ * g + j, j % 2
                        eng.wait_ge(s_ta, 2 * n + 2 + LEAD)
                        eng.wait_ge(s_td, n + 1)
                        eng.wait_ge(s_v, 2 * n + 2)
                        eng.wait_ge(s_vld[u], 32 * g + 16 * (j // 2 + 1))
                        for c in range(DC):
                            cols = slice(c * P, (c + 1) * P)
                            for k in range(2):
                                pe.matmul(banks[:, T1, cols], v[u][:, k, cols], pt[:, k, cols], start=k == 0, stop=False)
                            ins = pe.matmul(banks[:, T1, cols], vlast[u][0:1, cols], pt[0:1, 2, cols], start=False,
                                            stop=True)
                        ins.then_inc(s_pv, 1)

                    def step(g, j, after):
                        n = SEQ * g + j
                        if after:
                            keys_values(n + 1, (j + 1) % 2)
                        turn(g, j, after)
                        if after:
                            scores(n + 1, (j + 1) % 2)
                        p_v(g, j)

                    def tile_out(g):
                        eng.wait_ge(s_ol, g + 1)
                        for c in range(DC):
                            ins = mm3(banks[:, T0, :], oh[:, c, :], ol[:, c, :], wo[0][:, c, :], wo[1][:, c, :],
                                      c == 0, c == DC - 1)
                        ins.then_inc(s_y, 1)

                    keys_values(0, 0)
                    scores(0, 0)
                    with pe.Fori(0, NT - 1) as g:
                        for j in range(SEQ):
                            step(g, j, True)
                        tile_out(g)
                    for j in range(SEQ):
                        step(NT - 1, j, j < SEQ - 1)
                    tile_out(NT - 1)

        for stage in d.get("stages", "ABCDEF"):
            if stage == "A":
                cross_one_head()
            elif stage == "B":
                self_attention("sa", False)
            elif stage == "C":
                layer_norm("nc")
                routing("ra", 0)
                experts("ea", UNITS0, d["L0_units"])
                free_semaphores()
            elif stage == "D":
                cross_heads()
            elif stage == "E":
                self_attention("sb", True)
            else:
                layer_norm("nf")
                routing("rb", 1)
                experts("eb", UNITS1, d["L1_units"])
        s_out = sem("x_stored")
        with nc.Block() as block:
            @block.sync
            def _(eng):
                eng.dma_start(out.rearrange("(t p) d -> p t d", p=P), x[:]).then_inc(s_out, 16)
                eng.wait_ge(s_out, 16)


def layouts(i):
    def t(w):
        return np.swapaxes(w, -1, -2)

    def units(up1, up2, down):
        def up(w):
            return w.reshape(-1, P, DC, P).transpose(0, 3, 2, 1).reshape(-1, P, D)
        dn = t(down).reshape(-1, P, D)
        return np.ascontiguousarray(np.stack([up(up1), up(up2), dn], axis=2))

    ctx = i["ctx_1024"]
    a = {
        "x": i["x"].reshape(T, D),
        "ctx": ctx,
        "ctxT": t(ctx).reshape(B, DC, P, S).transpose(0, 2, 1, 3),
        "ctxLastT": ctx[:, S - 1, :].T.reshape(DC, P, B).transpose(1, 0, 2),
        "L0_xattn_WkT": t(i["L0_xattn_Wk"]),
        "L0_attn_w_qkvT": t(i["L0_attn_w_qkv"]),
        "L0_attn_w_outT": t(i["L0_attn_w_out"]),
        "L0_ffn_gateT": t(i["L0_ffn_gate_w"]),
        "L0_units": units(np.concatenate([i["L0_ffn_w1"], i["L0_ffn_ws1"][None]]),
                          np.concatenate([i["L0_ffn_w3"], i["L0_ffn_ws3"][None]]),
                          np.concatenate([i["L0_ffn_w2"], i["L0_ffn_ws2"][None]])),
        "L1_attn_w64": np.concatenate([i["L1_attn_wq"], i["L1_attn_wk"], i["L1_attn_wv"], i["L1_attn_wv"]], axis=1),
        "L1_attn_fcqk": np.concatenate([i["L1_attn_fcq_w"], i["L1_attn_fck_w"]]),
        "L1_attn_fcvv": np.concatenate([i["L1_attn_fcv_w"], i["L1_attn_fcv_w"]]),
        "L1_ffn_gateT": t(i["L1_ffn_gate_w"]),
        "L1_units": units(i["L1_ffn_w12"][:, :I1], i["L1_ffn_w12"][:, I1:], i["L1_ffn_w3"]),
    }
    for name in ("L0_xattn_Wq", "L0_xattn_bq", "L0_xattn_bk", "L0_xattn_Wv", "L0_xattn_bv", "L0_attn_ln_gamma",
                 "L0_attn_ln_beta", "L0_attn_b_out", "L0_ffn_gate_bias", "L1_xattn_W_Q", "L1_xattn_b_Q",
                 "L1_xattn_W_K", "L1_xattn_b_K", "L1_xattn_W_V", "L1_xattn_b_V", "L1_xattn_W_O", "L1_xattn_b_O",
                 "L1_attn_fcq_b", "L1_attn_fck_b", "L1_attn_fcv_b", "L1_attn_fco_w", "L1_attn_fco_b"):
        a[name] = i[name]
    for name in ("L0_xattn_bq", "L0_xattn_bk", "L1_xattn_b_Q", "L1_xattn_b_K", "L1_attn_fcq_b", "L1_attn_fck_b"):
        a[name] = i[name].reshape(-1, P).T
    return {k: np.ascontiguousarray(v) for k, v in a.items()}


def kernel(**inputs):
    from concourse import bacc
    from concourse.bass_utils import run_bass_kernel_spmd

    arrays = layouts({k: np.asarray(v) for k, v in inputs.items()})
    nc = bacc.Bacc("TRN2", target_bir_lowering=False, num_devices=1)
    d = {k: nc.dram_tensor(f"in_{k}", v.shape, mybir.dt.from_np(v.dtype), kind="ExternalInput").ap()
         for k, v in arrays.items()}
    out = nc.dram_tensor("out_x", (T, D), F32, kind="ExternalOutput").ap()
    build(nc, d, out)
    r = run_bass_kernel_spmd(nc, [{f"in_{k}": v for k, v in arrays.items()}], core_ids=[0])
    return r.results[0]["out_x"].reshape(B, NQ, D)
```

```python
from contextlib import ExitStack

import numpy as np
import concourse.bass as bass
from concourse import mybir

F32 = mybir.dt.float32
F32R = mybir.dt.float32r
U32 = mybir.dt.uint32
ALU = mybir.AluOpType
ACT = mybir.ActivationFunctionType
AX_X = mybir.AxisListType.X

P = 128
B, NQ, D = 32, 32, 512
S = 257
SE = 258
T = B * NQ
NT = T // P
SEQ = P // NQ
DC = D // P
HALF = 512
NHALF = T // HALF
DH = 64
HH = 8
E0, I0, K0 = 16, 256, 4
G0, GK0 = 4, 2
E1, I1, K1 = 8, 1024, 2
XH, XD = 16, 32
CAP = 2 * P
WEIGHT_BUFFERS = 4
LEAD = 2
FAR = 1e30
MASKED = -3.4028234663852886e38
LN_EPS = 1e-5
F_SIZE, R_SIZE = 74 * 256, 69 * 256
N_SIZE = 2304


class Links:

    def __init__(self, engine, sem):
        self.engine, self.sem, self.done, self.turn, self.k, self.per = engine, sem, 0, 0, 0, 0

    def enter(self, turn, per):
        self.turn, self.per, self.k = turn * per, per, 0

    def leave(self, turns):
        assert self.k == self.per, (self.k, self.per)
        self.done, self.turn, self.k, self.per = self.done + turns * self.per, 0, 0, 0

    def link(self, instruction):
        instruction.then_inc(self.sem, 1)
        self.k += 1
        self.engine.wait_ge(self.sem, self.turn + (self.done + self.k))
        if not self.per:
            self.done, self.k = self.done + 1, 0


class Area:

    def __init__(self, tensor, size, at=0):
        self.tensor, self.size, self.at = tensor, size, at

    def take(self, *shape):
        n = int(np.prod(shape))
        at, self.at = self.at, self.at + n + n % 2
        assert self.at <= self.size, ("arena", self.at, self.size)
        ap = self.tensor[:, at:at + n]
        if len(shape) > 1:
            names = "abcd"[:len(shape)]
            ap = ap.rearrange(f"p ({' '.join(names)}) -> p {' '.join(names)}", **dict(zip(names, shape)))
        return ap


def build(nc, d, out):
    with ExitStack() as ctx:
        def sb(name, shape, dt=F32):
            return ctx.enter_context(nc.sbuf_tensor(name, shape, dt))

        layer_sems = []

        def sem(name):
            layer_sems.append(nc.alloc_semaphore(name=name))
            return layer_sems[-1]

        def gather_sem(name):
            return nc.alloc_semaphore(name=name)

        def free_semaphores():
            with nc.Block() as block:
                @block.sync
                def _(eng):
                    for s in layer_sems:
                        eng.sem_clear(s)
            for s in layer_sems:
                nc.release_semaphore(s)
            layer_sems.clear()

        pe, act, dve, pool = nc.tensor, nc.scalar, nc.vector, nc.gpsimd
        x = sb("x", [P, NT, D])
        xh = sb("xh", [P, DC, T], F32R)
        xl = sb("xl", [P, DC, T], F32R)
        ident = sb("ident", [P, P])
        epst = sb("epst", [P, 1])
        stats = sb("stats", [P, NT, 6])
        moments = sb("moments", [P, NT, 2])
        rstd = sb("rstd", [P, NT])
        fa = sb("fa", [P, F_SIZE])
        ra = sb("ra", [P, R_SIZE], F32R)
        na = sb("na", [P, N_SIZE])
        banks = ctx.enter_context(nc.psum_tensor("banks", [P, 8, 512], F32))
        ones, earlier = sb("ones", [P, P], F32R), sb("earlier", [P, P], F32R)
        normed_dram = nc.dram_tensor("normed_scratch", [T, D], F32, kind="Internal").ap()
        vlast_dram = nc.dram_tensor("vlast_scratch", [B, D], F32, kind="Internal").ap()

        def mm3(psum, lh, ll, rh, rl, first=True, last=True):
            pe.matmul(psum, lh, rh, start=first, stop=False)
            pe.matmul(psum, lh, rl, start=False, stop=False)
            return pe.matmul(psum, ll, rh, start=False, stop=last)

        def chunks(ap):
            return ap.rearrange("p (c t) -> p c t", c=DC)

        s_x, s_id = sem("x_loaded"), sem("ident_made")
        with nc.Block() as block:
            @block.sync
            def _(eng):
                eng.dma_start(x[:], d["x"].rearrange("(t p) d -> p t d", p=P)).then_inc(s_x, 16)
                eng.wait_ge(s_x, 16)

            @block.gpsimd
            def _(eng):
                pool.memset(ident[:], 0.0).then_inc(s_id, 1)
                pool.memset(epst[:], LN_EPS)
                plain = Area(fa, F_SIZE).take(P)
                pool.memset(plain, 1.0).then_inc(s_id, 1)
                eng.wait_ge(s_id, 2)
                pool.affine_select(out=ident[:], in_=ident[:], compare_op=ALU.not_equal, fill=1.0,
                                   base=0, pattern=[[-1, P]], channel_multiplier=1)
                pool.tensor_copy(ones[:], plain)
                pool.affine_select(out=earlier[:], in_=plain, compare_op=ALU.is_gt, fill=0.0,
                                   base=0, pattern=[[1, P]], channel_multiplier=-1)

        def layer_norm(tag, affine=None, ahead=(), rows=None):
            f = Area(na, N_SIZE)
            xn = [f.take(D) for _ in range(LEAD)]
            gain, shift = f.take(D), f.take(D)
            root = f.take(NT)
            first = Area(fa, F_SIZE).take(NT, D)
            s_gain, s_stats, s_mom, s_root = (sem(f"{tag}_{n}") for n in ("gain", "statistics", "moments", "root"))
            s_xn, s_turned, s_hi, s_lo, s_links = (sem(f"{tag}_{n}") for n in ("normed", "turned", "high", "low", "links"))

            s_rows = [sem(f"{tag}_rows_stored{u}") for u in range(LEAD)] if rows is not None else None

            with nc.Block() as block:
                @block.sync
                def _(eng):
                    if rows is not None:
                        for u in range(LEAD):
                            eng.sem_inc(s_rows[u], 16)
                        with eng.Fori(0, NT // 2) as i:
                            for u in range(LEAD):
                                eng.wait_ge(s_xn, 2 * i + u + 1)
                                eng.dma_start(rows.rearrange("(t p) d -> t p d", p=P)[2 * i + u],
                                              xn[u]).then_inc(s_rows[u], 16)
                        for u in range(LEAD):
                            eng.wait_ge(s_rows[u], 16 + 16 * (NT // 2))
                    if affine:
                        eng.dma_start(gain, affine[0].partition_broadcast(P)).then_inc(s_gain, 16)
                        eng.dma_start(shift, affine[1].partition_broadcast(P)).then_inc(s_gain, 16)
                    for load, _, _ in ahead:
                        load(eng)

                @block.gpsimd
                def _(eng):
                    for _, _, low in ahead:
                        low(eng, pool, (0, 2))

                @block.vector
                def _(eng):
                    links = Links(eng, s_links)

                    def moments_of(source, k):
                        with dve.Fori(0, NT) as t:
                            dve.bn_stats(stats[:, t, :], source[:, t, :]).then_inc(s_stats, 1)
                        for t in range(NT):
                            eng.wait_ge(s_stats, NT * k + t + 1)
                            dve.bn_aggr(moments[:, t, :], stats[:, t, :]).then_inc(s_mom, 1)
                        eng.wait_ge(s_root, k + 1)
                        links.link(dve.reciprocal(rstd[:], root))

                    source = x
                    moments_of(x, 0)
                    if affine:
                        for t in range(NT):
                            ins = dve.tensor_scalar(first[:, t, :], x[:, t, :], moments[:, t, 0:1], rstd[:, t:t + 1],
                                                    ALU.subtract, ALU.mult)
                        links.link(ins)
                        source = first
                        moments_of(first, 1)
                        eng.wait_ge(s_gain, 32)

                    def normalise(n, u, k):
                        eng.wait_ge(s_turned, n + 1)
                        if rows is not None:
                            eng.wait_ge(s_rows[u], 16 * k + 16)
                        mean, r = moments[:, n, 0:1], rstd[:, bass.ds(n, 1)]
                        if affine:
                            links.link(dve.scalar_tensor_tensor(xn[u], source[:, n, :], mean, gain, ALU.subtract,
                                                                ALU.mult))
                            ins = dve.scalar_tensor_tensor(xn[u], xn[u], r, shift, ALU.mult, ALU.add)
                        else:
                            ins = dve.tensor_scalar(xn[u], source[:, n, :], mean, r, ALU.subtract, ALU.mult)
                        ins.then_inc(s_xn, 1)

                    def low_part(n, u):
                        eng.wait_ge(s_hi, n + 1)
                        dve.tensor_tensor(xl[:, :, bass.ts(n, P)], chunks(banks[:, u, :]),
                                          xh[:, :, bass.ts(n, P)].bitcast(F32), ALU.subtract).then_inc(s_lo, 1)

                    eng.sem_inc(s_lo, LEAD)
                    links.enter(0, 1 if affine else 0)
                    normalise(0, 0, 0)
                    links.leave(1)
                    with dve.Fori(0, NT // 2 - 1) as i:
                        links.enter(i, 2 if affine else 0)
                        for u in range(2):
                            normalise(2 * i + u + 1, 1 - u, i + u)
                            low_part(2 * i + u, u)
                        links.leave(NT // 2 - 1)
                    normalise(NT - 1, 1, NT // 2 - 1)
                    low_part(NT - 2, 0)
                    low_part(NT - 1, 1)
                    for _, _, low in ahead:
                        low(eng, dve, (1, 3))

                @block.scalar
                def _(eng):
                    for k in range(2 if affine else 1):
                        eng.wait_ge(s_mom, NT * k + NT)
                        act.activation(root, moments[:, :, 1], ACT.Sqrt, bias=epst[:]).then_inc(s_root, 1)
                    with act.Fori(0, NT // 2) as i:
                        for u in range(LEAD):
                            n = 2 * i + u
                            eng.wait_ge(s_turned, n + 1 + LEAD)
                            act.activation(xh[:, :, bass.ts(n, P)], chunks(banks[:, u, :]),
                                           ACT.Copy).then_inc(s_hi, 1)
                    for _, high, _ in ahead:
                        high(eng)

                @block.tensor
                def _(eng):
                    eng.sem_inc(s_turned, LEAD)
                    with pe.Fori(0, NT // 2) as i:
                        for u in range(LEAD):
                            n = 2 * i + u
                            eng.wait_ge(s_xn, n + 1)
                            eng.wait_ge(s_lo, n + 1)
                            for c in range(DC):
                                ins = pe.transpose(banks[:, u, c * P:(c + 1) * P],
                                                   xn[u][:, c * P:(c + 1) * P], ident[:])
                            ins.then_inc(s_turned, 1)

        def split_programs(tag, weights, staging):
            s_ld = [sem(f"{tag}_weight{k}") for k in range(len(weights))]
            s_hi = [sem(f"{tag}_high{k}") for k in range(len(weights))]
            s_w = [sem(f"{tag}_split{k}") for k in range(len(weights))]
            slots = len(staging)

            def load(eng):
                for k, (_, _, src) in enumerate(weights):
                    if k >= slots:
                        eng.wait_ge(s_w[k - slots], 1)
                    eng.dma_start(staging[k % slots], src).then_inc(s_ld[k], 16)

            def high(eng):
                for k, (hi, _, _) in enumerate(weights):
                    eng.wait_ge(s_ld[k], 16)
                    act.activation(hi, staging[k % slots], ACT.Copy).then_inc(s_hi[k], 1)

            def low(eng, unit, which):
                for k in which:
                    if k < len(weights):
                        hi, lo, _ = weights[k]
                        eng.wait_ge(s_hi[k], 1)
                        unit.tensor_tensor(lo, staging[k % slots], hi.bitcast(F32), ALU.subtract).then_inc(s_w[k], 1)
            return load, high, low, s_w

        def columns(w):
            return w.rearrange("(c p) n -> p c n", p=P)

        def cross_one_head():
            scale = float(D) ** -0.5
            f, r = Area(fa, F_SIZE), Area(ra, R_SIZE)
            qp, bv, bk, bq, shift = f.take(DC, T), f.take(D), f.take(DC), f.take(DC), f.take(NT)
            f2 = f.at
            staging = [f.take(DC, D) for _ in range(3)]
            wv = r.take(DC, D), r.take(DC, D)
            r2 = r.at
            wq, wk = (r.take(DC, D), r.take(DC, D)), (r.take(DC, D), r.take(DC, D))
            q = [r.take(DC, HALF) for _ in range(2)]
            load, high, low, s_w = split_programs("xa", [
                (*wq, columns(d["L0_xattn_Wq"])), (*wk, columns(d["L0_xattn_WkT"])),
                (*wv, columns(d["L0_xattn_Wv"]))], staging)
            layer_norm("na", ahead=[(load, high, low)])
            s_b, s_mm, s_hi, s_out = sem("xa_biases"), sem("xa_product"), sem("xa_high"), sem("xa_taken")
            jobs = [(h, kind, c) for h in range(NHALF) for kind, c in
                    [("q", c) for c in range(DC)] + [("k", c) for c in range(DC)] + [("shift", 0)]]
            NB = 4

            with nc.Block() as block:
                @block.sync
                def _(eng):
                    eng.dma_start(bq, d["L0_xattn_bq"]).then_inc(s_b, 16)
                    eng.dma_start(bk, d["L0_xattn_bk"]).then_inc(s_b, 16)
                    eng.dma_start(bv, d["L0_xattn_bv"].partition_broadcast(P)).then_inc(s_b, 16)

                @block.scalar
                def _(eng):
                    eng.wait_ge(s_b, 48)
                    for j, (h, kind, c) in enumerate(jobs):
                        if kind != "q":
                            continue
                        eng.wait_ge(s_mm, j + 1)
                        if h:
                            eng.wait_ge(s_mm, len(jobs) // 2)
                        act.activation(q[0][:, c, :], banks[:, j % NB, :], ACT.Identity,
                                       bias=bq[:, c:c + 1]).then_inc(s_hi, 1)

                @block.vector
                def _(eng):
                    eng.wait_ge(s_b, 48)
                    highs = 0
                    for j, (h, kind, c) in enumerate(jobs):
                        bank = banks[:, j % NB, :]
                        eng.wait_ge(s_mm, j + 1)
                        if kind == "q":
                            highs += 1
                            eng.wait_ge(s_hi, highs)
                            ins = dve.scalar_tensor_tensor(q[1][:, c, :], bank, bq[:, c:c + 1],
                                                           q[0][:, c, :].bitcast(F32), ALU.add, ALU.subtract)
                        elif kind == "k":
                            ins = dve.tensor_copy(qp[:, c, h * HALF:(h + 1) * HALF], bank)
                        else:
                            ins = dve.tensor_copy(shift[:, 4 * h:4 * h + 4], bank[:, 0:4])
                        ins.then_inc(s_out, 1)

                @block.tensor
                def _(eng):
                    for j, (h, kind, c) in enumerate(jobs):
                        bank = banks[:, j % NB, :]
                        if j >= NB:
                            eng.wait_ge(s_out, j - NB + 1)
                        cols = slice(c * P, (c + 1) * P)
                        tok = slice(h * HALF, (h + 1) * HALF)
                        if kind == "q":
                            eng.wait_ge(s_w[0], 1)
                            for k in range(DC):
                                ins = mm3(bank, wq[0][:, k, cols], wq[1][:, k, cols], xh[:, k, tok],
                                          xl[:, k, tok], k == 0, k == DC - 1)
                        elif kind == "k":
                            eng.wait_ge(s_w[1], 1)
                            eng.wait_ge(s_out, j - c)
                            for k in range(DC):
                                ins = mm3(bank, wk[0][:, k, cols], wk[1][:, k, cols], q[0][:, k, :],
                                          q[1][:, k, :], k == 0, k == DC - 1)
                        else:
                            for t in range(4):
                                for k in range(DC):
                                    for part in range(2):
                                        ins = pe.matmul(bank[:, t:t + 1],
                                                        q[part][:, k, t * P:(t + 1) * P].bitcast(F32),
                                                        bk[:, k:k + 1], start=(k + part == 0),
                                                        stop=(k == DC - 1 and part == 1))
                        ins.then_inc(s_mm, 1)

            f = Area(fa, F_SIZE, f2)
            r = Area(ra, R_SIZE, r2)
            qg = [f.take(DC, P) for _ in range(2)]
            ct = [f.take(DC, S) for _ in range(SEQ)]
            cn = [f.take(3, D) for _ in range(SEQ)]
            pr = [f.take(S) for _ in range(2)]
            pt = [f.take(3, P) for _ in range(2)]
            a = [f.take(D) for _ in range(2)]
            mx, top, bias, rs, rinv = (f.take(2) for _ in range(5))
            at = [(r.take(DC, P), r.take(DC, P)) for _ in range(2)]
            s_ctxT = [sem(f"xa_ctxT{j}") for j in range(SEQ)]
            s_ctx = [sem(f"xa_ctx{j}") for j in range(SEQ)]
            (s_qg, s_sc, s_bias, s_exp, s_tp, s_pt, s_pv, s_a, s_at, s_ah, s_al, s_o, s_x, s_links) = (
                sem(f"xa_{n}") for n in ("q_tile", "scores", "bias", "exp", "p_turned", "p_kept", "pv", "a_kept",
                                         "a_turned", "a_high", "a_low", "out", "x_added", "links"))

            with nc.Block() as block:
                @block.sync
                def _(eng):
                    with eng.Fori(0, NT) as n:
                        eng.wait_ge(s_sc, n + LEAD)
                        for j in range(SEQ):
                            eng.dma_start(ct[j], d["ctxT"][SEQ * n + j]).then_inc(s_ctxT[j], 16)
                        for j in range(SEQ):
                            eng.wait_ge(s_pv, SEQ * n + j + 1)
                            eng.dma_start(cn[j][:, 0:2, :], d["ctx"][SEQ * n + j, 0:2 * P, :]
                                          .rearrange("(k p) e -> p k e", p=P)).then_inc(s_ctx[j], 16)
                            eng.dma_start(cn[j][0:1, 2, :], d["ctx"][SEQ * n + j, 2 * P:S, :]).then_inc(s_ctx[j], 16)

                @block.gpsimd
                def _(eng):
                    with pool.Fori(0, NT // 2) as i:
                        for u in range(2):
                            n = 2 * i + u
                            eng.wait_ge(s_sc, n + 1)
                            eng.wait_ge(s_w[2], 1)
                            pool.tensor_copy(qg[u], qp[:, :, bass.ts(n, P)]).then_inc(s_qg, 1)

                @block.scalar
                def _(eng):
                    eng.sem_inc(s_exp, LEAD)
                    with act.Fori(0, NT // 2) as i:
                        for u in range(2):
                            n = 2 * i + u
                            eng.wait_ge(s_bias, n + 1)
                            act.activation(pr[u], banks[:, u, 0:S], ACT.Exp, bias=bias[:, u:u + 1], scale=scale,
                                           accum_out=rs[:, u:u + 1]).then_inc(s_exp, 1)
                            eng.wait_ge(s_at, n + 1 + LEAD)
                            act.activation(at[u][0], chunks(banks[:, 6, :]), ACT.Copy).then_inc(s_ah, 1)

                @block.vector
                def _(eng):
                    links = Links(eng, s_links)
                    eng.sem_inc(s_pt, LEAD)
                    eng.sem_inc(s_a, LEAD)
                    eng.sem_inc(s_al, 1)
                    eng.sem_inc(s_x, 1)

                    def softmax_top(n, u):
                        eng.wait_ge(s_sc, n + 1 + LEAD)
                        links.link(dve.reduce_max(mx[:, u:u + 1], banks[:, u, 0:S], AX_X))
                        sh = shift[:, bass.ds(n, 1)]
                        links.link(dve.tensor_tensor(top[:, u:u + 1], mx[:, u:u + 1], sh, ALU.add))
                        dve.tensor_scalar(bias[:, u:u + 1], top[:, u:u + 1], sh, -scale, ALU.subtract,
                                          ALU.mult).then_inc(s_bias, 1)

                    def rest(n, u):
                        eng.wait_ge(s_exp, n + 1 + LEAD)
                        dve.reciprocal(rinv[:, u:u + 1], rs[:, u:u + 1])
                        eng.wait_ge(s_tp, n + 1)
                        dve.tensor_copy(pt[u][:, 0:2, :], banks[:, 2 + u, 0:2 * P].rearrange("p (k t) -> p k t", k=2))
                        dve.tensor_copy(pt[u][0:1, 2, :], banks[0:1, 2 + u, 2 * P:3 * P]).then_inc(s_pt, 1)
                        eng.wait_ge(s_pv, SEQ * n + 2 * SEQ)
                        dve.tensor_scalar(a[u], banks[:, 4 + u, :], rinv[:, u:u + 1], None, ALU.mult).then_inc(s_a, 1)
                        eng.wait_ge(s_ah, n + 1)
                        dve.tensor_tensor(at[u][1], chunks(banks[:, 6, :]), at[u][0].bitcast(F32),
                                          ALU.subtract).then_inc(s_al, 1)
                        eng.wait_ge(s_o, n + 1)
                        links.link(dve.tensor_tensor(a[u], banks[:, 7, :], bv, ALU.add))
                        dve.tensor_tensor(x[:, n, :], x[:, n, :], a[u], ALU.add).then_inc(s_x, 1)

                    links.enter(0, 2)
                    softmax_top(0, 0)
                    links.leave(1)
                    with dve.Fori(0, NT // 2 - 1) as i:
                        links.enter(i, 6)
                        for u in range(2):
                            softmax_top(2 * i + u + 1, 1 - u)
                            rest(2 * i + u, u)
                        links.leave(NT // 2 - 1)
                    softmax_top(NT - 1, 1)
                    rest(NT - 2, 0)
                    rest(NT - 1, 1)

                @block.tensor
                def _(eng):
                    eng.sem_inc(s_sc, LEAD)
                    eng.sem_inc(s_pv, SEQ)
                    eng.sem_inc(s_at, LEAD)

                    def scores(n, u):
                        eng.wait_ge(s_qg, n + 1)
                        eng.wait_ge(s_exp, n + 1)
                        for j in range(SEQ):
                            eng.wait_ge(s_ctxT[j], 16 * n + 16)
                            for c in range(DC):
                                ins = pe.matmul(banks[NQ * j:NQ * j + NQ, u, 0:S], qg[u][:, c, NQ * j:NQ * j + NQ],
                                                ct[j][:, c, :], start=c == 0, stop=c == DC - 1)
                        ins.then_inc(s_sc, 1)

                    def rest(n, u):
                        eng.wait_ge(s_exp, n + 1 + LEAD)
                        eng.wait_ge(s_pt, n + 1)
                        for k in range(3):
                            rows = P if k < 2 else 1
                            ins = pe.transpose(banks[0:rows, 2 + u, k * P:(k + 1) * P],
                                               pr[u][:, k * P:k * P + rows], ident[:])
                        ins.then_inc(s_tp, 1)
                        eng.wait_ge(s_pt, n + 1 + LEAD)
                        eng.wait_ge(s_a, n + 1)
                        for j in range(SEQ):
                            eng.wait_ge(s_ctx[j], 32 * n + 32)
                            for k in range(3):
                                rows = P if k < 2 else 1
                                ins = pe.matmul(banks[NQ * j:NQ * j + NQ, 4 + u, :],
                                                pt[u][0:rows, k, NQ * j:NQ * j + NQ], cn[j][0:rows, k, :],
                                                start=k == 0, stop=k == 2)
                            ins.then_inc(s_pv, 1)
                        eng.wait_ge(s_a, n + 1 + LEAD)
                        eng.wait_ge(s_al, n + 1)
                        for c in range(DC):
                            ins = pe.transpose(banks[:, 6, c * P:(c + 1) * P], a[u][:, c * P:(c + 1) * P], ident[:])
                        ins.then_inc(s_at, 1)
                        eng.wait_ge(s_al, n + 2)
                        eng.wait_ge(s_x, n + 1)
                        for c in range(DC):
                            ins = mm3(banks[:, 7, :], at[u][0][:, c, :], at[u][1][:, c, :], wv[0][:, c, :],
                                      wv[1][:, c, :], c == 0, c == DC - 1)
                        ins.then_inc(s_o, 1)

                    scores(0, 0)
                    with pe.Fori(0, NT // 2 - 1) as i:
                        for u in range(2):
                            scores(2 * i + u + 1, 1 - u)
                            rest(2 * i + u, u)
                    scores(NT - 1, 1)
                    rest(NT - 2, 0)
                    rest(NT - 1, 1)

        def self_attention(tag, low_rank):
            scale = float(DH) ** -0.5
            HD = HH * DH
            EC = HD // P
            f, r = Area(fa, F_SIZE), Area(ra, R_SIZE)
            bo = f.take(D)
            zero_off = [f.take(HH, P) for _ in range(2)]
            mask, ss = f.take(HH, NQ), [f.take(HH, NQ) for _ in range(2)]
            bqc, bkc, bvb = f.take(2 * EC), f.take(2 * EC), f.take(2 * HD)
            f1 = f.at
            rqk = rv = None
            if low_rank:
                rqk, rv = (r.take(T), r.take(T)), (r.take(T), r.take(T))
            r1 = r.at
            s_c = sem(f"{tag}_constants")
            s_cl = sem(f"{tag}_constant_loads")
            pb = zero_off

            first_half = half_weights(tag, low_rank, 0, HD, EC, f1, r1, rqk, rv)
            if low_rank:
                fw, rw = Area(fa, F_SIZE, f1), Area(ra, R_SIZE, R_SIZE - 4 * DC * P)
                staging = [fw.take(DC, 2 * P)]
                w64 = rw.take(DC, 2 * P), rw.take(DC, 2 * P)
                load, high, low, s_w = split_programs(f"{tag}0", [(*w64, columns(d["L1_attn_w64"]))], staging)
                layer_norm("ne", ahead=[(load, high, low)])
                s_mm, s_hi, s_lo = sem(f"{tag}0_product"), sem(f"{tag}0_high"), sem(f"{tag}0_low")
                jobs = [(h, k) for h in range(NHALF) for k in range(2)]
            else:
                layer_norm("nb", (d["L0_attn_ln_gamma"], d["L0_attn_ln_beta"]), ahead=[first_half[1][:3]])
            with nc.Block() as block:
                @block.sync
                def _(eng):
                    loads = [(bo, d["L1_attn_fco_b" if low_rank else "L0_attn_b_out"].partition_broadcast(P))]
                    if low_rank:
                        loads += [(bqc, d["L1_attn_fcq_b"]),
                                  (bkc, d["L1_attn_fck_b"]),
                                  (bvb, d["L1_attn_fcv_b"].partition_broadcast(P))]
                    for dst, src in loads:
                        eng.dma_start(dst, src).then_inc(s_cl, 16)
                    if low_rank:
                        first_half[1][0](eng)
                    eng.wait_ge(s_cl, 16 * len(loads))

                @block.gpsimd
                def _(eng):
                    if low_rank:
                        first_half[1][2](eng, pool, range(3))
                    for u in range(2):
                        pool.memset(pb[u], 0.0)
                    if not low_rank:
                        for u in range(2):
                            pool.memset(ss[u], MASKED)
                        pool.memset(mask, 1.0).then_inc(s_c, 1)
                        for j in range(SEQ):
                            eng.wait_ge(s_c, j + 1)
                            m = mask[NQ * j:NQ * j + NQ]
                            pool.affine_select(out=m, in_=m, compare_op=ALU.is_ge, fill=0.0, base=0,
                                               pattern=[[0, HH], [-1, NQ]], channel_multiplier=1).then_inc(s_c, 1)

                @block.scalar
                def _(eng):
                    if low_rank:
                        for j, (h, k) in enumerate(jobs):
                            eng.wait_ge(s_mm, j + 1)
                            act.activation((rqk, rv)[k][0][:, h * HALF:(h + 1) * HALF], banks[:, j, :],
                                           ACT.Copy).then_inc(s_hi, 1)
                        first_half[1][1](eng)

                @block.vector
                def _(eng):
                    if low_rank:
                        for j, (h, k) in enumerate(jobs):
                            eng.wait_ge(s_hi, j + 1)
                            tok = slice(h * HALF, (h + 1) * HALF)
                            dve.tensor_tensor((rqk, rv)[k][1][:, tok], banks[:, j, :],
                                              (rqk, rv)[k][0][:, tok].bitcast(F32), ALU.subtract)

                @block.tensor
                def _(eng):
                    if low_rank:
                        eng.wait_ge(s_w[0], 1)
                        for j, (h, k) in enumerate(jobs):
                            tok = slice(h * HALF, (h + 1) * HALF)
                            for c in range(DC):
                                ins = mm3(banks[:, j, :], w64[0][:, c, k * P:(k + 1) * P], w64[1][:, c, k * P:(k + 1) * P],
                                          xh[:, c, tok], xl[:, c, tok], c == 0, c == DC - 1)
                            ins.then_inc(s_mm, 1)

            second_half = half_weights(tag, low_rank, 1, HD, EC, f1, r1, rqk, rv)
            for hh, (buffers, programs) in enumerate((first_half, second_half)):
                half_of_heads(tag, low_rank, hh, scale, HD, EC, bo, pb, mask, ss, bqc, bkc, bvb, rqk, rv, buffers,
                              programs, second_half[1] if hh == 0 else None)

        def half_weights(tag, low_rank, hh, HD, EC, f1, r1, rqk, rv):
            name = f"{tag}{hh + 1}"
            f, r = Area(fa, F_SIZE, f1), Area(ra, R_SIZE, r1)
            qt, kt = f.take(EC, T), f.take(EC, T)
            f2 = f.at
            heads = slice(hh * HD, (hh + 1) * HD)
            wo = r.take(EC, D), r.take(EC, D)
            tail = Area(fa, F_SIZE, F_SIZE - 4 * HD).take(4, HD)
            staging = [tail, f.take(4, HD), tail]
            if low_rank:
                wv, r2 = (r.take(HD), r.take(HD)), r.at
                r.at += 4096
                wqk = (r.take(HD), r.take(HD))
                weights = [(*wqk, d["L1_attn_fcqk"][:, heads]), (*wv, d["L1_attn_fcvv"][:, heads]),
                           (*wo, d["L1_attn_fco_w"][heads, :].rearrange("(c p) n -> p c n", p=P))]
                staging = [tail[:, 0, :], tail[:, 1, :], staging[1]]
                w = (wqk, wqk, wv, wo)
            else:
                wv, r2 = (r.take(DC, HD), r.take(DC, HD)), r.at
                wk, wq = ((r.take(DC, HD), r.take(DC, HD)) for _ in range(2))
                qkv, inner = d["L0_attn_w_qkvT"], 2 * HD

                def part(k):
                    return qkv[:, k * inner + hh * HD:k * inner + (hh + 1) * HD].rearrange("(c p) n -> p c n", p=P)
                weights = [(*wq, part(0)), (*wk, part(1)), (*wv, part(2)),
                           (*wo, d["L0_attn_w_outT"][heads, :].rearrange("(c p) n -> p c n", p=P))]
                w = (wq, wk, wv, wo)
            if hh == 0:
                programs = split_programs(name, weights, staging if low_rank else staging[:2])
            else:
                programs = (split_programs(name, weights[:1], staging[:1]),
                            split_programs(name + "r", weights[1:], staging[1:]))
            return (qt, kt, f2, r2, w), programs

        def half_of_heads(tag, low_rank, hh, scale, HD, EC, bo, pb, mask, ss, bqc, bkc, bvb, rqk, rv, buffers, programs,
                          following):
            name = f"{tag}{hh + 1}"
            heads = slice(hh * HD, (hh + 1) * HD)
            qt, kt, f2, r2, (wq, wk, wv, wo) = buffers
            wqk = wq
            s_w = programs[3] if hh == 0 else programs[0][3] + programs[1][3]
            s_mm, s_out = sem(f"{name}_qk_product"), sem(f"{name}_qk_taken")
            jobs = [(k, e, h) for k in range(2) for e in range(EC) for h in range(NHALF)]
            NB = 4

            with nc.Block() as block:
                if hh == 0:
                    @block.gpsimd
                    def _(eng):
                        pool.tensor_tensor(x[:], x[:], bo.unsqueeze(1).to_broadcast([P, NT, D]), ALU.add)
                else:
                    @block.sync
                    def _(eng):
                        programs[1][0](eng)

                    @block.gpsimd
                    def _(eng):
                        programs[1][2](eng, pool, range(3))

                    @block.scalar
                    def _(eng):
                        programs[1][1](eng)

                @block.vector
                def _(eng):
                    for j, (k, e, h) in enumerate(jobs):
                        eng.wait_ge(s_mm, j + 1)
                        dst = (qt, kt)[k][:, e, h * HALF:(h + 1) * HALF]
                        if low_rank:
                            b = (bqc, bkc)[k][:, hh * EC + e:hh * EC + e + 1]
                            ins = dve.tensor_scalar(dst, banks[:, j % NB, :], b, None, ALU.add)
                        else:
                            ins = dve.tensor_copy(dst, banks[:, j % NB, :])
                        ins.then_inc(s_out, 1)

                @block.tensor
                def _(eng):
                    for j, (k, e, h) in enumerate(jobs):
                        if j >= NB:
                            eng.wait_ge(s_out, j - NB + 1)
                        cols, tok = slice(e * P, (e + 1) * P), slice(h * HALF, (h + 1) * HALF)
                        eng.wait_ge(s_w[0 if low_rank else k], 1)
                        if low_rank:
                            rows = slice(DH * k, DH * k + DH)
                            ins = mm3(banks[:, j % NB, :], wqk[0][rows, cols], wqk[1][rows, cols],
                                      rqk[0][rows, tok], rqk[1][rows, tok])
                        else:
                            w = (wq, wk)[k]
                            for c in range(DC):
                                ins = mm3(banks[:, j % NB, :], w[0][:, c, cols], w[1][:, c, cols], xh[:, c, tok],
                                          xl[:, c, tok], c == 0, c == DC - 1)
                        ins.then_inc(s_mm, 1)

            f, r = Area(fa, F_SIZE, f2), Area(ra, R_SIZE, r2)
            qg, kg, vg = ([f.take(EC, P) for _ in range(2)] for _ in range(3))
            sh, ex = ([f.take(HH, NQ) for _ in range(2)] for _ in range(2))
            mx, sums, rinv = (f.take(2, HH) for _ in range(3))
            xg = [(r.take(P), r.take(P)) if low_rank else (r.take(DC, P), r.take(DC, P)) for _ in range(2)]
            ot = [(r.take(EC, P), r.take(EC, P)) for _ in range(2)]
            (s_g, s_v, s_vg, s_s, s_sh, s_ex, s_pb, s_o, s_oh, s_ol, s_y, s_xa, s_links) = (
                sem(f"{name}_{n}") for n in ("tile", "v", "v_kept", "scores", "shifted", "exp", "p_turned", "o",
                                             "o_high", "o_low", "out", "x_added", "links"))
            s_passed, s_qk, s_vk = (sem(f"{name}_{n}") for n in ("passed", "qk_tile", "v_unbiased"))
            src = rv if low_rank else (xh, xl)
            if not low_rank:
                s_vk = s_vg

            with nc.Block() as block:
                if hh == 0:
                    @block.sync
                    def _(eng):
                        following[0][0](eng)

                @block.gpsimd
                def _(eng):
                    def x_tile(n, u):
                        eng.wait_ge(s_v, n + 1)
                        eng.wait_ge(s_w[0], 1)
                        for part in range(2):
                            if low_rank:
                                ins = pool.tensor_copy(xg[u][part], src[part][:, bass.ts(n, P)])
                            else:
                                ins = pool.tensor_copy(xg[u][part], src[part][:, :, bass.ts(n, P)])
                        ins.then_inc(s_g, 1)

                    def v_bias(n, u):
                        if low_rank:
                            eng.wait_ge(s_vk, n + 1)
                            v = vg[u].rearrange("p c t -> p (c t)")
                            pool.tensor_tensor(v, v, bvb[:, heads], ALU.add).then_inc(s_vg, 1)

                    x_tile(0, 0)
                    x_tile(1, 1)
                    v_bias(0, 0)
                    if hh == 0:
                        following[0][2](eng, pool, range(1))
                    with pool.Fori(0, NT // 2 - 1) as i:
                        for u in range(2):
                            x_tile(2 * i + u + 2, u)
                            v_bias(2 * i + u + 1, 1 - u)
                    v_bias(NT - 1, 1)

                @block.scalar
                def _(eng):
                    def qk_tile(n, u):
                        eng.wait_ge(s_s, n + 1)
                        act.activation(qg[u], qt[:, :, bass.ts(n, P)], ACT.Copy)
                        act.activation(kg[u], kt[:, :, bass.ts(n, P)], ACT.Copy).then_inc(s_qk, 1)

                    def exps(n, u):
                        eng.wait_ge(s_sh, n + 1)
                        act.activation(ex[u], sh[u], ACT.Exp, scale=scale).then_inc(s_ex, 1)

                    def keep_v(n, u):
                        eng.wait_ge(s_v, n + 1 + LEAD)
                        eng.wait_ge(s_o, n + 1)
                        act.activation(vg[u], chunks(banks[:, 4 * u, :]), ACT.Copy).then_inc(s_vk, 1)

                    def o_high(n, u):
                        eng.wait_ge(s_o, n + 1 + LEAD)
                        act.activation(ot[u][0], chunks(banks[:, 4 * u + 3, :]), ACT.Copy).then_inc(s_oh, 1)

                    qk_tile(0, 0)
                    qk_tile(1, 1)
                    exps(0, 0)
                    keep_v(0, 0)
                    if hh == 0:
                        following[0][1](eng)
                    with act.Fori(0, NT // 2 - 1) as i:
                        for u in range(2):
                            n = 2 * i + u
                            qk_tile(n + 2, u)
                            exps(n + 1, 1 - u)
                            o_high(n, u)
                            keep_v(n + 1, 1 - u)
                    exps(NT - 1, 1)
                    o_high(NT - 2, 0)
                    keep_v(NT - 1, 1)
                    o_high(NT - 1, 1)

                @block.vector
                def _(eng):
                    links = Links(eng, s_links)
                    eng.sem_inc(s_xa, LEAD)

                    def shifted(n, u):
                        bs = banks[:, 4 * u + 1:4 * u + 3, :].rearrange("p k (h t) -> p (k h) t", h=4)
                        eng.wait_ge(s_s, n + 1 + LEAD)
                        eng.sem_inc(s_passed, 1)
                        for j in range(SEQ):
                            rows = slice(NQ * j, NQ * j + NQ)
                            if low_rank:
                                ins = dve.tensor_copy(ss[u][rows], bs[rows, :, rows])
                            else:
                                ins = dve.copy_predicated(ss[u][rows], mask[rows].bitcast(U32), bs[rows, :, rows])
                        links.link(ins)
                        links.link(dve.reduce_max(mx[:, u, :], ss[u], AX_X))
                        dve.tensor_tensor(sh[u], ss[u], mx[:, u, :].unsqueeze(2).to_broadcast([P, HH, NQ]),
                                          ALU.subtract).then_inc(s_sh, 1)

                    def o_low(n, u):
                        eng.wait_ge(s_oh, n + 1)
                        dve.tensor_tensor(ot[u][1], chunks(banks[:, 4 * u + 3, :]), ot[u][0].bitcast(F32),
                                          ALU.subtract).then_inc(s_ol, 1)

                    def turned(n, u):
                        eng.wait_ge(s_ex, n + 1)
                        links.link(dve.reduce_sum(sums[:, u, :], ex[u], AX_X))
                        links.link(dve.reciprocal(rinv[:, u, :], sums[:, u, :]))
                        links.link(dve.tensor_tensor(ex[u], ex[u], rinv[:, u, :].unsqueeze(2).to_broadcast([P, HH, NQ]),
                                                     ALU.mult))
                        for j in range(SEQ):
                            rows = slice(NQ * j, NQ * j + NQ)
                            ins = dve.transpose(pb[u][rows, :, rows], ex[u][rows])
                        ins.then_inc(s_pb, 1)

                    def add(n, u):
                        eng.wait_ge(s_y, n + 1)
                        dve.tensor_tensor(x[:, n, :], banks[:, 4 * u, :], x[:, n, :], ALU.add).then_inc(s_xa, 1)

                    def step(n, u):
                        shifted(n + 1, 1 - u)
                        o_low(n, u)
                        turned(n + 1, 1 - u)
                        add(n, u)

                    STEPS = 5
                    links.enter(0, STEPS)
                    shifted(0, 0)
                    turned(0, 0)
                    links.leave(1)
                    with dve.Fori(0, NT // 2 - 1) as i:
                        links.enter(i, 2 * STEPS)
                        for u in range(2):
                            step(2 * i + u, u)
                        links.leave(NT // 2 - 1)
                    step(NT - 2, 0)
                    o_low(NT - 1, 1)
                    add(NT - 1, 1)

                @block.tensor
                def _(eng):
                    eng.sem_inc(s_s, LEAD)
                    eng.sem_inc(s_v, LEAD)
                    eng.sem_inc(s_o, LEAD)

                    def scores(n, u):
                        eng.wait_ge(s_qk, n + 1)
                        for h in range(HH):
                            rows = slice(DH * (h % 2), DH * (h % 2) + DH)
                            ins = pe.matmul(banks[:, 4 * u + 1 + h % 2, (h // 2) * P:(h // 2 + 1) * P],
                                            qg[u][rows, h // 2, :], kg[u][rows, h // 2, :], start=True, stop=True)
                        ins.then_inc(s_s, 1)

                    def values(n, u):
                        eng.wait_ge(s_g, n + 1)
                        eng.wait_ge(s_xa, n + 1)
                        if low_rank:
                            ins = mm3(banks[:, 4 * u, :], xg[u][0][0:DH], xg[u][1][0:DH], wv[0][0:DH], wv[1][0:DH])
                        else:
                            for c in range(DC):
                                ins = mm3(banks[:, 4 * u, :], xg[u][0][:, c, :], xg[u][1][:, c, :], wv[0][:, c, :],
                                          wv[1][:, c, :], c == 0, c == DC - 1)
                        ins.then_inc(s_v, 1)

                    def p_v(n, u):
                        eng.wait_ge(s_vg, n + 1)
                        eng.wait_ge(s_pb, n + 1)
                        for h in range(HH):
                            rows = slice(DH * (h % 2), DH * (h % 2) + DH)
                            v = vg[u].rearrange("p c t -> p (c t)")
                            ins = pe.matmul(banks[rows, 4 * u + 3, (h // 2) * P:(h // 2 + 1) * P],
                                            v[:, h * DH:(h + 1) * DH], pb[u][:, (h % 2) * 4 + h // 2, :],
                                            start=True, stop=True)
                        ins.then_inc(s_o, 1)

                    def output(n, u):
                        eng.wait_ge(s_ol, n + 1)
                        for c in range(EC):
                            ins = mm3(banks[:, 4 * u, :], ot[u][0][:, c, :], ot[u][1][:, c, :], wo[0][:, c, :],
                                      wo[1][:, c, :], c == 0, c == EC - 1)
                        ins.then_inc(s_y, 1)

                    def step(n, u):
                        scores(n + 1, 1 - u)
                        p_v(n, u)
                        values(n + 1, 1 - u)
                        output(n, u)

                    scores(0, 0)
                    values(0, 0)
                    with pe.Fori(0, NT // 2 - 1) as i:
                        for u in range(2):
                            step(2 * i + u, u)
                    step(NT - 2, 0)
                    p_v(NT - 1, 1)
                    output(NT - 1, 1)

        class Plan:

            def __init__(self, layer):
                self.layer, self.experts, self.choices = layer, (E0, E1)[layer], (K0, K1)[layer]
                self.routed = (self.choices * T + self.experts * (CAP - 1)) // CAP
                self.shared = layer == 0
                self.kinds = self.choices + self.shared
                self.tiles = self.routed + (T // CAP if self.shared else 0)
                self.units = (I0, I1)[layer] // P
                f = Area(fa, F_SIZE)
                self.slot = f.take(self.kinds, NT)
                self.weight = f.take(self.kinds, NT)
                self.token = f.take(2 * self.tiles)
                self.expert = f.take(self.tiles)
                self.at = f.at

        def routing(tag, plan):
            layer, E, K = plan.layer, plan.experts, plan.choices
            KN, H = plan.kinds * NT, 2 * plan.tiles
            f = Area(fa, F_SIZE, plan.at)
            gate, gbias = f.take(DC, P), f.take(E)
            logits = f.take(T)
            lg, sc, sel, t1 = (f.take(NT, E) for _ in range(4))
            r = Area(ra, R_SIZE)
            gate_high, gate_low, kept = r.take(DC, P), r.take(DC, P), r.take(NT, E)
            gt, eq = f.take(NT, E, E), f.take(NT, E, E)
            tri = f.take(E, E)
            gm, gk = f.take(NT, G0), f.take(NT, G0)
            mx, sm, rank = f.take(NT), f.take(NT), f.take(NT, E)
            before, end, first_slot = f.take(E), f.take(E), f.take(NT, E)
            need = [f.take(E) for _ in range(T // CAP)]
            choice_slot, choice_weight = f.take(plan.kinds, NT, E), f.take(plan.kinds, NT, E)
            slot, group, place, bits = (f.take(plan.kinds, NT) for _ in range(4))
            from_zero, ids = f.take(P), f.take(NT)
            in_block, in_place = r.take(KN, H), r.take(KN, P)
            tile_end, tile_expert = f.take(plan.tiles, E), f.take(plan.tiles)
            s_ld, s_tri, s_clear, s_gate, s_mm, s_act, s_in, s_kept, s_spread, s_links = (
                sem(f"{tag}_{n}") for n in ("gate", "earlier", "cleared", "gate_split", "products", "activated", "shifted",
                                            "kept", "spread", "links"))

            def compare(links, v, n, dst):
                a4, b4 = gt[:, :, 0:n, 0:n], eq[:, :, 0:n, 0:n]
                if n == E:
                    a4, b4 = gt, eq
                other = v.unsqueeze(2).to_broadcast([P, NT, n, n])
                own = v.unsqueeze(3).to_broadcast([P, NT, n, n])
                dve.tensor_tensor(a4, other, own, ALU.is_gt)
                links.link(dve.tensor_tensor(b4, other, own, ALU.is_equal))
                links.link(dve.tensor_tensor(b4, b4, tri[:, 0:n, 0:n].unsqueeze(1).to_broadcast([P, NT, n, n]),
                                             ALU.mult))
                links.link(dve.tensor_tensor(a4, a4, b4, ALU.add))
                links.link(dve.reduce_sum(dst, a4, AX_X))

            with nc.Block() as block:
                @block.sync
                def _(eng):
                    eng.wait_ge(s_clear, 1)
                    eng.dma_start(gate[:, :, 0:E], d["L0_ffn_gateT" if layer == 0 else "L1_ffn_gateT"]
                                  .rearrange("(c p) e -> p c e", p=P)).then_inc(s_ld, 16)
                    if layer == 0:
                        eng.dma_start(gbias, d["L0_ffn_gate_bias"].partition_broadcast(P)).then_inc(s_ld, 16)

                @block.gpsimd
                def _(eng):
                    pool.memset(gate, 0.0).then_inc(s_clear, 1)
                    pool.memset(tri, 1.0).then_inc(s_tri, 1)
                    eng.wait_ge(s_tri, 1)
                    pool.affine_select(out=tri, in_=tri, compare_op=ALU.is_gt, fill=0.0, base=0,
                                       pattern=[[1, E], [-1, E]], channel_multiplier=0)
                    exact = dict(allow_small_or_imprecise_dtypes=True)
                    pool.iota(from_zero, [[1, P]], base=0, channel_multiplier=0, **exact)
                    pool.iota(ids, [[P, NT]], base=0, channel_multiplier=1, **exact).then_inc(s_tri, 1)

                @block.scalar
                def _(eng):
                    eng.wait_ge(s_mm, 1)
                    act.activation(logits[0:E].rearrange("e (h t) -> e h t", h=NHALF), banks[0:E, 4:4 + NHALF, :],
                                   ACT.Copy).then_inc(s_act, 1)
                    if layer == 0:
                        eng.wait_ge(s_mm, 2)
                        act.activation(sc.rearrange("p t e -> p (t e)"), banks[:, 0, 0:NT * E],
                                       ACT.Sigmoid).then_inc(s_act, 1)
                    else:
                        eng.wait_ge(s_in, 1)
                        act.activation(sc, t1, ACT.Exp).then_inc(s_act, 1)

                @block.vector
                def _(eng):
                    links = Links(eng, s_links)
                    eng.wait_ge(s_tri, 2)
                    eng.wait_ge(s_ld, 32 if layer == 0 else 16)
                    links.link(dve.tensor_copy(gate_high, gate))
                    dve.tensor_tensor(gate_low, gate, gate_high.bitcast(F32), ALU.subtract).then_inc(s_gate, 1)
                    if layer == 0:
                        eng.wait_ge(s_act, 2)
                        links.link(dve.tensor_tensor(sel, sc, gbias.unsqueeze(1).to_broadcast([P, NT, E]), ALU.add))
                        links.link(dve.reduce_max(gm, sel.rearrange("p t (g e) -> p t g e", g=G0), AX_X))
                        compare(links, gm, G0, gk)
                        links.link(dve.tensor_scalar(gm, gk, float(GK0), None, ALU.is_lt))
                        links.link(dve.tensor_scalar(gk, gm, -1.0, FAR, ALU.add, ALU.mult))
                        s4 = sel.rearrange("p t (g e) -> p t g e", g=G0)
                        shape = [P, NT, G0, E // G0]
                        links.link(dve.tensor_tensor(s4, s4, gm.unsqueeze(3).to_broadcast(shape), ALU.mult))
                        links.link(dve.tensor_tensor(s4, s4, gk.unsqueeze(3).to_broadcast(shape), ALU.add))
                    else:
                        eng.wait_ge(s_mm, 2)
                        links.link(dve.tensor_copy(sel.rearrange("p t e -> p (t e)"), banks[:, 0, 0:NT * E]))
                        links.link(dve.reduce_max(mx, sel, AX_X))
                        dve.tensor_tensor(t1, sel, mx.unsqueeze(2).to_broadcast([P, NT, E]),
                                          ALU.subtract).then_inc(s_in, 1)
                        eng.wait_ge(s_act, 2)
                    compare(links, sel, E, rank)
                    dve.tensor_scalar(kept, rank, float(K), None, ALU.is_lt).then_inc(s_kept, 1)
                    if layer == 0:
                        weight = sc
                    else:
                        eng.wait_ge(s_kept, 1)
                        links.link(dve.tensor_tensor(lg, kept.bitcast(F32), sc, ALU.mult))
                        links.link(dve.reduce_sum(sm, lg, AX_X))
                        links.link(dve.reciprocal(mx, sm))
                        links.link(dve.tensor_tensor(t1, lg, mx.unsqueeze(2).to_broadcast([P, NT, E]), ALU.mult))
                        weight = t1
                    for k in range(K):
                        dve.scalar_tensor_tensor(choice_weight[:, k, :, :], rank, float(k), weight, ALU.is_equal, ALU.mult)
                    eng.wait_ge(s_mm, 3)
                    total = banks[:, 2, 0:E]
                    links.link(dve.tensor_scalar(need[0], total, 0.0, None, ALU.is_gt))
                    for j in range(1, T // CAP):
                        links.link(dve.scalar_tensor_tensor(need[j], total, float(CAP * j), need[j - 1], ALU.is_gt, ALU.add))
                    tiles = need[-1]
                    links.link(dve.tensor_tensor(gt[:, 0, :, :], tiles.unsqueeze(1).to_broadcast([P, E, E]), tri, ALU.mult))
                    links.link(dve.reduce_sum(before, gt[:, 0, :, :], AX_X))
                    dve.tensor_tensor(end, before, tiles, ALU.add)
                    links.link(dve.scalar_tensor_tensor(
                        first_slot, before.unsqueeze(1).to_broadcast([P, NT, E]), float(CAP),
                        banks[:, 1, 0:NT * E].rearrange("p (t e) -> p t e", t=NT), ALU.mult, ALU.add))
                    for k in range(K):
                        ins = dve.scalar_tensor_tensor(choice_slot[:, k, :, :], rank, float(k), first_slot, ALU.is_equal, ALU.mult)
                    links.link(ins)
                    dve.reduce_sum(plan.weight[:, 0:K, :], choice_weight[:, 0:K, :, :], AX_X)
                    if plan.shared:
                        dve.memset(plan.weight[:, K, :], 1.0)
                        dve.tensor_scalar(slot[:, K, :], ids, float(CAP * plan.routed), None, ALU.add)
                    links.link(dve.reduce_sum(slot[:, 0:K, :], choice_slot[:, 0:K, :, :], AX_X))
                    links.link(dve.tensor_copy(plan.slot.bitcast(U32), slot))
                    for dst, amount, op in ((group, P.bit_length() - 1, ALU.logical_shift_right),
                                            (place, P - 1, ALU.bitwise_and)):
                        links.link(dve.tensor_scalar(bits.bitcast(U32), plan.slot.bitcast(U32), amount, None, op))
                        links.link(dve.tensor_copy(dst, bits.bitcast(U32)))
                    for k in range(plan.kinds):
                        own = slice(k * NT, (k + 1) * NT)
                        dve.tensor_tensor(in_place[:, own, :], from_zero.unsqueeze(1).to_broadcast([P, NT, P]),
                                          place[:, k, :].unsqueeze(2).to_broadcast([P, NT, P]), ALU.is_equal)
                        part, shape = in_block[:, own, :], [P, NT, H]
                        links.link(dve.tensor_tensor(part, from_zero[:, 0:H].unsqueeze(1).to_broadcast(shape),
                                                     group[:, k, :].unsqueeze(2).to_broadcast(shape), ALU.is_equal))
                        dve.tensor_tensor(part, part.bitcast(F32), ids.unsqueeze(2).to_broadcast(shape),
                                          ALU.mult).then_inc(s_spread, 1)
                    shape = [P, plan.tiles, E]
                    links.link(dve.tensor_tensor(tile_end, end.unsqueeze(1).to_broadcast(shape),
                                                 from_zero[:, 0:plan.tiles].unsqueeze(2).to_broadcast(shape), ALU.is_le))
                    links.link(dve.reduce_sum(tile_expert, tile_end, AX_X))
                    links.link(dve.tensor_scalar(tile_expert, tile_expert, float(E - 1), None, ALU.min))
                    if plan.shared:
                        links.link(dve.memset(tile_expert[:, plan.routed:plan.tiles], float(E)))
                    dve.tensor_copy(plan.expert.bitcast(U32), tile_expert)
                    eng.wait_ge(s_mm, 4)
                    dve.tensor_copy(plan.token.bitcast(U32), banks[:, 3, 0:H])

                @block.tensor
                def _(eng):
                    eng.wait_ge(s_gate, 1)
                    for h in range(NHALF):
                        tok = slice(h * HALF, (h + 1) * HALF)
                        for c in range(DC):
                            ins = mm3(banks[:, 4 + h, :], gate_high[:, c, :], gate_low[:, c, :], xh[:, c, tok],
                                      xl[:, c, tok], c == 0, c == DC - 1)
                    ins.then_inc(s_mm, 1)
                    eng.wait_ge(s_act, 1)
                    for t in range(NT):
                        ins = pe.transpose(banks[:, 0, t * E:(t + 1) * E], logits[0:E, t * P:(t + 1) * P], ident[0:E, 0:E])
                    ins.then_inc(s_mm, 1)
                    eng.wait_ge(s_kept, 1)
                    before_own = banks[:, 1, 0:NT * E].rearrange("p (t e) -> p t e", e=E)
                    for t in range(NT):
                        pe.matmul(banks[:, 2, 0:E], ones[:], kept[:, t, :], start=t == 0, stop=t == NT - 1)
                    pe.matmul(before_own, earlier[:], kept, start=True, stop=False)
                    for t in reversed(range(NT - 1)):
                        ins = pe.matmul(before_own[:, t + 1:NT, :], ones[:], kept[:, t:t + 1, :]
                                        .to_broadcast([P, NT - 1 - t, E]), start=False, stop=t == 0)
                    ins.then_inc(s_mm, 1)
                    for m in range(KN):
                        if m % NT == 0:
                            eng.wait_ge(s_spread, m // NT + 1)
                        ins = pe.matmul(banks[:, 3, 0:H], in_place[:, m, :], in_block[:, m, :], start=m == 0,
                                        stop=m == KN - 1)
                    ins.then_inc(s_mm, 1)

        def experts(tag, plan, w):
            U, TILES, W = plan.units, plan.tiles, WEIGHT_BUFFERS
            total = U * TILES
            y_dram = nc.dram_tensor(f"{tag}_y_scratch", [TILES * CAP, D], F32, kind="Internal").ap()
            f, r = Area(fa, F_SIZE, plan.at), Area(ra, R_SIZE)
            st = [f.take(3, D) for _ in range(W)]
            sg, hf = ([f.take(CAP) for _ in range(2)] for _ in range(2))
            xt, ys = ([f.take(2, D) for _ in range(2)] for _ in range(2))
            ids, table = [f.take(2) for _ in range(2)], f.take(1)
            wh, wl = ([r.take(3, D) for _ in range(W)] for _ in range(2))
            hh_, hl = ([r.take(CAP) for _ in range(2)] for _ in range(2))
            gh, gl = ([r.take(DC, CAP) for _ in range(2)] for _ in range(2))
            s_ld = [sem(f"{tag}_loaded{b}") for b in range(W)]
            s_rows = [gather_sem(f"{tag}_rows{u}") for u in range(2)]
            s_stored = [sem(f"{tag}_stored{u}") for u in range(2)]
            (s_wh, s_wp, s_wd, s_h, s_sg, s_hf, s_hh, s_hl, s_y, s_kept, s_ids, s_passed, s_turned, s_xh, s_xl) = (
                sem(f"{tag}_{n}") for n in ("w_high", "w_low_pool", "w_low_vector", "h_products", "silu", "h", "h_high",
                                            "h_low", "y", "y_kept", "ids", "passed", "turned", "x_high", "x_low"))
            HB, YB, XB = 0, 2, 4
            PEELED = 3
            PAIRED = (TILES - PEELED) // 2
            assert (TILES - PEELED) % 2 == 0 and (2 * U) % W == 0
            TURN = U - 2

            def split_rows(ap):
                return ap.rearrange("p (s t) -> p s t", s=2)

            def all_tiles(engine, tile, first=lambda: None):
                with engine.Fori(0, PAIRED) as i:
                    first()
                    for u in range(2):
                        tile(2 * i + u, u, i, False)
                for j in range(2 * PAIRED, TILES):
                    tile(j, j % 2, j // 2, True)

            def there(n, limit):
                return not isinstance(n, int) or n < limit

            with nc.Block() as block:
                @block.sync
                def _(eng):
                    def tile(j, u, i, _):
                        e = eng.value_load(plan.expert.bitcast(U32)[0:1, bass.ds(j, 1)], min_val=0,
                                           max_val=w.shape[0] // U - 1)
                        for q in range(U):
                            n, b = U * j + q, (U * u + q) % W
                            eng.wait_ge(s_wp, n + 1)
                            eng.wait_ge(s_wd, n + 1)
                            eng.dma_start(st[b], w[e * U + q]).then_inc(s_ld[b], 16)
                    all_tiles(eng, tile)

                @block.gpsimd
                def _(eng):
                    def gather(j, u):
                        eng.wait_ge(s_turned, j + 1)
                        eng.sem_inc(s_passed, 1)
                        pool.tensor_copy(ids[u].bitcast(U32), plan.token.bitcast(U32)[:, bass.ts(j, 2)]).then_inc(s_ids, 1)
                        eng.wait_ge(s_ids, j + 1)
                        eng.sem_inc(s_passed, 1)
                        for s in range(2):
                            pool.indirect_dma_start(xt[u][:, s, :], None, normed_dram, bass.IndirectOffsetOnAxis(
                                ap=ids[u].bitcast(U32)[:, s:s + 1], axis=0)).then_inc(s_rows[u], 16)

                    def weights_low(n, b):
                        eng.wait_ge(s_wh, n + 1)
                        pool.tensor_tensor(wl[b][:, 0:2, :], st[b][:, 0:2, :], wh[b][:, 0:2, :].bitcast(F32),
                                           ALU.subtract).then_inc(s_wp, 1)

                    eng.sem_inc(s_wp, W)
                    gather(0, 0)
                    gather(1, 1)
                    for n in range(W - 1):
                        weights_low(n, n)
                    gather(2, 0)

                    def tile(j, u, i, _):
                        for q in range(U):
                            if there(U * j + q + W - 1, total):
                                weights_low(U * j + q + (W - 1), (U * u + q + W - 1) % W)
                            if q == TURN and there(j + 3, TILES):
                                gather(j + 3, 1 - u)
                    all_tiles(eng, tile)

                @block.scalar
                def _(eng):
                    def weights_high(n, b, k):
                        eng.wait_ge(s_ld[b], 16 * k + 16)
                        eng.wait_ge(s_y, n + 1)
                        act.activation(wh[b], st[b], ACT.Copy).then_inc(s_wh, 1)

                    def rows_high(j, u):
                        eng.wait_ge(s_turned, j + 1 + LEAD)
                        act.activation(gh[u].rearrange("p c (s t) -> p s c t", s=2),
                                       banks[:, XB:XB + 2, :].rearrange("p s (c t) -> p s c t", c=DC),
                                       ACT.Copy).then_inc(s_xh, 1)

                    def keep_y(j, u, i):
                        eng.wait_ge(s_y, U * j + (U + W))
                        eng.wait_ge(s_stored[u], 16 * i + 16)
                        act.activation(ys[u], banks[:, YB:YB + 2, :], ACT.Copy).then_inc(s_kept, 1)
                        eng.wait_ge(s_kept, j + 2)
                        eng.dma_start(y_dram.rearrange("(j s p) d -> j p s d", s=2, p=P)[j],
                                      ys[u]).then_inc(s_stored[u], 16)

                    def hidden(n, b):
                        eng.wait_ge(s_h, n + 1)
                        act.activation(sg[b], banks[:, HB + b, 0:CAP], ACT.Silu).then_inc(s_sg, 1)
                        eng.wait_ge(s_hf, n + 1 + LEAD)
                        eng.wait_ge(s_y, n + (W - 1))
                        act.activation(hh_[b], hf[b], ACT.Copy).then_inc(s_hh, 1)

                    eng.sem_inc(s_kept, 1)
                    for u in range(2):
                        eng.sem_inc(s_stored[u], 16)
                    for n in range(W - 1):
                        weights_high(n, n, 0)
                        if n == 0:
                            rows_high(0, 0)

                    def tile(j, u, i, _):
                        for q in range(U):
                            n = U * j + q
                            hidden(n, q % 2)
                            if q == TURN and there(j + 1, TILES):
                                rows_high(j + 1, 1 - u)
                            if there(n + W - 1, total):
                                ahead = U * u + q + W - 1
                                weights_high(n + (W - 1), ahead % W, (2 * U // W) * i + ahead // W)
                            if q == U - 1:
                                keep_y(j, u, i)
                    all_tiles(eng, tile, lambda: act.activation(table, epst[:], ACT.Silu))
                    for u in range(2):
                        eng.wait_ge(s_stored[u], 16 + 16 * ((TILES + 1 - u) // 2))

                @block.vector
                def _(eng):
                    def weights_low(n, b):
                        eng.wait_ge(s_wh, n + 1)
                        dve.tensor_tensor(wl[b][:, 2, :], st[b][:, 2, :], wh[b][:, 2, :].bitcast(F32),
                                          ALU.subtract).then_inc(s_wd, 1)

                    def rows_low(j, u):
                        eng.wait_ge(s_xh, j + 1)
                        for s in range(2):
                            cols = slice(s * P, (s + 1) * P)
                            ins = dve.tensor_tensor(gl[u][:, :, cols], chunks(banks[:, XB + s, :]),
                                                    gh[u][:, :, cols].bitcast(F32), ALU.subtract)
                        ins.then_inc(s_xl, 1)

                    eng.sem_inc(s_wd, W)
                    eng.sem_inc(s_hf, LEAD)
                    eng.sem_inc(s_xl, 1)
                    for n in range(W - 1):
                        weights_low(n, n)
                        if n == 0:
                            rows_low(0, 0)

                    def tile(j, u, i, _):
                        for q in range(U):
                            n, b = U * j + q, q % 2
                            eng.wait_ge(s_sg, n + 1)
                            dve.tensor_tensor(hf[b], banks[:, HB + b, CAP:2 * CAP], sg[b], ALU.mult).then_inc(s_hf, 1)
                            eng.wait_ge(s_hh, n + 1)
                            dve.tensor_tensor(hl[b], hf[b], hh_[b].bitcast(F32), ALU.subtract).then_inc(s_hl, 1)
                            if q == TURN and there(j + 1, TILES):
                                rows_low(j + 1, 1 - u)
                            if there(n + W - 1, total):
                                weights_low(n + (W - 1), (U * u + q + W - 1) % W)
                    all_tiles(eng, tile)

                @block.tensor
                def _(eng):
                    eng.sem_inc(s_y, W)
                    eng.sem_inc(s_turned, LEAD)

                    def turn(j, u, i):
                        eng.wait_ge(s_rows[u], 32 * i + 32)
                        eng.wait_ge(s_xl, j + 1)
                        for s in range(2):
                            for c in range(DC):
                                cols = slice(c * P, (c + 1) * P)
                                ins = pe.transpose(banks[:, XB + s, cols], xt[u][:, s, cols], ident[:])
                        ins.then_inc(s_turned, 1)

                    def up(n, j, u, q, b):
                        if q == 0:
                            eng.wait_ge(s_xl, j + 2)
                        eng.wait_ge(s_wp, n + 1 + W)
                        eng.wait_ge(s_hf, n + 1)
                        for k in range(2):
                            for c in range(DC):
                                cols = slice(c * P, (c + 1) * P)
                                ins = mm3(banks[:, HB + q % 2, k * CAP:(k + 1) * CAP], wh[b][:, k, cols], wl[b][:, k, cols],
                                          gh[u][:, c, :], gl[u][:, c, :], c == 0, c == DC - 1)
                        ins.then_inc(s_h, 1)

                    def down(n, j, q, b):
                        eng.wait_ge(s_hl, n + 1)
                        eng.wait_ge(s_wd, n + 1 + W)
                        if q == 0:
                            eng.wait_ge(s_kept, j + 1)
                        for s in range(2):
                            cols = slice(s * P, (s + 1) * P)
                            ins = mm3(banks[:, YB + s, :], hh_[q % 2][:, cols], hl[q % 2][:, cols], wh[b][:, 2, :],
                                      wl[b][:, 2, :], q == 0, q == U - 1)
                        ins.then_inc(s_y, 1)

                    def tile(j, u, i, _):
                        for q in range(U):
                            n = U * j + q
                            if q == TURN and there(j + 1, TILES):
                                turn(j + 1, 1 - u, i + u)
                            if q < U - 1:
                                up(n + 1, j, u, q + 1, (U * u + q + 1) % W)
                            elif there(j + 1, TILES):
                                up(n + 1, j + 1, 1 - u, 0, (U * u + q + 1) % W)
                            down(n, j, q, (U * u + q) % W)

                    turn(0, 0, 0)
                    up(0, 0, 0, 0, 0)
                    all_tiles(eng, tile)

            yt = [Area(fa, F_SIZE, plan.at + D * m).take(D) for m in range(plan.kinds * NT // 2)]
            yt += [Area(ra, R_SIZE, D * m).take(D).bitcast(F32) for m in range(plan.kinds * NT // 2)]
            QUARTER = NT // 2
            s_got = [gather_sem(f"{tag}_y_rows{m}") for m in range(plan.kinds * 2)]
            s_links = sem(f"{tag}_sum_links")
            with nc.Block() as block:
                @block.gpsimd
                def _(eng):
                    for m in range(plan.kinds * NT):
                        k, t = divmod(m, NT)
                        pool.indirect_dma_start(yt[m], None, y_dram, bass.IndirectOffsetOnAxis(
                            ap=plan.slot.bitcast(U32)[:, k, t:t + 1], axis=0)).then_inc(s_got[m // QUARTER], 16)

                @block.vector
                def _(eng):
                    links = Links(eng, s_links)
                    for m in range(plan.kinds * NT):
                        k, t = divmod(m, NT)
                        if m % QUARTER == 0:
                            eng.wait_ge(s_got[m // QUARTER], 16 * QUARTER)
                        ins = dve.scalar_tensor_tensor(x[:, t, :], yt[m], plan.weight[:, k, t:t + 1], x[:, t, :],
                                                       ALU.mult, ALU.add)
                        if m % QUARTER == QUARTER - 1:
                            links.link(ins)

        def cross_heads():
            scale = float(XD) ** -0.5
            f, r = Area(fa, F_SIZE), Area(ra, R_SIZE)
            qt, bvb, bob = f.take(DC, T), f.take(D), f.take(D)
            bqc, bkc, own = f.take(DC), f.take(DC), f.take(4)
            qblk = [f.take(DC, P) for _ in range(2)]
            stg = [f.take(DC, SE) for _ in range(2)]
            f2 = f.at
            staging = [f.take(DC, D) for _ in range(3)]
            lastT, vl = f.take(DC, B), f.take(D)
            wk, wv, wo = ((r.take(DC, D), r.take(DC, D)) for _ in range(3))
            r2 = r.at
            wq = r.take(DC, D), r.take(DC, D)
            load, high, low, s_w = split_programs("xb", [
                (*wv, columns(d["L1_xattn_W_V"])), (*wq, columns(d["L1_xattn_W_Q"])),
                (*wk, columns(d["L1_xattn_W_K"])), (*wo, columns(d["L1_xattn_W_O"]))], staging)
            layer_norm("nd", ahead=[(load, high, low)])
            s_b, s_mm, s_out, s_vl = sem("xb_biases"), sem("xb_product"), sem("xb_taken"), sem("xb_last_v")
            s_own = sem("xb_own_heads")
            jobs = [(e, h) for e in range(DC) for h in range(NHALF)]
            NB = 4

            with nc.Block() as block:
                @block.sync
                def _(eng):
                    for dst, src in ((bqc, d["L1_xattn_b_Q"]),
                                     (bkc, d["L1_xattn_b_K"]),
                                     (bvb, d["L1_xattn_b_V"].partition_broadcast(P)),
                                     (bob, d["L1_xattn_b_O"].partition_broadcast(P)),
                                     (lastT, d["ctxLastT"])):
                        eng.dma_start(dst, src).then_inc(s_b, 16)
                    eng.wait_ge(s_out, 1)
                    eng.dma_start(vlast_dram, vl[0:B, :]).then_inc(s_vl, 16)
                    eng.wait_ge(s_vl, 16)
                    eng.wait_ge(s_b, 80)

                @block.gpsimd
                def _(eng):
                    for u in range(2):
                        pool.memset(stg[u][:, :, S:SE], 0.0)
                    pool.memset(own, 1.0).then_inc(s_own, 1)
                    eng.wait_ge(s_own, 1)
                    pool.affine_select(out=own, in_=own, compare_op=ALU.is_ge, fill=0.0, base=0,
                                       pattern=[[-XD, 4]], channel_multiplier=1).then_inc(s_own, 1)
                    eng.wait_ge(s_own, 2)
                    pool.affine_select(out=own, in_=own, compare_op=ALU.is_gt, fill=0.0, base=XD,
                                       pattern=[[XD, 4]], channel_multiplier=-1)

                @block.vector
                def _(eng):
                    eng.wait_ge(s_b, 80)
                    eng.wait_ge(s_mm, 1)
                    dve.tensor_tensor(vl[0:B, :], banks[0:B, 7, :], bvb[0:B, :], ALU.add).then_inc(s_out, 1)
                    for j, (e, h) in enumerate(jobs):
                        eng.wait_ge(s_mm, j + 2)
                        dve.tensor_scalar(qt[:, e, h * HALF:(h + 1) * HALF], banks[:, j % NB, :], bqc[:, e:e + 1],
                                          None, ALU.add).then_inc(s_out, 1)

                @block.tensor
                def _(eng):
                    eng.wait_ge(s_b, 80)
                    eng.wait_ge(s_w[0], 1)
                    for c in range(DC):
                        for part in range(2):
                            ins = pe.matmul(banks[0:B, 7, :], lastT[:, c, :], wv[part][:, c, :].bitcast(F32),
                                            start=c + part == 0, stop=c == DC - 1 and part == 1)
                    ins.then_inc(s_mm, 1)
                    eng.wait_ge(s_w[1], 1)
                    for j, (e, h) in enumerate(jobs):
                        if j >= NB:
                            eng.wait_ge(s_out, j - NB + 2)
                        cols, tok = slice(e * P, (e + 1) * P), slice(h * HALF, (h + 1) * HALF)
                        for c in range(DC):
                            ins = mm3(banks[:, j % NB, :], wq[0][:, c, cols], wq[1][:, c, cols], xh[:, c, tok],
                                      xl[:, c, tok], c == 0, c == DC - 1)
                        ins.then_inc(s_mm, 1)

            f, r = Area(fa, F_SIZE, f2), Area(ra, R_SIZE, r2)
            kt = [f.take(DC, SE) for _ in range(2)]
            v = [f.take(2, D) for _ in range(2)]
            vlast = [f.take(D) for _ in range(2)]
            pr = [f.take(DC, SE) for _ in range(2)]
            pt, ot = f.take(3, D), f.take(DC, P)
            mx, bias, rs, rinv = (f.take(2, DC) for _ in range(4))
            cx = [(r.take(DC, SE), r.take(DC, SE)) for _ in range(2)]
            oh, ol = r.take(DC, P), r.take(DC, P)
            s_ld = [sem(f"xb_ctx{u}") for u in range(2)]
            s_vld = [sem(f"xb_vlast{u}") for u in range(2)]
            (s_ch, s_cl, s_kp, s_vp, s_k, s_v, s_qb, s_sc, s_bias, s_ex, s_rinv, s_pn, s_t, s_ta, s_td, s_pv,
             s_o, s_oh, s_ol, s_y, s_x, s_links) = (
                sem(f"xb_{n}") for n in (
                    "ctx_high", "ctx_low", "k_product", "v_product", "k_kept", "v_kept", "q_block", "scores", "bias",
                    "exp", "sums", "p_normed", "p_turned", "p_kept_a", "p_kept_d", "pv", "o_kept", "o_high", "o_low",
                    "out", "x_added", "links"))
            SC = 2
            T0, T1 = 6, 7

            with nc.Block() as block:
                @block.sync
                def _(eng):
                    with eng.Fori(0, B // 2) as i:
                        for u in range(2):
                            n = 2 * i + u
                            eng.wait_ge(s_cl, n + 1)
                            eng.dma_start(stg[u][:, :, 0:S], d["ctxT"][n]).then_inc(s_ld[u], 16)
                            eng.wait_ge(s_pv, n + 1)
                            eng.dma_start(vlast[u][0:1, :], vlast_dram[bass.ds(n, 1), :]).then_inc(s_vld[u], 16)

                @block.gpsimd
                def _(eng):
                    eng.sem_inc(s_cl, LEAD)

                    def ctx_low(n, u):
                        eng.wait_ge(s_ch, n + 1)
                        pool.tensor_tensor(cx[u][1], stg[u], cx[u][0].bitcast(F32), ALU.subtract).then_inc(s_cl, 1)

                    def step(m, u, after):
                        eng.wait_ge(s_sc, m + 1)
                        shape = [P, DC, 4, NQ]
                        pool.tensor_tensor(qblk[u].rearrange("p c (h q) -> p c h q", h=4),
                                           qt[:, :, bass.ts(m, NQ)].unsqueeze(2).to_broadcast(shape),
                                           own.unsqueeze(1).unsqueeze(3).to_broadcast(shape), ALU.mult).then_inc(s_qb, 1)
                        if after:
                            ctx_low(m + 1, 1 - u)
                        eng.wait_ge(s_rinv, m + 1)
                        pool.tensor_tensor(pr[u][:, :, 0:S], pr[u][:, :, 0:S],
                                           rinv[:, u, :].unsqueeze(2).to_broadcast([P, DC, S]),
                                           ALU.mult).then_inc(s_pn, 1)

                    ctx_low(0, 0)
                    step(0, 0, True)
                    with pool.Fori(0, NT - 1) as g:
                        for j in range(SEQ):
                            step(SEQ * g + j + 1, (j + 1) % 2, True)
                    for m in range(B - SEQ + 1, B):
                        step(m, m % 2, m + 1 < B)

                @block.scalar
                def _(eng):
                    def ctx_high(half, n, u):
                        eng.wait_ge(s_ld[u], 16 * half + 16)
                        if not (isinstance(n, int) and n < LEAD):
                            eng.wait_ge(s_vp, 2 * n)
                        act.activation(cx[u][0], stg[u], ACT.Copy).then_inc(s_ch, 1)

                    def keep_k(m, u):
                        for e in range(DC):
                            eng.wait_ge(s_kp, DC * m + (e + 1))
                            if e == 0:
                                eng.wait_ge(s_sc, m + 1)
                            act.activation(kt[u][:, e, :], banks[:, e % 2, 0:SE], ACT.Identity,
                                           bias=bkc[:, e:e + 1]).then_inc(s_k, 1)

                    def exps(m, u):
                        eng.wait_ge(s_bias, m + 1)
                        for c in range(DC):
                            ins = act.activation(pr[u][:, c, 0:S], banks[:, SC + c, 0:S], ACT.Exp,
                                                 bias=bias[:, u, c:c + 1], scale=scale, accum_out=rs[:, u, c:c + 1])
                        ins.then_inc(s_ex, 1)

                    def keep_p(n):
                        eng.wait_ge(s_t, 3 * n + 1)
                        act.activation(pt[:, 0, :], banks[:, T0, :], ACT.Copy).then_inc(s_ta, 1)
                        eng.wait_ge(s_t, 3 * n + 3)
                        act.activation(pt[0:1, 2, :], banks[0:1, 0, :], ACT.Copy).then_inc(s_ta, 1)

                    def step(g, j, after, after2):
                        n = SEQ * g + j
                        if after:
                            keep_k(n + 1, (j + 1) % 2)
                        if after2:
                            ctx_high(2 * g + (j + 2) // 2, n + 2, j % 2)
                        keep_p(n)
                        if after:
                            exps(n + 1, (j + 1) % 2)

                    def tile_out(g):
                        eng.wait_ge(s_o, SEQ * g + (SEQ + 1))
                        eng.wait_ge(s_y, g + 1)
                        act.activation(oh, ot, ACT.Copy).then_inc(s_oh, 1)

                    eng.sem_inc(s_ta, LEAD)
                    ctx_high(0, 0, 0)
                    keep_k(0, 0)
                    ctx_high(0, 1, 1)
                    exps(0, 0)
                    with act.Fori(0, NT - 1) as g:
                        for j in range(SEQ):
                            step(g, j, True, True)
                        tile_out(g)
                    for j in range(SEQ):
                        step(NT - 1, j, j < SEQ - 1, j < SEQ - 2)
                    tile_out(NT - 1)

                @block.vector
                def _(eng):
                    links = Links(eng, s_links)

                    def keep_v(m, u):
                        for k in range(2):
                            eng.wait_ge(s_vp, 2 * m + (k + 1 + LEAD))
                            if k == 0:
                                eng.wait_ge(s_pv, m + 1)
                            dve.tensor_tensor(v[u][:, k, :], banks[:, k, :], bvb, ALU.add).then_inc(s_v, 1)

                    def tops(m, u):
                        eng.wait_ge(s_sc, m + 1 + LEAD)
                        links.link(dve.reduce_max(mx[:, u, :], banks[:, SC:SC + DC, 0:S], AX_X))
                        dve.tensor_scalar(bias[:, u, :], mx[:, u, :], -scale, None, ALU.mult).then_inc(s_bias, 1)

                    def sums(m, u):
                        eng.wait_ge(s_ex, m + 1)
                        dve.reciprocal(rinv[:, u, :], rs[:, u, :]).then_inc(s_rinv, 1)

                    def step(g, j, after):
                        n = SEQ * g + j
                        if after:
                            keep_v(n + 1, (j + 1) % 2)
                        eng.wait_ge(s_t, 3 * n + 2)
                        dve.tensor_copy(pt[:, 1, :], banks[:, T1, :]).then_inc(s_td, 1)
                        if after:
                            tops(n + 1, (j + 1) % 2)
                            sums(n + 1, (j + 1) % 2)
                        eng.wait_ge(s_pv, n + 1 + LEAD)
                        o = chunks(banks[:, T1, :])
                        for h in range(4):
                            rows = slice(XD * h, XD * h + XD)
                            ins = dve.tensor_copy(ot[rows, :, NQ * j:NQ * j + NQ], o[rows, :, rows])
                        ins.then_inc(s_o, 1)

                    def tile_out(g):
                        eng.wait_ge(s_oh, g + 1)
                        dve.tensor_tensor(ol, ot, oh.bitcast(F32), ALU.subtract).then_inc(s_ol, 1)
                        links.link(dve.tensor_tensor(x[:, g, :], x[:, g, :], bob, ALU.add))
                        eng.wait_ge(s_y, g + 2)
                        dve.tensor_tensor(x[:, g, :], banks[:, T0, :], x[:, g, :], ALU.add).then_inc(s_x, 1)

                    eng.sem_inc(s_x, 1)
                    eng.sem_inc(s_o, 1)
                    keep_v(0, 0)
                    tops(0, 0)
                    sums(0, 0)
                    with dve.Fori(0, NT - 1) as g:
                        links.enter(g, SEQ + 1)
                        for j in range(SEQ):
                            step(g, j, True)
                        tile_out(g)
                        links.leave(NT - 1)
                    for j in range(SEQ):
                        step(NT - 1, j, j < SEQ - 1)
                    tile_out(NT - 1)

                @block.tensor
                def _(eng):
                    eng.sem_inc(s_vp, 2)
                    eng.sem_inc(s_y, 1)
                    eng.sem_inc(s_sc, LEAD)
                    eng.sem_inc(s_pv, LEAD)

                    def keys_values(m, u):
                        eng.wait_ge(s_cl, m + 1 + LEAD)
                        if not (isinstance(m, int) and m == 0):
                            eng.wait_ge(s_v, 2 * m)
                            eng.wait_ge(s_ta, 2 * m)
                        for e in range(DC):
                            if e >= 2:
                                eng.wait_ge(s_k, DC * m + (e - 1))
                            cols = slice(e * P, (e + 1) * P)
                            for c in range(DC):
                                ins = mm3(banks[:, e % 2, 0:SE], wk[0][:, c, cols], wk[1][:, c, cols], cx[u][0][:, c, :],
                                          cx[u][1][:, c, :], c == 0, c == DC - 1)
                            ins.then_inc(s_kp, 1)
                        for k in range(2):
                            eng.wait_ge(s_k, DC * m + (k + 3))
                            for c in range(DC):
                                rows = slice(k * P, (k + 1) * P)
                                ins = mm3(banks[:, k, :], cx[u][0][:, c, rows], cx[u][1][:, c, rows], wv[0][:, c, :],
                                          wv[1][:, c, :], c == 0, c == DC - 1)
                            ins.then_inc(s_vp, 1)

                    def scores(m, u):
                        eng.wait_ge(s_qb, m + 1)
                        eng.wait_ge(s_k, DC * m + DC)
                        if not (isinstance(m, int) and m == 0):
                            eng.wait_ge(s_ex, m)
                        for c in range(DC):
                            ins = pe.matmul(banks[:, SC + c, 0:S], qblk[u][:, c, :], kt[u][:, c, 0:S], start=True, stop=True)
                        ins.then_inc(s_sc, 1)

                    def turn(g, j, after):
                        n, u = SEQ * g + j, j % 2
                        eng.wait_ge(s_pn, n + 1)
                        eng.wait_ge(s_ta, 2 * n + 1)
                        eng.wait_ge(s_x, g + 1)
                        eng.wait_ge(s_o, n + 1)
                        for k in range(3):
                            rows = P if k < 2 else 1
                            if k == 2 and after:
                                eng.wait_ge(s_v, 2 * n + 3)
                            for c in range(DC):
                                ins = pe.transpose(banks[0:rows, (T0, T1, 0)[k], c * P:(c + 1) * P],
                                                   pr[u][:, c, k * P:k * P + rows], ident[:])
                            ins.then_inc(s_t, 1)

                    def p_v(g, j):
                        n, u = SEQ * g + j, j % 2
                        eng.wait_ge(s_ta, 2 * n + 2 + LEAD)
                        eng.wait_ge(s_td, n + 1)
                        eng.wait_ge(s_v, 2 * n + 2)
                        eng.wait_ge(s_vld[u], 32 * g + 16 * (j // 2 + 1))
                        for c in range(DC):
                            cols = slice(c * P, (c + 1) * P)
                            for k in range(2):
                                pe.matmul(banks[:, T1, cols], v[u][:, k, cols], pt[:, k, cols], start=k == 0, stop=False)
                            ins = pe.matmul(banks[:, T1, cols], vlast[u][0:1, cols], pt[0:1, 2, cols], start=False,
                                            stop=True)
                        ins.then_inc(s_pv, 1)

                    def step(g, j, after):
                        n = SEQ * g + j
                        if after:
                            keys_values(n + 1, (j + 1) % 2)
                        turn(g, j, after)
                        if after:
                            scores(n + 1, (j + 1) % 2)
                        p_v(g, j)

                    def tile_out(g):
                        eng.wait_ge(s_ol, g + 1)
                        for c in range(DC):
                            ins = mm3(banks[:, T0, :], oh[:, c, :], ol[:, c, :], wo[0][:, c, :], wo[1][:, c, :],
                                      c == 0, c == DC - 1)
                        ins.then_inc(s_y, 1)

                    keys_values(0, 0)
                    scores(0, 0)
                    with pe.Fori(0, NT - 1) as g:
                        for j in range(SEQ):
                            step(g, j, True)
                        tile_out(g)
                    for j in range(SEQ):
                        step(NT - 1, j, j < SEQ - 1)
                    tile_out(NT - 1)

        for stage in d.get("stages", "ABCDEF"):
            if stage == "A":
                cross_one_head()
            elif stage == "B":
                self_attention("sa", False)
                free_semaphores()
            elif stage == "C":
                layer_norm("nc", rows=normed_dram)
                plan = Plan(0)
                routing("ra", plan)
                experts("ea", plan, d["L0_units"])
                free_semaphores()
            elif stage == "D":
                cross_heads()
            elif stage == "E":
                self_attention("sb", True)
                free_semaphores()
            else:
                layer_norm("nf", rows=normed_dram)
                plan = Plan(1)
                routing("rb", plan)
                experts("eb", plan, d["L1_units"])
        s_out = sem("x_stored")
        with nc.Block() as block:
            @block.sync
            def _(eng):
                eng.dma_start(out.rearrange("(t p) d -> p t d", p=P), x[:]).then_inc(s_out, 16)
                eng.wait_ge(s_out, 16)


def layouts(i):
    def t(w):
        return np.swapaxes(w, -1, -2)

    def units(up1, up2, down):
        def up(w):
            return w.reshape(-1, P, DC, P).transpose(0, 3, 2, 1).reshape(-1, P, D)
        dn = t(down).reshape(-1, P, D)
        return np.ascontiguousarray(np.stack([up(up1), up(up2), dn], axis=2))

    ctx = i["ctx_1024"]
    a = {
        "x": i["x"].reshape(T, D),
        "ctx": ctx,
        "ctxT": t(ctx).reshape(B, DC, P, S).transpose(0, 2, 1, 3),
        "ctxLastT": ctx[:, S - 1, :].T.reshape(DC, P, B).transpose(1, 0, 2),
        "L0_xattn_WkT": t(i["L0_xattn_Wk"]),
        "L0_attn_w_qkvT": t(i["L0_attn_w_qkv"]),
        "L0_attn_w_outT": t(i["L0_attn_w_out"]),
        "L0_ffn_gateT": t(i["L0_ffn_gate_w"]),
        "L0_units": units(np.concatenate([i["L0_ffn_w1"], i["L0_ffn_ws1"][None]]),
                          np.concatenate([i["L0_ffn_w3"], i["L0_ffn_ws3"][None]]),
                          np.concatenate([i["L0_ffn_w2"], i["L0_ffn_ws2"][None]])),
        "L1_attn_w64": np.concatenate([i["L1_attn_wq"], i["L1_attn_wk"], i["L1_attn_wv"], i["L1_attn_wv"]], axis=1),
        "L1_attn_fcqk": np.concatenate([i["L1_attn_fcq_w"], i["L1_attn_fck_w"]]),
        "L1_attn_fcvv": np.concatenate([i["L1_attn_fcv_w"], i["L1_attn_fcv_w"]]),
        "L1_ffn_gateT": t(i["L1_ffn_gate_w"]),
        "L1_units": units(i["L1_ffn_w12"][:, :I1], i["L1_ffn_w12"][:, I1:], i["L1_ffn_w3"]),
    }
    for name in ("L0_xattn_Wq", "L0_xattn_bq", "L0_xattn_bk", "L0_xattn_Wv", "L0_xattn_bv", "L0_attn_ln_gamma",
                 "L0_attn_ln_beta", "L0_attn_b_out", "L0_ffn_gate_bias", "L1_xattn_W_Q", "L1_xattn_b_Q",
                 "L1_xattn_W_K", "L1_xattn_b_K", "L1_xattn_W_V", "L1_xattn_b_V", "L1_xattn_W_O", "L1_xattn_b_O",
                 "L1_attn_fcq_b", "L1_attn_fck_b", "L1_attn_fcv_b", "L1_attn_fco_w", "L1_attn_fco_b"):
        a[name] = i[name]
    for name in ("L0_xattn_bq", "L0_xattn_bk", "L1_xattn_b_Q", "L1_xattn_b_K", "L1_attn_fcq_b", "L1_attn_fck_b"):
        a[name] = i[name].reshape(-1, P).T
    return {k: np.ascontiguousarray(v) for k, v in a.items()}


def kernel(**inputs):
    from concourse import bacc
    from concourse.bass_utils import run_bass_kernel_spmd

    arrays = layouts({k: np.asarray(v) for k, v in inputs.items()})
    nc = bacc.Bacc("TRN2", target_bir_lowering=False, num_devices=1)
    d = {k: nc.dram_tensor(f"in_{k}", v.shape, mybir.dt.from_np(v.dtype), kind="ExternalInput").ap()
         for k, v in arrays.items()}
    out = nc.dram_tensor("out_x", (T, D), F32, kind="ExternalOutput").ap()
    build(nc, d, out)
    r = run_bass_kernel_spmd(nc, [{f"in_{k}": v for k, v in arrays.items()}], core_ids=[0])
    return r.results[0]["out_x"].reshape(B, NQ, D)
```

```python
from contextlib import ExitStack

import numpy as np
import concourse.bass as bass
from concourse import mybir

F32 = mybir.dt.float32
F32R = mybir.dt.float32r
U32 = mybir.dt.uint32
ALU = mybir.AluOpType
ACT = mybir.ActivationFunctionType
AX_X = mybir.AxisListType.X

P = 128
B, NQ, D = 32, 32, 512
S = 257
SE = 258
T = B * NQ
NT = T // P
SEQ = P // NQ
DC = D // P
HALF = 512
NHALF = T // HALF
DH = 64
HH = 8
E0, I0, K0 = 16, 256, 4
G0, GK0 = 4, 2
E1, I1, K1 = 8, 1024, 2
XH, XD = 16, 32
CAP = 2 * P
WEIGHT_BUFFERS = 4
LEAD = 2
FAR = 1e30
MASKED = -3.4028234663852886e38
LN_EPS = 1e-5
F_SIZE, R_SIZE = 74 * 256, 69 * 256
N_SIZE = 2304


class Links:

    def __init__(self, engine, sem):
        self.engine, self.sem, self.done, self.turn, self.k, self.per = engine, sem, 0, 0, 0, 0

    def enter(self, turn, per):
        self.turn, self.per, self.k = turn * per, per, 0

    def leave(self, turns):
        assert self.k == self.per, (self.k, self.per)
        self.done, self.turn, self.k, self.per = self.done + turns * self.per, 0, 0, 0

    def link(self, instruction):
        instruction.then_inc(self.sem, 1)
        self.k += 1
        self.engine.wait_ge(self.sem, self.turn + (self.done + self.k))
        if not self.per:
            self.done, self.k = self.done + 1, 0


class Area:

    def __init__(self, tensor, size, at=0):
        self.tensor, self.size, self.at = tensor, size, at

    def take(self, *shape):
        n = int(np.prod(shape))
        at, self.at = self.at, self.at + n + n % 2
        assert self.at <= self.size, ("arena", self.at, self.size)
        ap = self.tensor[:, at:at + n]
        if len(shape) > 1:
            names = "abcd"[:len(shape)]
            ap = ap.rearrange(f"p ({' '.join(names)}) -> p {' '.join(names)}", **dict(zip(names, shape)))
        return ap


def build(nc, d, out):
    with ExitStack() as ctx:
        def sb(name, shape, dt=F32):
            return ctx.enter_context(nc.sbuf_tensor(name, shape, dt))

        layer_sems = []

        def sem(name):
            layer_sems.append(nc.alloc_semaphore(name=name))
            return layer_sems[-1]

        def gather_sem(name):
            return nc.alloc_semaphore(name=name)

        def free_semaphores():
            with nc.Block() as block:
                @block.sync
                def _(eng):
                    for s in layer_sems:
                        eng.sem_clear(s)
            for s in layer_sems:
                nc.release_semaphore(s)
            layer_sems.clear()

        pe, act, dve, pool = nc.tensor, nc.scalar, nc.vector, nc.gpsimd
        x = sb("x", [P, NT, D])
        xh = sb("xh", [P, DC, T], F32R)
        xl = sb("xl", [P, DC, T], F32R)
        ident = sb("ident", [P, P])
        epst = sb("epst", [P, 1])
        stats = sb("stats", [P, NT, 6])
        moments = sb("moments", [P, NT, 2])
        rstd = sb("rstd", [P, NT])
        fa = sb("fa", [P, F_SIZE])
        ra = sb("ra", [P, R_SIZE], F32R)
        na = sb("na", [P, N_SIZE])
        banks = ctx.enter_context(nc.psum_tensor("banks", [P, 8, 512], F32))
        ones, earlier = sb("ones", [P, P], F32R), sb("earlier", [P, P], F32R)
        normed_dram = nc.dram_tensor("normed_scratch", [T, D], F32, kind="Internal").ap()
        vlast_dram = nc.dram_tensor("vlast_scratch", [B, DC, D], F32, kind="Internal").ap()

        def mm3(psum, lh, ll, rh, rl, first=True, last=True):
            pe.matmul(psum, lh, rh, start=first, stop=False)
            pe.matmul(psum, lh, rl, start=False, stop=False)
            return pe.matmul(psum, ll, rh, start=False, stop=last)

        def chunks(ap):
            return ap.rearrange("p (c t) -> p c t", c=DC)

        s_x, s_id = sem("x_loaded"), sem("ident_made")
        with nc.Block() as block:
            @block.sync
            def _(eng):
                eng.dma_start(x[:], d["x"].rearrange("(t p) d -> p t d", p=P)).then_inc(s_x, 16)
                eng.wait_ge(s_x, 16)

            @block.gpsimd
            def _(eng):
                pool.memset(ident[:], 0.0).then_inc(s_id, 1)
                pool.memset(epst[:], LN_EPS)
                plain = Area(fa, F_SIZE).take(P)
                pool.memset(plain, 1.0).then_inc(s_id, 1)
                eng.wait_ge(s_id, 2)
                pool.affine_select(out=ident[:], in_=ident[:], compare_op=ALU.not_equal, fill=1.0,
                                   base=0, pattern=[[-1, P]], channel_multiplier=1)
                pool.tensor_copy(ones[:], plain)
                pool.affine_select(out=earlier[:], in_=plain, compare_op=ALU.is_gt, fill=0.0,
                                   base=0, pattern=[[1, P]], channel_multiplier=-1)

        made = set()

        def row_statistics(eng, sem_added, count, passed, n):
            eng.wait_ge(sem_added, count)
            eng.sem_inc(passed, 1)
            dve.bn_stats(stats[:, n, :], x[:, n, :])

        def layer_norm(tag, affine=None, ahead=None, rows=None):
            f = Area(na, N_SIZE)
            L = 2 if affine else 4
            assert NT % L == 0
            xn = [f.take(D) for _ in range(L)]
            gain, shift = (f.take(D), f.take(D)) if affine else (None, None)
            root, var2, rstd2 = f.take(NT), f.take(NT), f.take(NT)
            s_gain, s_stats, s_mom, s_root = (sem(f"{tag}_{n}") for n in ("gain", "statistics", "moments", "root"))
            s_xn, s_turned, s_hi, s_lo, s_links = (sem(f"{tag}_{n}") for n in ("normed", "turned", "high", "low", "links"))
            s_rows = [sem(f"{tag}_rows_stored{u}") for u in range(L)] if rows is not None else None

            with nc.Block() as block:
                @block.sync
                def _(eng):
                    if ahead and rows is not None:
                        programs, loads, splits = ahead
                        programs[0](eng, loads)
                    if rows is not None:
                        for u in range(L):
                            eng.sem_inc(s_rows[u], 16)
                        with eng.Fori(0, NT // L) as i:
                            for u in range(L):
                                eng.wait_ge(s_xn, L * i + u + 1)
                                eng.dma_start(rows.rearrange("(t p) d -> t p d", p=P)[L * i + u],
                                              xn[u]).then_inc(s_rows[u], 16)
                        for u in range(L):
                            eng.wait_ge(s_rows[u], 16 + 16 * (NT // L))
                    if affine:
                        eng.dma_start(gain, affine[0].partition_broadcast(P)).then_inc(s_gain, 16)
                        eng.dma_start(shift, affine[1].partition_broadcast(P)).then_inc(s_gain, 16)
                    if ahead and rows is None:
                        programs, loads, splits = ahead
                        programs[0](eng, loads)

                @block.gpsimd
                def _(eng):
                    if ahead:
                        programs, loads, splits = ahead
                        programs[2](eng, splits)

                @block.vector
                def _(eng):
                    links = Links(eng, s_links)

                    if "statistics" not in made:
                        with dve.Fori(0, NT) as t:
                            dve.bn_stats(stats[:, t, :], x[:, t, :]).then_inc(s_stats, 1)
                        eng.wait_ge(s_stats, NT)
                    for t in range(NT):
                        dve.bn_aggr(moments[:, t, :], stats[:, t, :]).then_inc(s_mom, 1)
                    eng.wait_ge(s_root, 1)
                    links.link(dve.reciprocal(rstd[:], root))
                    if affine:
                        links.link(dve.tensor_tensor(var2, moments[:, :, 1], rstd[:], ALU.mult))
                        dve.tensor_tensor(var2, var2, rstd[:], ALU.mult).then_inc(s_mom, 1)
                        eng.wait_ge(s_root, 2)
                        links.link(dve.reciprocal(rstd2, root))
                        links.link(dve.tensor_tensor(rstd[:], rstd[:], rstd2, ALU.mult))
                        eng.wait_ge(s_gain, 32)

                    def normalise(n, u, k):
                        eng.wait_ge(s_turned, n + 1)
                        if rows is not None:
                            eng.wait_ge(s_rows[u], 16 * k + 16)
                        mean, r = moments[:, n, 0:1], rstd[:, bass.ds(n, 1)]
                        if affine:
                            links.link(dve.scalar_tensor_tensor(xn[u], x[:, n, :], mean, gain, ALU.subtract, ALU.mult))
                            ins = dve.scalar_tensor_tensor(xn[u], xn[u], r, shift, ALU.mult, ALU.add)
                        else:
                            ins = dve.tensor_scalar(xn[u], x[:, n, :], mean, r, ALU.subtract, ALU.mult)
                        ins.then_inc(s_xn, 1)

                    def low_part(n, u):
                        eng.wait_ge(s_hi, n + 1)
                        dve.tensor_tensor(xl[:, :, bass.ts(n, P)], chunks(banks[:, u, :]),
                                          xh[:, :, bass.ts(n, P)].bitcast(F32), ALU.subtract).then_inc(s_lo, 1)

                    eng.sem_inc(s_lo, L)
                    links.enter(0, L if affine else 0)
                    for u in range(L):
                        normalise(u, u, 0)
                    links.leave(1)
                    with dve.Fori(0, NT // L - 1) as i:
                        links.enter(i, L if affine else 0)
                        for u in range(L):
                            normalise(L * i + u + L, u, i + 1)
                            low_part(L * i + u, u)
                        links.leave(NT // L - 1)
                    for u in range(L):
                        low_part(NT - L + u, u)

                @block.scalar
                def _(eng):
                    eng.wait_ge(s_mom, NT)
                    act.activation(root, moments[:, :, 1], ACT.Sqrt, bias=epst[:]).then_inc(s_root, 1)
                    if affine:
                        eng.wait_ge(s_mom, NT + 1)
                        act.activation(root, var2, ACT.Sqrt, bias=epst[:]).then_inc(s_root, 1)

                    def high_part(n, u):
                        eng.wait_ge(s_turned, n + 1 + L)
                        act.activation(xh[:, :, bass.ts(n, P)], chunks(banks[:, u, :]), ACT.Copy).then_inc(s_hi, 1)

                    with act.Fori(0, NT // (2 * L)) as i:
                        for u in range(L):
                            high_part(L * i + u, u)
                    if ahead:
                        programs, loads, splits = ahead
                        programs[1](eng, splits[:1])
                    with act.Fori(0, NT // (2 * L)) as i:
                        for u in range(L):
                            high_part(L * i + u + NT // 2, u)
                    if ahead:
                        programs[1](eng, splits[1:])

                @block.tensor
                def _(eng):
                    eng.sem_inc(s_turned, L)
                    with pe.Fori(0, NT // L) as i:
                        for u in range(L):
                            n = L * i + u
                            eng.wait_ge(s_xn, n + 1)
                            eng.wait_ge(s_lo, n + 1)
                            for c in range(DC):
                                ins = pe.transpose(banks[:, u, c * P:(c + 1) * P],
                                                   xn[u][:, c * P:(c + 1) * P], ident[:])
                            ins.then_inc(s_turned, 1)

        def split_programs(tag, weights, staging):
            s_ld = [sem(f"{tag}_weight{k}") for k in range(len(weights))]
            s_hi = [sem(f"{tag}_high{k}") for k in range(len(weights))]
            s_w = [sem(f"{tag}_split{k}") for k in range(len(weights))]
            slots = len(staging)

            def load(eng, which=range(len(weights))):
                for k in which:
                    if k >= slots:
                        eng.wait_ge(s_w[k - slots], 1)
                    eng.dma_start(staging[k % slots], weights[k][2]).then_inc(s_ld[k], 16)

            def high(eng, which=range(len(weights))):
                for k in which:
                    eng.wait_ge(s_ld[k], 16)
                    act.activation(weights[k][0], staging[k % slots], ACT.Copy).then_inc(s_hi[k], 1)

            def low(eng, which=range(len(weights))):
                for k in which:
                    hi, lo, _ = weights[k]
                    eng.wait_ge(s_hi[k], 1)
                    pool.tensor_tensor(lo, staging[k % slots], hi.bitcast(F32), ALU.subtract).then_inc(s_w[k], 1)
            return load, high, low, s_w

        def columns(w):
            return w.rearrange("(c p) n -> p c n", p=P)

        def cross_one_head():
            scale = float(D) ** -0.5
            f, r = Area(fa, F_SIZE), Area(ra, R_SIZE)
            qp, bv, bk, bq, shift = f.take(DC, T), f.take(D), f.take(DC), f.take(DC), f.take(NT)
            f2 = f.at
            staging = [f.take(DC, D) for _ in range(3)]
            ct = [f.take(DC, S) for _ in range(SEQ)]
            f3 = f.at
            wv = r.take(DC, D), r.take(DC, D)
            bk_parts = r.take(DC, 2)
            r2 = r.at
            wq, wk = (r.take(DC, D), r.take(DC, D)), (r.take(DC, D), r.take(DC, D))
            q = [r.take(DC, HALF) for _ in range(2)]
            load, high, low, s_w = split_programs("xa", [
                (*wq, columns(d["L0_xattn_Wq"])), (*wk, columns(d["L0_xattn_WkT"])),
                (*wv, columns(d["L0_xattn_Wv"]))], staging)
            s_ctxT = [sem(f"xa_ctxT{j}") for j in range(SEQ)]
            s_sc, s_bk = sem("xa_scores"), sem("xa_bk_split")

            def load_turned(eng, n):
                for j in range(SEQ):
                    if not (isinstance(n, int) and n == 0):
                        eng.wait_ge(s_sc, SEQ * n + (SEQ + 1 + j))
                    eng.dma_start(ct[j], d["ctxT"][SEQ * n + j]).then_inc(s_ctxT[j], 16)

            layer_norm("na", ahead=((load, high, low), (0, 1, 2), (0,)))
            s_b, s_mm, s_hi, s_out = sem("xa_biases"), sem("xa_product"), sem("xa_high"), sem("xa_taken")
            jobs = [(h, kind, c) for h in range(NHALF) for kind, c in
                    [("q", c) for c in range(DC)] + [("k", c) for c in range(DC)] + [("shift", 0)]]
            NB = 4

            with nc.Block() as block:
                @block.sync
                def _(eng):
                    eng.dma_start(bq, d["L0_xattn_bq"]).then_inc(s_b, 16)
                    eng.dma_start(bk, d["L0_xattn_bk"]).then_inc(s_b, 16)
                    eng.dma_start(bv, d["L0_xattn_bv"].partition_broadcast(P)).then_inc(s_b, 16)
                    load_turned(eng, 0)

                @block.gpsimd
                def _(eng):
                    low(eng, (1, 2))

                @block.scalar
                def _(eng):
                    high(eng, (1, 2))
                    eng.wait_ge(s_b, 48)
                    for j, (h, kind, c) in enumerate(jobs):
                        if kind != "q":
                            continue
                        eng.wait_ge(s_mm, j + 1)
                        if h:
                            eng.wait_ge(s_mm, len(jobs) // 2)
                        act.activation(q[0][:, c, :], banks[:, j % NB, :], ACT.Identity,
                                       bias=bq[:, c:c + 1]).then_inc(s_hi, 1)

                @block.vector
                def _(eng):
                    eng.wait_ge(s_b, 48)
                    eng.wait_ge(s_b, 48)
                    dve.tensor_copy(bk_parts[:, :, 0], bk).then_inc(s_bk, 1)
                    eng.wait_ge(s_bk, 1)
                    dve.tensor_tensor(bk_parts[:, :, 1], bk, bk_parts[:, :, 0].bitcast(F32),
                                      ALU.subtract).then_inc(s_bk, 1)
                    highs = 0
                    for j, (h, kind, c) in enumerate(jobs):
                        bank = banks[:, j % NB, :]
                        eng.wait_ge(s_mm, j + 1)
                        if kind == "q":
                            highs += 1
                            eng.wait_ge(s_hi, highs)
                            ins = dve.scalar_tensor_tensor(q[1][:, c, :], bank, bq[:, c:c + 1],
                                                           q[0][:, c, :].bitcast(F32), ALU.add, ALU.subtract)
                        elif kind == "k":
                            ins = dve.tensor_copy(qp[:, c, h * HALF:(h + 1) * HALF], bank)
                        else:
                            ins = dve.reduce_sum(shift[:, 4 * h:4 * h + 4],
                                                 bank[:, 0:8].rearrange("p (t k) -> p t k", k=2), AX_X)
                        ins.then_inc(s_out, 1)

                @block.tensor
                def _(eng):
                    for j, (h, kind, c) in enumerate(jobs):
                        bank = banks[:, j % NB, :]
                        if j >= NB:
                            eng.wait_ge(s_out, j - NB + 1)
                        cols = slice(c * P, (c + 1) * P)
                        tok = slice(h * HALF, (h + 1) * HALF)
                        if kind == "q":
                            eng.wait_ge(s_w[0], 1)
                            for k in range(DC):
                                ins = mm3(bank, wq[0][:, k, cols], wq[1][:, k, cols], xh[:, k, tok],
                                          xl[:, k, tok], k == 0, k == DC - 1)
                        elif kind == "k":
                            eng.wait_ge(s_w[1], 1)
                            eng.wait_ge(s_out, j - c)
                            for k in range(DC):
                                ins = mm3(bank, wk[0][:, k, cols], wk[1][:, k, cols], q[0][:, k, :],
                                          q[1][:, k, :], k == 0, k == DC - 1)
                        else:
                            eng.wait_ge(s_bk, 2)
                            for t in range(4):
                                for k in range(DC):
                                    for part in range(2):
                                        ins = pe.matmul(bank[:, 2 * t:2 * t + 2], q[part][:, k, t * P:(t + 1) * P],
                                                        bk_parts[:, k, :], start=(k + part == 0),
                                                        stop=(k == DC - 1 and part == 1))
                        ins.then_inc(s_mm, 1)

            f = Area(fa, F_SIZE, f2)
            cn = [f.take(2, D) for _ in range(SEQ)]
            cl = f.take(D)
            f = Area(fa, F_SIZE, f3)
            r = Area(ra, R_SIZE, r2)
            qg = [f.take(DC, P) for _ in range(2)]
            pr = [f.take(S) for _ in range(2)]
            pt = [f.take(3, P) for _ in range(2)]
            own, last = f.take(SEQ), [f.take(SEQ) for _ in range(2)]
            a = [f.take(D) for _ in range(2)]
            mx, top, bias, rs, rinv = (f.take(2) for _ in range(5))
            at = [(r.take(DC, P), r.take(DC, P)) for _ in range(2)]
            s_ctx = [sem(f"xa_ctx{j}") for j in range(SEQ)]
            s_passed, s_cl, s_own, s_last = (sem(f"xa_{n}") for n in ("passed", "last_rows", "own", "p_last"))
            (s_qg, s_bias, s_exp, s_tp, s_pt, s_pv, s_a, s_at, s_ah, s_al, s_o, s_x, s_links) = (
                sem(f"xa_{n}") for n in ("q_tile", "bias", "exp", "p_turned", "p_kept", "pv", "a_kept",
                                         "a_turned", "a_high", "a_low", "out", "x_added", "links"))

            with nc.Block() as block:
                @block.sync
                def _(eng):
                    def load_rows(n):
                        eng.wait_ge(s_pv, SEQ * n + SEQ)
                        eng.dma_start(cl[0:SEQ, :], d["ctxLast"][bass.ds(SEQ * n, SEQ), :]).then_inc(s_cl, 16)
                        for j in range(SEQ):
                            eng.wait_ge(s_pv, SEQ * n + j + 1)
                            eng.dma_start(cn[j], d["ctx"][SEQ * n + j, 0:2 * P, :]
                                          .rearrange("(k p) e -> p k e", p=P)).then_inc(s_ctx[j], 16)

                    with eng.Fori(0, NT - 1) as n:
                        load_turned(eng, n + 1)
                        load_rows(n)
                    load_rows(NT - 1)

                @block.gpsimd
                def _(eng):
                    pool.memset(own, 1.0).then_inc(s_own, 1)
                    eng.wait_ge(s_own, 1)
                    pool.affine_select(out=own, in_=own, compare_op=ALU.is_ge, fill=0.0, base=0,
                                       pattern=[[-NQ, SEQ]], channel_multiplier=1).then_inc(s_own, 1)
                    eng.wait_ge(s_own, 2)
                    pool.affine_select(out=own, in_=own, compare_op=ALU.is_gt, fill=0.0, base=NQ,
                                       pattern=[[NQ, SEQ]], channel_multiplier=-1).then_inc(s_own, 1)

                @block.scalar
                def _(eng):
                    def q_tile(n, u):
                        eng.wait_ge(s_sc, SEQ * n + SEQ)
                        act.activation(qg[u], qp[:, :, bass.ts(n, P)], ACT.Copy).then_inc(s_qg, 1)

                    def exps(n, u):
                        eng.wait_ge(s_bias, n + 1)
                        act.activation(pr[u], banks[:, u, 0:S], ACT.Exp, bias=bias[:, u:u + 1], scale=scale,
                                       accum_out=rs[:, u:u + 1]).then_inc(s_exp, 1)

                    def a_high(n, u):
                        eng.wait_ge(s_at, n + 1)
                        act.activation(at[u][0], chunks(banks[:, 6, :]), ACT.Copy).then_inc(s_ah, 1)

                    eng.sem_inc(s_exp, LEAD)
                    q_tile(0, 0)
                    q_tile(1, 1)
                    exps(0, 0)
                    exps(1, 1)
                    with act.Fori(0, NT // 2 - 1) as i:
                        for u in range(2):
                            q_tile(2 * i + u + 2, u)
                            exps(2 * i + u + 2, u)
                            a_high(2 * i + u, u)
                    a_high(NT - 2, 0)
                    a_high(NT - 1, 1)

                @block.vector
                def _(eng):
                    links = Links(eng, s_links)
                    eng.sem_inc(s_pt, LEAD)
                    eng.sem_inc(s_a, LEAD)
                    eng.sem_inc(s_al, 1)
                    eng.sem_inc(s_x, 1)

                    def softmax_top(n, u):
                        eng.wait_ge(s_sc, SEQ * n + 3 * SEQ)
                        links.link(dve.reduce_max(mx[:, u:u + 1], banks[:, u, 0:S], AX_X))
                        sh = shift[:, bass.ds(n, 1)]
                        links.link(dve.tensor_tensor(top[:, u:u + 1], mx[:, u:u + 1], sh, ALU.add))
                        dve.tensor_scalar(bias[:, u:u + 1], top[:, u:u + 1], sh, -scale, ALU.subtract,
                                          ALU.mult).then_inc(s_bias, 1)

                    def last_p(n, u):
                        eng.wait_ge(s_exp, n + 1 + LEAD)
                        dve.tensor_scalar(last[u], own, pr[u][:, S - 1:S], None, ALU.mult).then_inc(s_last, 1)

                    def keep_p(n, u):
                        eng.wait_ge(s_tp, n + 1)
                        dve.reciprocal(rinv[:, u:u + 1], rs[:, u:u + 1])
                        dve.tensor_copy(pt[u][:, 0:2, :], banks[:, 2 + u, 0:2 * P].rearrange("p (k t) -> p k t", k=2))
                        dve.tensor_copy(pt[u][0:SEQ, 2, :], banks[0:SEQ, 2 + u, 2 * P:3 * P]).then_inc(s_pt, 1)

                    def a_low(n, u):
                        eng.wait_ge(s_ah, n + 1)
                        dve.tensor_tensor(at[u][1], chunks(banks[:, 6, :]), at[u][0].bitcast(F32),
                                          ALU.subtract).then_inc(s_al, 1)

                    def keep_a(n, u):
                        eng.wait_ge(s_pv, SEQ * n + 2 * SEQ)
                        dve.tensor_scalar(a[u], banks[:, 4 + u, :], rinv[:, u:u + 1], None, ALU.mult).then_inc(s_a, 1)

                    def add(n, u):
                        eng.wait_ge(s_o, n + 1)
                        links.link(dve.tensor_tensor(a[u], banks[:, 7, :], bv, ALU.add))
                        dve.tensor_tensor(x[:, n, :], x[:, n, :], a[u], ALU.add).then_inc(s_x, 1)
                        row_statistics(eng, s_x, n + 2, s_passed, n)

                    links.enter(0, 4)
                    softmax_top(0, 0)
                    softmax_top(1, 1)
                    links.leave(1)
                    eng.wait_ge(s_own, 3)
                    last_p(0, 0)
                    last_p(1, 1)
                    keep_p(0, 0)
                    keep_a(0, 0)
                    with dve.Fori(0, NT // 2 - 1) as i:
                        links.enter(i, 6)
                        for u in range(2):
                            n = 2 * i + u + 1
                            softmax_top(n + 1, u)
                            keep_p(n, 1 - u)
                            last_p(n + 1, u)
                            a_low(n - 1, u)
                            keep_a(n, 1 - u)
                            add(n - 1, u)
                        links.leave(NT // 2 - 1)
                    keep_p(NT - 1, 1)
                    a_low(NT - 2, 0)
                    keep_a(NT - 1, 1)
                    add(NT - 2, 0)
                    a_low(NT - 1, 1)
                    add(NT - 1, 1)

                @block.tensor
                def _(eng):
                    eng.sem_inc(s_sc, 2 * SEQ)
                    eng.sem_inc(s_pv, SEQ)

                    def scores(n, u):
                        eng.wait_ge(s_qg, n + 1)
                        eng.wait_ge(s_exp, n + 1)
                        for j in range(SEQ):
                            eng.wait_ge(s_ctxT[j], 16 * n + 16)
                            for c in range(DC):
                                ins = pe.matmul(banks[NQ * j:NQ * j + NQ, u, 0:S], qg[u][:, c, NQ * j:NQ * j + NQ],
                                                ct[j][:, c, :], start=c == 0, stop=c == DC - 1)
                            ins.then_inc(s_sc, 1)

                    def turn_p(n, u):
                        eng.wait_ge(s_last, n + 1)
                        eng.wait_ge(s_pt, n + 1)
                        for k in range(2):
                            pe.transpose(banks[:, 2 + u, k * P:(k + 1) * P], pr[u][:, k * P:(k + 1) * P], ident[:])
                        pe.transpose(banks[0:SEQ, 2 + u, 2 * P:3 * P], last[u], ident[:]).then_inc(s_tp, 1)

                    def p_ctx(n, u):
                        eng.wait_ge(s_pt, n + 1 + LEAD)
                        eng.wait_ge(s_a, n + 1)
                        eng.wait_ge(s_cl, 16 * n + 16)
                        pe.matmul(banks[:, 4 + u, :], pt[u][0:SEQ, 2, :], cl[0:SEQ, :], start=True, stop=False)
                        for j in range(SEQ):
                            eng.wait_ge(s_ctx[j], 16 * n + 16)
                            for k in range(2):
                                ins = pe.matmul(banks[NQ * j:NQ * j + NQ, 4 + u, :],
                                                pt[u][:, k, NQ * j:NQ * j + NQ], cn[j][:, k, :],
                                                start=False, stop=k == 1)
                            ins.then_inc(s_pv, 1)

                    def turn_a(n, u):
                        eng.wait_ge(s_a, n + 1 + LEAD)
                        eng.wait_ge(s_al, n + 1)
                        for c in range(DC):
                            ins = pe.transpose(banks[:, 6, c * P:(c + 1) * P], a[u][:, c * P:(c + 1) * P], ident[:])
                        ins.then_inc(s_at, 1)

                    def values(n, u):
                        eng.wait_ge(s_al, n + 2)
                        eng.wait_ge(s_x, n + 1)
                        for c in range(DC):
                            ins = mm3(banks[:, 7, :], at[u][0][:, c, :], at[u][1][:, c, :], wv[0][:, c, :],
                                      wv[1][:, c, :], c == 0, c == DC - 1)
                        ins.then_inc(s_o, 1)

                    scores(0, 0)
                    scores(1, 1)
                    turn_p(0, 0)
                    p_ctx(0, 0)
                    with pe.Fori(0, NT // 2 - 1) as i:
                        for u in range(2):
                            n = 2 * i + u + 1
                            scores(n + 1, u)
                            turn_p(n, 1 - u)
                            turn_a(n - 1, u)
                            p_ctx(n, 1 - u)
                            values(n - 1, u)
                    turn_p(NT - 1, 1)
                    turn_a(NT - 2, 0)
                    p_ctx(NT - 1, 1)
                    values(NT - 2, 0)
                    turn_a(NT - 1, 1)
                    values(NT - 1, 1)

        def self_attention(tag, low_rank):
            scale = float(DH) ** -0.5
            HD = HH * DH
            EC = HD // P
            f, r = Area(fa, F_SIZE), Area(ra, R_SIZE)
            bo = f.take(D)
            zero_off = [f.take(HH, P) for _ in range(2)]
            mask, ss = f.take(HH, NQ), [f.take(HH, NQ) for _ in range(2)]
            bqc, bkc, bvb = f.take(2 * EC), f.take(2 * EC), f.take(2 * HD)
            f1 = f.at
            rqk = rv = None
            if low_rank:
                rqk, rv = (r.take(T), r.take(T)), (r.take(T), r.take(T))
            r1 = r.at
            s_c = sem(f"{tag}_constants")
            s_cl = sem(f"{tag}_constant_loads")
            pb = zero_off

            first_half = half_weights(tag, low_rank, 0, HD, EC, f1, r1, rqk, rv)
            if low_rank:
                fw, rw = Area(fa, F_SIZE, f1), Area(ra, R_SIZE, R_SIZE - 4 * DC * P)
                staging = [fw.take(DC, 2 * P)]
                w64 = rw.take(DC, 2 * P), rw.take(DC, 2 * P)
                load, high, low, s_w = split_programs(f"{tag}0", [(*w64, columns(d["L1_attn_w64"]))], staging)
                layer_norm("ne", ahead=((load, high, low), (0,), (0,)))
                s_mm, s_hi, s_lo = sem(f"{tag}0_product"), sem(f"{tag}0_high"), sem(f"{tag}0_low")
                jobs = [(h, k) for h in range(NHALF) for k in range(2)]
            else:
                layer_norm("nb", (d["L0_attn_ln_gamma"], d["L0_attn_ln_beta"]), ahead=(first_half[1][:3], (0, 1, 2), (0,)))

            def constant_loads(eng):
                loads = [(bo, d["L1_attn_fco_b" if low_rank else "L0_attn_b_out"].partition_broadcast(P))]
                if low_rank:
                    loads += [(bqc, d["L1_attn_fcq_b"]),
                              (bkc, d["L1_attn_fck_b"]),
                              (bvb, d["L1_attn_fcv_b"].partition_broadcast(P))]
                for dst, src in loads:
                    eng.dma_start(dst, src).then_inc(s_cl, 16)
                eng.wait_ge(s_cl, 16 * len(loads))

            def constants(eng):
                for u in range(2):
                    pool.memset(pb[u], 0.0)
                if not low_rank:
                    for u in range(2):
                        pool.memset(ss[u], MASKED)
                    pool.memset(mask, 1.0).then_inc(s_c, 1)
                    for j in range(SEQ):
                        eng.wait_ge(s_c, j + 1)
                        m = mask[NQ * j:NQ * j + NQ]
                        pool.affine_select(out=m, in_=m, compare_op=ALU.is_ge, fill=0.0, base=0,
                                           pattern=[[0, HH], [-1, NQ]], channel_multiplier=1).then_inc(s_c, 1)
                    eng.wait_ge(s_c, SEQ + 1)

            if low_rank:
                with nc.Block() as block:
                    @block.sync
                    def _(eng):
                        first_half[1][0](eng)
                        constant_loads(eng)

                    @block.gpsimd
                    def _(eng):
                        first_half[1][2](eng, (0, 1))
                        constants(eng)

                    @block.scalar
                    def _(eng):
                        for j, (h, k) in enumerate(jobs):
                            eng.wait_ge(s_mm, j + 1)
                            act.activation((rqk, rv)[k][0][:, h * HALF:(h + 1) * HALF], banks[:, j, :],
                                           ACT.Copy).then_inc(s_hi, 1)
                            if j == 0:
                                first_half[1][1](eng, (0, 1))

                    @block.vector
                    def _(eng):
                        for j, (h, k) in enumerate(jobs):
                            eng.wait_ge(s_hi, j + 1)
                            tok = slice(h * HALF, (h + 1) * HALF)
                            dve.tensor_tensor((rqk, rv)[k][1][:, tok], banks[:, j, :],
                                              (rqk, rv)[k][0][:, tok].bitcast(F32), ALU.subtract)

                    @block.tensor
                    def _(eng):
                        eng.wait_ge(s_w[0], 1)
                        for j, (h, k) in enumerate(jobs):
                            tok = slice(h * HALF, (h + 1) * HALF)
                            for c in range(DC):
                                ins = mm3(banks[:, j, :], w64[0][:, c, k * P:(k + 1) * P], w64[1][:, c, k * P:(k + 1) * P],
                                          xh[:, c, tok], xl[:, c, tok], c == 0, c == DC - 1)
                            ins.then_inc(s_mm, 1)

            second_half = half_weights(tag, low_rank, 1, HD, EC, f1, r1, rqk, rv)
            for hh, (buffers, programs) in enumerate((first_half, second_half)):
                half_of_heads(tag, low_rank, hh, scale, HD, EC, bo, pb, mask, ss, bqc, bkc, bvb, rqk, rv, buffers,
                              programs, second_half[1] if hh == 0 else None, constant_loads, constants)

        def half_weights(tag, low_rank, hh, HD, EC, f1, r1, rqk, rv):
            name = f"{tag}{hh + 1}"
            f, r = Area(fa, F_SIZE, f1), Area(ra, R_SIZE, r1)
            qt, kt = f.take(EC, T), f.take(EC, T)
            f2 = f.at
            heads = slice(hh * HD, (hh + 1) * HD)
            wo = r.take(EC, D), r.take(EC, D)
            tail = Area(fa, F_SIZE, F_SIZE - 4 * HD).take(4, HD)
            staging = [tail, f.take(4, HD), f.take(4, HD)]
            if low_rank:
                wv, r2 = (r.take(HD), r.take(HD)), r.at
                r.at += 4096
                wqk = (r.take(HD), r.take(HD))
                weights = [(*wqk, d["L1_attn_fcqk"][:, heads]), (*wv, d["L1_attn_fcvv"][:, heads]),
                           (*wo, d["L1_attn_fco_w"][heads, :].rearrange("(c p) n -> p c n", p=P))]
                staging = [tail[:, 0, :], tail[:, 1, :], staging[1]]
                w = (wqk, wqk, wv, wo)
            else:
                wv, r2 = (r.take(DC, HD), r.take(DC, HD)), r.at
                wk, wq = ((r.take(DC, HD), r.take(DC, HD)) for _ in range(2))
                qkv, inner = d["L0_attn_w_qkvT"], 2 * HD

                def part(k):
                    return qkv[:, k * inner + hh * HD:k * inner + (hh + 1) * HD].rearrange("(c p) n -> p c n", p=P)
                weights = [(*wq, part(0)), (*wk, part(1)), (*wv, part(2)),
                           (*wo, d["L0_attn_w_outT"][heads, :].rearrange("(c p) n -> p c n", p=P))]
                w = (wq, wk, wv, wo)
            if hh == 0:
                programs = split_programs(name, weights, staging)
            else:
                programs = (split_programs(name, weights[:1], staging[:1]),
                            split_programs(name + "r", weights[1:], staging[1:]))
            return (qt, kt, f2, r2, w), programs

        def half_of_heads(tag, low_rank, hh, scale, HD, EC, bo, pb, mask, ss, bqc, bkc, bvb, rqk, rv, buffers, programs,
                          following, constant_loads, constants):
            name = f"{tag}{hh + 1}"
            heads = slice(hh * HD, (hh + 1) * HD)
            qt, kt, f2, r2, (wq, wk, wv, wo) = buffers
            wqk = wq
            s_w = programs[3] if hh == 0 else programs[0][3] + programs[1][3]
            s_mm, s_out = sem(f"{name}_qk_product"), sem(f"{name}_qk_taken")
            jobs = [(k, e, h) for k in range(2) for e in range(EC) for h in range(NHALF)]
            NB = 4

            with nc.Block() as block:
                rest = ((2,) if low_rank else (1, 2, 3)) if hh == 0 else None

                @block.sync
                def _(eng):
                    if hh:
                        programs[1][0](eng)
                    elif not low_rank:
                        programs[0](eng, (3,))
                        constant_loads(eng)

                @block.gpsimd
                def _(eng):
                    if hh:
                        programs[1][2](eng)
                    else:
                        if not low_rank:
                            constants(eng)
                        programs[2](eng, rest)

                @block.scalar
                def _(eng):
                    if hh:
                        programs[1][1](eng)
                    else:
                        programs[1](eng, rest)

                @block.vector
                def _(eng):
                    for j, (k, e, h) in enumerate(jobs):
                        eng.wait_ge(s_mm, j + 1)
                        dst = (qt, kt)[k][:, e, h * HALF:(h + 1) * HALF]
                        if low_rank:
                            b = (bqc, bkc)[k][:, hh * EC + e:hh * EC + e + 1]
                            ins = dve.tensor_scalar(dst, banks[:, j % NB, :], b, None, ALU.add)
                        else:
                            ins = dve.tensor_copy(dst, banks[:, j % NB, :])
                        ins.then_inc(s_out, 1)

                @block.tensor
                def _(eng):
                    for j, (k, e, h) in enumerate(jobs):
                        if j >= NB:
                            eng.wait_ge(s_out, j - NB + 1)
                        cols, tok = slice(e * P, (e + 1) * P), slice(h * HALF, (h + 1) * HALF)
                        eng.wait_ge(s_w[0 if low_rank else k], 1)
                        if low_rank:
                            rows = slice(DH * k, DH * k + DH)
                            ins = mm3(banks[:, j % NB, :], wqk[0][rows, cols], wqk[1][rows, cols],
                                      rqk[0][rows, tok], rqk[1][rows, tok])
                        else:
                            w = (wq, wk)[k]
                            for c in range(DC):
                                ins = mm3(banks[:, j % NB, :], w[0][:, c, cols], w[1][:, c, cols], xh[:, c, tok],
                                          xl[:, c, tok], c == 0, c == DC - 1)
                        ins.then_inc(s_mm, 1)

            f, r = Area(fa, F_SIZE, f2), Area(ra, R_SIZE, r2)
            qg, kg, vg = ([f.take(EC, P) for _ in range(2)] for _ in range(3))
            sh, ex = ([f.take(HH, NQ) for _ in range(2)] for _ in range(2))
            mx, sums, rinv = (f.take(2, HH) for _ in range(3))
            xg = [(r.take(P), r.take(P)) if low_rank else (r.take(DC, P), r.take(DC, P)) for _ in range(2)]
            ot = [(r.take(EC, P), r.take(EC, P)) for _ in range(2)]
            (s_g, s_v, s_vg, s_s, s_sh, s_ex, s_pb, s_o, s_oh, s_ol, s_y, s_xa, s_links) = (
                sem(f"{name}_{n}") for n in ("tile", "v", "v_kept", "scores", "shifted", "exp", "p_turned", "o",
                                             "o_high", "o_low", "out", "x_added", "links"))
            s_passed, s_qk, s_vk, s_xb = (sem(f"{name}_{n}") for n in ("passed", "qk_tile", "v_unbiased", "x_biased"))
            src = rv if low_rank else (xh, xl)
            if not low_rank:
                s_vk = s_vg

            def all_steps(engine, step, before=lambda i: None, after=lambda: None):
                with engine.Fori(0, NT // 2 - 2) as i:
                    before(i)
                    for u in range(2):
                        step(2 * i + u, u)
                    after()
                for n in range(NT - 4, NT):
                    step(n, n % 2)

            def there(n):
                return not isinstance(n, int) or n < NT

            with nc.Block() as block:
                if hh == 0:
                    @block.sync
                    def _(eng):
                        following[0][0](eng)

                @block.gpsimd
                def _(eng):
                    def x_tile(n, u):
                        eng.wait_ge(s_v, n + 1)
                        eng.wait_ge(s_w[0], 1)
                        for part in range(2):
                            if low_rank:
                                ins = pool.tensor_copy(xg[u][part], src[part][:, bass.ts(n, P)])
                            else:
                                ins = pool.tensor_copy(xg[u][part], src[part][:, :, bass.ts(n, P)])
                        ins.then_inc(s_g, 1)
                        if hh == 0:
                            pool.tensor_tensor(x[:, n, :], x[:, n, :], bo, ALU.add).then_inc(s_xb, 1)

                    def v_bias(n, u):
                        if low_rank:
                            eng.wait_ge(s_vk, n + 1)
                            v = vg[u].rearrange("p c t -> p (c t)")
                            pool.tensor_tensor(v, v, bvb[:, heads], ALU.add).then_inc(s_vg, 1)

                    x_tile(0, 0)
                    x_tile(1, 1)
                    v_bias(0, 0)
                    if hh == 0:
                        following[0][2](eng)
                    with pool.Fori(0, NT // 2 - 1) as i:
                        for u in range(2):
                            x_tile(2 * i + u + 2, u)
                            v_bias(2 * i + u + 1, 1 - u)
                    v_bias(NT - 1, 1)

                @block.scalar
                def _(eng):
                    def qk_tile(n, u):
                        eng.wait_ge(s_s, n + 1)
                        act.activation(qg[u], qt[:, :, bass.ts(n, P)], ACT.Copy)
                        act.activation(kg[u], kt[:, :, bass.ts(n, P)], ACT.Copy).then_inc(s_qk, 1)

                    def exps(n, u):
                        eng.wait_ge(s_sh, n + 1)
                        act.activation(ex[u], sh[u], ACT.Exp, scale=scale).then_inc(s_ex, 1)

                    def keep_v(n, u):
                        eng.wait_ge(s_v, n + 1 + LEAD)
                        eng.wait_ge(s_o, n + 1)
                        act.activation(vg[u], chunks(banks[:, 4 * u, :]), ACT.Copy).then_inc(s_vk, 1)

                    def o_high(n, u):
                        eng.wait_ge(s_o, n + 1 + LEAD)
                        act.activation(ot[u][0], chunks(banks[:, 4 * u + 3, :]), ACT.Copy).then_inc(s_oh, 1)

                    def step(n, u):
                        o_high(n, u)
                        if there(n + 1):
                            keep_v(n + 1, 1 - u)
                        if there(n + 2):
                            exps(n + 2, u)
                        if there(n + 3):
                            qk_tile(n + 3, 1 - u)

                    qk_tile(0, 0)
                    qk_tile(1, 1)
                    exps(0, 0)
                    exps(1, 1)
                    keep_v(0, 0)
                    qk_tile(2, 0)
                    if hh == 0:
                        following[0][1](eng)
                    all_steps(act, step)

                @block.vector
                def _(eng):
                    links = Links(eng, s_links)
                    eng.sem_inc(s_xa, LEAD)

                    def shifted(n, u):
                        bs = banks[:, 4 * u + 1:4 * u + 3, :].rearrange("p k (h t) -> p (k h) t", h=4)
                        eng.wait_ge(s_s, n + 1 + LEAD)
                        eng.sem_inc(s_passed, 1)
                        for j in range(SEQ):
                            rows = slice(NQ * j, NQ * j + NQ)
                            if low_rank:
                                ins = dve.tensor_copy(ss[u][rows], bs[rows, :, rows])
                            else:
                                ins = dve.copy_predicated(ss[u][rows], mask[rows].bitcast(U32), bs[rows, :, rows])
                        links.link(ins)
                        links.link(dve.reduce_max(mx[:, u, :], ss[u], AX_X))
                        dve.tensor_tensor(sh[u], ss[u], mx[:, u, :].unsqueeze(2).to_broadcast([P, HH, NQ]),
                                          ALU.subtract).then_inc(s_sh, 1)

                    def o_low(n, u):
                        eng.wait_ge(s_oh, n + 1)
                        dve.tensor_tensor(ot[u][1], chunks(banks[:, 4 * u + 3, :]), ot[u][0].bitcast(F32),
                                          ALU.subtract).then_inc(s_ol, 1)

                    def turned(n, u):
                        eng.wait_ge(s_ex, n + 1)
                        links.link(dve.reduce_sum(sums[:, u, :], ex[u], AX_X))
                        links.link(dve.reciprocal(rinv[:, u, :], sums[:, u, :]))
                        links.link(dve.tensor_tensor(ex[u], ex[u], rinv[:, u, :].unsqueeze(2).to_broadcast([P, HH, NQ]),
                                                     ALU.mult))
                        for j in range(SEQ):
                            rows = slice(NQ * j, NQ * j + NQ)
                            ins = dve.transpose(pb[u][rows, :, rows], ex[u][rows])
                        ins.then_inc(s_pb, 1)

                    def add(n, u):
                        eng.wait_ge(s_y, n + 1)
                        if hh == 0:
                            eng.wait_ge(s_xb, n + 1)
                        dve.tensor_tensor(x[:, n, :], banks[:, 4 * u, :], x[:, n, :], ALU.add).then_inc(s_xa, 1)
                        if hh:
                            row_statistics(eng, s_xa, n + 1 + LEAD, s_passed, n)

                    STEPS = 5

                    def step(n, u):
                        o_low(n, u)
                        if there(n + 2):
                            shifted(n + 2, u)
                            turned(n + 2, u)
                        add(n, u)

                    links.enter(0, 2 * STEPS)
                    for n in range(2):
                        shifted(n, n)
                        turned(n, n)
                    links.leave(1)
                    all_steps(dve, step, lambda i: links.enter(i, 2 * STEPS), lambda: links.leave(NT // 2 - 2))

                @block.tensor
                def _(eng):
                    eng.sem_inc(s_s, LEAD)
                    eng.sem_inc(s_v, LEAD)
                    eng.sem_inc(s_o, LEAD)

                    def scores(n, u):
                        eng.wait_ge(s_qk, n + 1)
                        for h in range(HH):
                            rows = slice(DH * (h % 2), DH * (h % 2) + DH)
                            ins = pe.matmul(banks[:, 4 * u + 1 + h % 2, (h // 2) * P:(h // 2 + 1) * P],
                                            qg[u][rows, h // 2, :], kg[u][rows, h // 2, :], start=True, stop=True)
                        ins.then_inc(s_s, 1)

                    def values(n, u):
                        eng.wait_ge(s_g, n + 1)
                        eng.wait_ge(s_xa, n + 1)
                        if low_rank:
                            ins = mm3(banks[:, 4 * u, :], xg[u][0][0:DH], xg[u][1][0:DH], wv[0][0:DH], wv[1][0:DH])
                        else:
                            for c in range(DC):
                                ins = mm3(banks[:, 4 * u, :], xg[u][0][:, c, :], xg[u][1][:, c, :], wv[0][:, c, :],
                                          wv[1][:, c, :], c == 0, c == DC - 1)
                        ins.then_inc(s_v, 1)

                    def p_v(n, u):
                        eng.wait_ge(s_vg, n + 1)
                        eng.wait_ge(s_pb, n + 1)
                        for h in range(HH):
                            rows = slice(DH * (h % 2), DH * (h % 2) + DH)
                            v = vg[u].rearrange("p c t -> p (c t)")
                            ins = pe.matmul(banks[rows, 4 * u + 3, (h // 2) * P:(h // 2 + 1) * P],
                                            v[:, h * DH:(h + 1) * DH], pb[u][:, (h % 2) * 4 + h // 2, :],
                                            start=True, stop=True)
                        ins.then_inc(s_o, 1)

                    def output(n, u):
                        eng.wait_ge(s_ol, n + 1)
                        for c in range(EC):
                            ins = mm3(banks[:, 4 * u, :], ot[u][0][:, c, :], ot[u][1][:, c, :], wo[0][:, c, :],
                                      wo[1][:, c, :], c == 0, c == EC - 1)
                        ins.then_inc(s_y, 1)

                    def step(n, u):
                        p_v(n, u)
                        if there(n + 2):
                            scores(n + 2, u)
                        if there(n + 1):
                            values(n + 1, 1 - u)
                        output(n, u)

                    scores(0, 0)
                    scores(1, 1)
                    values(0, 0)
                    all_steps(pe, step)

        class Plan:

            def __init__(self, layer):
                self.layer, self.experts, self.choices = layer, (E0, E1)[layer], (K0, K1)[layer]
                self.routed = (self.choices * T + self.experts * (CAP - 1)) // CAP
                self.shared = layer == 0
                self.kinds = self.choices + self.shared
                self.tiles = self.routed + (T // CAP if self.shared else 0)
                self.units = (I0, I1)[layer] // P
                f = Area(fa, F_SIZE)
                self.slot = f.take(self.kinds, NT)
                self.weight = f.take(self.kinds, NT)
                self.token = f.take(2 * self.tiles)
                self.expert = f.take(self.tiles)
                self.at = f.at

        def routing(tag, plan, norm):
            layer, E, K = plan.layer, plan.experts, plan.choices
            KN, H = plan.kinds * NT, 2 * plan.tiles
            f = Area(fa, F_SIZE, plan.at)
            gate, gbias = f.take(DC, P), f.take(E)
            logits = f.take(T)
            lg, sc, sel, t1 = (f.take(NT, E) for _ in range(4))
            r = Area(ra, R_SIZE)
            gate_high, gate_low, kept = r.take(DC, P), r.take(DC, P), r.take(NT, E)
            gt, eq = f.take(NT, E, E), f.take(NT, E, E)
            tri = f.take(E, E)
            gm, gk = f.take(NT, G0), f.take(NT, G0)
            mx, sm, rank = f.take(NT), f.take(NT), f.take(NT, E)
            before, end, first_slot = f.take(E), f.take(E), f.take(NT, E)
            need = [f.take(E) for _ in range(T // CAP)]
            choice_slot, choice_weight = f.take(plan.kinds, NT, E), f.take(plan.kinds, NT, E)
            slot, group, place, bits = (f.take(plan.kinds, NT) for _ in range(4))
            from_zero, ids = f.take(P), f.take(NT)
            in_block, in_place = r.take(KN, H), r.take(KN, P)
            tile_end, tile_expert = f.take(plan.tiles, E), f.take(plan.tiles)
            s_ld, s_tri, s_clear, s_gate, s_mm, s_act, s_in, s_kept, s_spread, s_links = (
                sem(f"{tag}_{n}") for n in ("gate", "earlier", "cleared", "gate_split", "products", "activated", "shifted",
                                            "kept", "spread", "links"))

            def compare(links, v, n, dst):
                a4, b4 = gt[:, :, 0:n, 0:n], eq[:, :, 0:n, 0:n]
                if n == E:
                    a4, b4 = gt, eq
                other = v.unsqueeze(2).to_broadcast([P, NT, n, n])
                own = v.unsqueeze(3).to_broadcast([P, NT, n, n])
                dve.tensor_tensor(a4, other, own, ALU.is_gt)
                links.link(dve.tensor_tensor(b4, other, own, ALU.is_equal))
                links.link(dve.tensor_tensor(b4, b4, tri[:, 0:n, 0:n].unsqueeze(1).to_broadcast([P, NT, n, n]),
                                             ALU.mult))
                links.link(dve.tensor_tensor(a4, a4, b4, ALU.add))
                links.link(dve.reduce_sum(dst, a4, AX_X))

            def load_gate(eng, _):
                if layer == 0:
                    eng.dma_start(gbias, d["L0_ffn_gate_bias"].partition_broadcast(P)).then_inc(s_ld, 16)
                eng.wait_ge(s_clear, 1)
                eng.dma_start(gate[:, :, 0:E], d["L0_ffn_gateT" if layer == 0 else "L1_ffn_gateT"]
                              .rearrange("(c p) e -> p c e", p=P)).then_inc(s_ld, 16)

            def gate_highs(eng, which):
                if which:
                    eng.wait_ge(s_ld, 32 if layer == 0 else 16)
                    act.activation(gate_high, gate, ACT.Copy).then_inc(s_gate, 1)

            def gate_lows(eng, _):
                pool.memset(gate, 0.0).then_inc(s_clear, 1)
                pool.memset(tri, 1.0).then_inc(s_tri, 1)
                eng.wait_ge(s_tri, 1)
                pool.affine_select(out=tri, in_=tri, compare_op=ALU.is_gt, fill=0.0, base=0,
                                   pattern=[[1, E], [-1, E]], channel_multiplier=0)
                exact = dict(allow_small_or_imprecise_dtypes=True)
                pool.iota(from_zero, [[1, P]], base=0, channel_multiplier=0, **exact)
                pool.iota(ids, [[P, NT]], base=0, channel_multiplier=1, **exact).then_inc(s_tri, 1)
                eng.wait_ge(s_gate, 1)
                pool.tensor_tensor(gate_low, gate, gate_high.bitcast(F32), ALU.subtract).then_inc(s_gate, 1)

            layer_norm(norm, ahead=((load_gate, gate_highs, gate_lows), (0,), (0,)), rows=normed_dram)

            with nc.Block() as block:
                @block.scalar
                def _(eng):
                    eng.wait_ge(s_mm, 1)
                    act.activation(logits[0:E].rearrange("e (h t) -> e h t", h=NHALF), banks[0:E, 4:4 + NHALF, :],
                                   ACT.Copy).then_inc(s_act, 1)
                    if layer == 0:
                        eng.wait_ge(s_mm, 2)
                        act.activation(sc.rearrange("p t e -> p (t e)"), banks[:, 0, 0:NT * E],
                                       ACT.Sigmoid).then_inc(s_act, 1)
                    else:
                        eng.wait_ge(s_in, 1)
                        act.activation(sc, t1, ACT.Exp).then_inc(s_act, 1)

                @block.vector
                def _(eng):
                    links = Links(eng, s_links)
                    eng.wait_ge(s_tri, 2)
                    if layer == 0:
                        eng.wait_ge(s_act, 2)
                        links.link(dve.tensor_tensor(sel, sc, gbias.unsqueeze(1).to_broadcast([P, NT, E]), ALU.add))
                        links.link(dve.reduce_max(gm, sel.rearrange("p t (g e) -> p t g e", g=G0), AX_X))
                        compare(links, gm, G0, gk)
                        links.link(dve.tensor_scalar(gm, gk, float(GK0), None, ALU.is_lt))
                        links.link(dve.tensor_scalar(gk, gm, -1.0, FAR, ALU.add, ALU.mult))
                        s4 = sel.rearrange("p t (g e) -> p t g e", g=G0)
                        shape = [P, NT, G0, E // G0]
                        links.link(dve.tensor_tensor(s4, s4, gm.unsqueeze(3).to_broadcast(shape), ALU.mult))
                        links.link(dve.tensor_tensor(s4, s4, gk.unsqueeze(3).to_broadcast(shape), ALU.add))
                    else:
                        eng.wait_ge(s_mm, 2)
                        links.link(dve.tensor_copy(sel.rearrange("p t e -> p (t e)"), banks[:, 0, 0:NT * E]))
                        links.link(dve.reduce_max(mx, sel, AX_X))
                        dve.tensor_tensor(t1, sel, mx.unsqueeze(2).to_broadcast([P, NT, E]),
                                          ALU.subtract).then_inc(s_in, 1)
                        eng.wait_ge(s_act, 2)
                    compare(links, sel, E, rank)
                    dve.tensor_scalar(kept, rank, float(K), None, ALU.is_lt).then_inc(s_kept, 1)
                    if layer == 0:
                        weight = sc
                    else:
                        eng.wait_ge(s_kept, 1)
                        links.link(dve.tensor_tensor(lg, kept.bitcast(F32), sc, ALU.mult))
                        links.link(dve.reduce_sum(sm, lg, AX_X))
                        links.link(dve.reciprocal(mx, sm))
                        links.link(dve.tensor_tensor(t1, lg, mx.unsqueeze(2).to_broadcast([P, NT, E]), ALU.mult))
                        weight = t1
                    for k in range(K):
                        dve.scalar_tensor_tensor(choice_weight[:, k, :, :], rank, float(k), weight, ALU.is_equal, ALU.mult)
                    eng.wait_ge(s_mm, 3)
                    total = banks[:, 2, 0:E]
                    links.link(dve.tensor_scalar(need[0], total, 0.0, None, ALU.is_gt))
                    for j in range(1, T // CAP):
                        links.link(dve.scalar_tensor_tensor(need[j], total, float(CAP * j), need[j - 1], ALU.is_gt, ALU.add))
                    tiles = need[-1]
                    links.link(dve.tensor_tensor(gt[:, 0, :, :], tiles.unsqueeze(1).to_broadcast([P, E, E]), tri, ALU.mult))
                    links.link(dve.reduce_sum(before, gt[:, 0, :, :], AX_X))
                    dve.tensor_tensor(end, before, tiles, ALU.add)
                    links.link(dve.scalar_tensor_tensor(
                        first_slot, before.unsqueeze(1).to_broadcast([P, NT, E]), float(CAP),
                        banks[:, 1, 0:NT * E].rearrange("p (t e) -> p t e", t=NT), ALU.mult, ALU.add))
                    for k in range(K):
                        ins = dve.scalar_tensor_tensor(choice_slot[:, k, :, :], rank, float(k), first_slot, ALU.is_equal, ALU.mult)
                    links.link(ins)
                    dve.reduce_sum(plan.weight[:, 0:K, :], choice_weight[:, 0:K, :, :], AX_X)
                    if plan.shared:
                        dve.memset(plan.weight[:, K, :], 1.0)
                        dve.tensor_scalar(slot[:, K, :], ids, float(CAP * plan.routed), None, ALU.add)
                    links.link(dve.reduce_sum(slot[:, 0:K, :], choice_slot[:, 0:K, :, :], AX_X))
                    links.link(dve.tensor_copy(plan.slot.bitcast(U32), slot))
                    for dst, amount, op in ((group, P.bit_length() - 1, ALU.logical_shift_right),
                                            (place, P - 1, ALU.bitwise_and)):
                        links.link(dve.tensor_scalar(bits.bitcast(U32), plan.slot.bitcast(U32), amount, None, op))
                        links.link(dve.tensor_copy(dst, bits.bitcast(U32)))
                    for k in range(plan.kinds):
                        own = slice(k * NT, (k + 1) * NT)
                        dve.tensor_tensor(in_place[:, own, :], from_zero.unsqueeze(1).to_broadcast([P, NT, P]),
                                          place[:, k, :].unsqueeze(2).to_broadcast([P, NT, P]), ALU.is_equal)
                        part, shape = in_block[:, own, :], [P, NT, H]
                        links.link(dve.tensor_tensor(part, from_zero[:, 0:H].unsqueeze(1).to_broadcast(shape),
                                                     group[:, k, :].unsqueeze(2).to_broadcast(shape), ALU.is_equal))
                        dve.tensor_tensor(part, part.bitcast(F32), ids.unsqueeze(2).to_broadcast(shape),
                                          ALU.mult).then_inc(s_spread, 1)
                    shape = [P, plan.tiles, E]
                    links.link(dve.tensor_tensor(tile_end, end.unsqueeze(1).to_broadcast(shape),
                                                 from_zero[:, 0:plan.tiles].unsqueeze(2).to_broadcast(shape), ALU.is_le))
                    links.link(dve.reduce_sum(tile_expert, tile_end, AX_X))
                    links.link(dve.tensor_scalar(tile_expert, tile_expert, float(E - 1), None, ALU.min))
                    if plan.shared:
                        links.link(dve.memset(tile_expert[:, plan.routed:plan.tiles], float(E)))
                    dve.tensor_copy(plan.expert.bitcast(U32), tile_expert)
                    eng.wait_ge(s_mm, 4)
                    dve.tensor_copy(plan.token.bitcast(U32), banks[:, 3, 0:H])

                @block.tensor
                def _(eng):
                    eng.wait_ge(s_gate, 2)
                    for h in range(NHALF):
                        tok = slice(h * HALF, (h + 1) * HALF)
                        for c in range(DC):
                            ins = mm3(banks[:, 4 + h, :], gate_high[:, c, :], gate_low[:, c, :], xh[:, c, tok],
                                      xl[:, c, tok], c == 0, c == DC - 1)
                    ins.then_inc(s_mm, 1)
                    eng.wait_ge(s_act, 1)
                    for t in range(NT):
                        ins = pe.transpose(banks[:, 0, t * E:(t + 1) * E], logits[0:E, t * P:(t + 1) * P], ident[0:E, 0:E])
                    ins.then_inc(s_mm, 1)
                    eng.wait_ge(s_kept, 1)
                    before_own = banks[:, 1, 0:NT * E].rearrange("p (t e) -> p t e", e=E)
                    for t in range(NT):
                        pe.matmul(banks[:, 2, 0:E], ones[:], kept[:, t, :], start=t == 0, stop=t == NT - 1)
                    pe.matmul(before_own, earlier[:], kept, start=True, stop=False)
                    for t in reversed(range(NT - 1)):
                        ins = pe.matmul(before_own[:, t + 1:NT, :], ones[:], kept[:, t:t + 1, :]
                                        .to_broadcast([P, NT - 1 - t, E]), start=False, stop=t == 0)
                    ins.then_inc(s_mm, 1)
                    for m in range(KN):
                        if m % NT == 0:
                            eng.wait_ge(s_spread, m // NT + 1)
                        ins = pe.matmul(banks[:, 3, 0:H], in_place[:, m, :], in_block[:, m, :], start=m == 0,
                                        stop=m == KN - 1)
                    ins.then_inc(s_mm, 1)

        def experts(tag, plan, w, to=None):
            U, TILES, W = plan.units, plan.tiles, WEIGHT_BUFFERS
            total = U * TILES
            y_dram = nc.dram_tensor(f"{tag}_y_scratch", [TILES * CAP, D], F32, kind="Internal").ap()
            f, r = Area(fa, F_SIZE, plan.at), Area(ra, R_SIZE)
            st = [f.take(3, D) for _ in range(W)]
            sg, hf = ([f.take(CAP) for _ in range(2)] for _ in range(2))
            xt, ys = ([f.take(2, D) for _ in range(2)] for _ in range(2))
            ids, table = [f.take(2) for _ in range(2)], f.take(1)
            wh, wl = ([r.take(3, D) for _ in range(W)] for _ in range(2))
            hh_, hl = ([r.take(CAP) for _ in range(2)] for _ in range(2))
            gh, gl = ([r.take(DC, CAP) for _ in range(2)] for _ in range(2))
            s_ld = [sem(f"{tag}_loaded{b}") for b in range(W)]
            s_rows = [gather_sem(f"{tag}_rows{u}") for u in range(2)]
            s_stored = [sem(f"{tag}_stored{u}") for u in range(2)]
            (s_wh, s_wp, s_wd, s_h, s_sg, s_hf, s_hh, s_hl, s_y, s_kept, s_ids, s_passed, s_turned, s_xh, s_xl) = (
                sem(f"{tag}_{n}") for n in ("w_high", "w_low_pool", "w_low_vector", "h_products", "silu", "h", "h_high",
                                            "h_low", "y", "y_kept", "ids", "passed", "turned", "x_high", "x_low"))
            HB, YB, XB = 0, 2, 4
            PEELED = 3
            PAIRED = (TILES - PEELED) // 2 - 1
            assert (TILES - PEELED) % 2 == 0 and (2 * U) % W == 0
            LAST = 2 * PAIRED + 2
            TURN = U - 2

            TILES_HALF = NT // 2
            spare = (F_SIZE - f.at) // D
            EARLY = 24 if plan.shared else 0
            yt = [Area(fa, F_SIZE, F_SIZE - D * (m + 1)).take(D) for m in range(spare)]
            yt += [part[:, m // 2, m % 2 * D:(m % 2 + 1) * D].bitcast(F32) for part in (xh, xl) for m in range(2 * DC)]
            assert EARLY <= len(yt)
            yt += [Area(fa, F_SIZE, plan.at + D * m).take(D) for m in range((F_SIZE - plan.at) // D - spare - 1)]
            yt += [Area(ra, R_SIZE, D * m).take(D).bitcast(F32) for m in range(max(0, plan.kinds * NT - len(yt)))]
            s_got = [gather_sem(f"{tag}_y_rows{m}") for m in range(plan.choices * 2)]
            if plan.shared:
                s_got += [sem(f"{tag}_shared_y_rows{m}") for m in range(2)]
            s_links = sem(f"{tag}_sum_links")
            summed = [0]

            def y_rows(m):
                k, t = divmod(m, NT)
                pool.indirect_dma_start(yt[m], None, y_dram[0:CAP * plan.routed, :], bass.IndirectOffsetOnAxis(
                    ap=plan.slot.bitcast(U32)[:, k, t:t + 1], axis=0)).then_inc(s_got[m // TILES_HALF], 16)

            def add_rows(eng, which):
                for m in which:
                    k, t = divmod(m, NT)
                    if m % TILES_HALF == 0:
                        eng.wait_ge(s_got[m // TILES_HALF], 16 * TILES_HALF)
                    ins = dve.scalar_tensor_tensor(x[:, t, :], yt[m], plan.weight[:, k, t:t + 1], x[:, t, :],
                                                   ALU.mult, ALU.add)
                    if m % TILES_HALF == TILES_HALF - 1:
                        ins.then_inc(s_links, 1)
                        summed[0] += 1
                        eng.wait_ge(s_links, summed[0])
                        if k == plan.choices - 1 and plan.layer == 0:
                            for tile in range(t + 1 - TILES_HALF, t + 1):
                                dve.bn_stats(stats[:, tile, :], x[:, tile, :])

            def all_tiles(engine, tile, first=lambda: None):
                for j in (0, 1):
                    tile(j, j, 0)
                with engine.Fori(0, PAIRED) as i:
                    first()
                    for u in range(2):
                        tile(2 * i + u + 2, u, i + 1)
                for j in range(LAST, TILES):
                    tile(j, j % 2, j // 2)

            POOL_UNITS = total - W + 1 if plan.shared else total

            def there(n, limit):
                return not isinstance(n, int) or n < limit

            def late(kinds):
                return [m for half in range(2) for k in kinds
                        for m in range(k * NT + half * TILES_HALF, k * NT + (half + 1) * TILES_HALF)]

            def wait_stored(eng, tiles):
                for u in range(2):
                    eng.wait_ge(s_stored[u], 16 + 16 * ((tiles + 1 - u) // 2))

            with nc.Block() as block:
                @block.sync
                def _(eng):
                    def tile(j, u, i):
                        e = eng.value_load(plan.expert.bitcast(U32)[0:1, bass.ds(j, 1)], min_val=0,
                                           max_val=w.shape[0] // U - 1)
                        for q in range(U):
                            n, b = U * j + q, (U * u + q) % W
                            eng.wait_ge(s_wp, n + 1)
                            eng.wait_ge(s_wd, n + 1)
                            eng.dma_start(st[b], w[e * U + q]).then_inc(s_ld[b], 16)
                    all_tiles(eng, tile)
                    wait_stored(eng, TILES)
                    if plan.shared:
                        for m in range(plan.choices * NT, plan.kinds * NT):
                            at = CAP * plan.routed + P * (m - plan.choices * NT)
                            eng.dma_start(yt[m], y_dram[at:at + P, :]).then_inc(s_got[m // TILES_HALF], 16)
                    if to is not None:
                        s_out = sem("x_stored")
                        for half in range(2):
                            eng.wait_ge(s_links, (half + 1) * plan.choices)
                            own = slice(half * TILES_HALF, (half + 1) * TILES_HALF)
                            eng.dma_start(to[:, own, :], x[:, own, :]).then_inc(s_out, 16)
                        eng.wait_ge(s_out, 32)

                @block.gpsimd
                def _(eng):
                    def gather(j, u):
                        eng.wait_ge(s_turned, j + 1)
                        eng.sem_inc(s_passed, 1)
                        pool.tensor_copy(ids[u].bitcast(U32), plan.token.bitcast(U32)[:, bass.ts(j, 2)]).then_inc(s_ids, 1)
                        eng.wait_ge(s_ids, j + 1)
                        eng.sem_inc(s_passed, 1)
                        for s in range(2):
                            pool.indirect_dma_start(xt[u][:, s, :], None, normed_dram, bass.IndirectOffsetOnAxis(
                                ap=ids[u].bitcast(U32)[:, s:s + 1], axis=0)).then_inc(s_rows[u], 16)

                    def weights_low(n, b):
                        eng.wait_ge(s_wh, n + 1)
                        pool.tensor_tensor(wl[b][:, 0:2, :], st[b][:, 0:2, :], wh[b][:, 0:2, :].bitcast(F32),
                                           ALU.subtract).then_inc(s_wp, 1)

                    eng.sem_inc(s_wp, W)
                    gather(0, 0)
                    gather(1, 1)
                    for n in range(W - 1):
                        weights_low(n, n)
                    gather(2, 0)

                    def tile(j, u, i):
                        for q in range(U):
                            if there(U * j + q + W - 1, POOL_UNITS):
                                weights_low(U * j + q + (W - 1), (U * u + q + W - 1) % W)
                            if q == TURN and there(j + 3, TILES):
                                gather(j + 3, 1 - u)
                    all_tiles(eng, tile)
                    if plan.shared:
                        wait_stored(eng, plan.routed)
                        for m in range(EARLY):
                            y_rows(m)
                    wait_stored(eng, TILES)
                    for m in late(range(plan.choices)):
                        if m >= EARLY:
                            y_rows(m)

                @block.scalar
                def _(eng):
                    def weights_high(n, b, k):
                        eng.wait_ge(s_ld[b], 16 * k + 16)
                        eng.wait_ge(s_y, n + 1)
                        act.activation(wh[b], st[b], ACT.Copy).then_inc(s_wh, 1)

                    def rows_high(j, u):
                        eng.wait_ge(s_turned, j + 1 + LEAD)
                        act.activation(gh[u].rearrange("p c (s t) -> p s c t", s=2),
                                       banks[:, XB:XB + 2, :].rearrange("p s (c t) -> p s c t", c=DC),
                                       ACT.Copy).then_inc(s_xh, 1)

                    def keep_y(j, u, i):
                        eng.wait_ge(s_y, U * j + W)
                        eng.wait_ge(s_stored[1 - u], 16 * (i + u))
                        act.activation(ys[1 - u], banks[:, YB:YB + 2, :], ACT.Copy).then_inc(s_kept, 1)
                        eng.wait_ge(s_kept, j + 1)
                        eng.dma_start(y_dram.rearrange("(j s p) d -> j p s d", s=2, p=P)[j - 1],
                                      ys[1 - u]).then_inc(s_stored[1 - u], 16)

                    def hidden(n, b):
                        eng.wait_ge(s_h, n + 1)
                        act.activation(sg[b], banks[:, HB + b, 0:CAP], ACT.Silu).then_inc(s_sg, 1)
                        eng.wait_ge(s_hf, n + 1 + LEAD)
                        eng.wait_ge(s_y, n + (W - 1))
                        act.activation(hh_[b], hf[b], ACT.Copy).then_inc(s_hh, 1)

                    eng.sem_inc(s_kept, 1)
                    for u in range(2):
                        eng.sem_inc(s_stored[u], 16)
                    for n in range(W - 1):
                        weights_high(n, n, 0)
                        if n == 0:
                            rows_high(0, 0)

                    def tile(j, u, i):
                        for q in range(U):
                            n = U * j + q
                            hidden(n, q % 2)
                            if q == 0 and not (isinstance(j, int) and j == 0):
                                keep_y(j, u, i)
                            if q == TURN and there(j + 1, TILES):
                                rows_high(j + 1, 1 - u)
                            if there(n + W - 1, total):
                                ahead = U * u + q + W - 1
                                weights_high(n + (W - 1), ahead % W, (2 * U // W) * i + ahead // W)
                    all_tiles(eng, tile, lambda: act.activation(table, epst[:], ACT.Silu))
                    keep_y(TILES, TILES % 2, TILES // 2)
                    wait_stored(eng, TILES)

                @block.vector
                def _(eng):
                    def weights_low(n, b):
                        eng.wait_ge(s_wh, n + 1)
                        if not there(n, POOL_UNITS):
                            eng.wait_ge(s_wp, POOL_UNITS + W)
                            dve.tensor_tensor(wl[b][:, 0:2, :], st[b][:, 0:2, :], wh[b][:, 0:2, :].bitcast(F32),
                                              ALU.subtract).then_inc(s_wp, 1)
                        dve.tensor_tensor(wl[b][:, 2, :], st[b][:, 2, :], wh[b][:, 2, :].bitcast(F32),
                                          ALU.subtract).then_inc(s_wd, 1)

                    def rows_low(j, u):
                        eng.wait_ge(s_xh, j + 1)
                        for s in range(2):
                            cols = slice(s * P, (s + 1) * P)
                            ins = dve.tensor_tensor(gl[u][:, :, cols], chunks(banks[:, XB + s, :]),
                                                    gh[u][:, :, cols].bitcast(F32), ALU.subtract)
                        ins.then_inc(s_xl, 1)

                    eng.sem_inc(s_wd, W)
                    eng.sem_inc(s_hf, LEAD)
                    eng.sem_inc(s_xl, 1)
                    for n in range(W - 1):
                        weights_low(n, n)
                        if n == 0:
                            rows_low(0, 0)

                    def tile(j, u, i):
                        for q in range(U):
                            n, b = U * j + q, q % 2
                            eng.wait_ge(s_sg, n + 1)
                            dve.tensor_tensor(hf[b], banks[:, HB + b, CAP:2 * CAP], sg[b], ALU.mult).then_inc(s_hf, 1)
                            eng.wait_ge(s_hh, n + 1)
                            dve.tensor_tensor(hl[b], hf[b], hh_[b].bitcast(F32), ALU.subtract).then_inc(s_hl, 1)
                            if q == TURN and there(j + 1, TILES):
                                rows_low(j + 1, 1 - u)
                            if there(n + W - 1, total):
                                weights_low(n + (W - 1), (U * u + q + W - 1) % W)
                            if plan.shared and isinstance(j, int) and j == TILES - 1:
                                add_rows(eng, range(q * TILES_HALF, (q + 1) * TILES_HALF))
                    all_tiles(eng, tile)
                    if plan.shared:
                        add_rows(eng, range(U * TILES_HALF, EARLY // TILES_HALF * TILES_HALF))
                        add_rows(eng, range(plan.choices * NT, plan.kinds * NT))
                    add_rows(eng, [m for m in late(range(plan.choices)) if m >= EARLY // TILES_HALF * TILES_HALF])

                @block.tensor
                def _(eng):
                    eng.sem_inc(s_y, W)
                    eng.sem_inc(s_turned, LEAD)

                    def turn(j, u, i):
                        eng.wait_ge(s_rows[u], 32 * i + 32)
                        eng.wait_ge(s_xl, j + 1)
                        for s in range(2):
                            for c in range(DC):
                                cols = slice(c * P, (c + 1) * P)
                                ins = pe.transpose(banks[:, XB + s, cols], xt[u][:, s, cols], ident[:])
                        ins.then_inc(s_turned, 1)

                    def up(n, j, u, q, b):
                        if q == 0:
                            eng.wait_ge(s_xl, j + 2)
                        eng.wait_ge(s_wp, n + 1 + W)
                        eng.wait_ge(s_hf, n + 1)
                        for k in range(2):
                            for c in range(DC):
                                cols = slice(c * P, (c + 1) * P)
                                ins = mm3(banks[:, HB + q % 2, k * CAP:(k + 1) * CAP], wh[b][:, k, cols], wl[b][:, k, cols],
                                          gh[u][:, c, :], gl[u][:, c, :], c == 0, c == DC - 1)
                        ins.then_inc(s_h, 1)

                    def down(n, j, q, b):
                        eng.wait_ge(s_hl, n + 1)
                        eng.wait_ge(s_wd, n + 1 + W)
                        if q == 0:
                            eng.wait_ge(s_kept, j + 1)
                        for s in range(2):
                            cols = slice(s * P, (s + 1) * P)
                            ins = mm3(banks[:, YB + s, :], hh_[q % 2][:, cols], hl[q % 2][:, cols], wh[b][:, 2, :],
                                      wl[b][:, 2, :], q == 0, q == U - 1)
                        ins.then_inc(s_y, 1)

                    def tile(j, u, i):
                        for q in range(U):
                            n = U * j + q
                            if q == TURN and there(j + 1, TILES):
                                turn(j + 1, 1 - u, i + u)
                            if q < U - 1:
                                up(n + 1, j, u, q + 1, (U * u + q + 1) % W)
                            elif there(j + 1, TILES):
                                up(n + 1, j + 1, 1 - u, 0, (U * u + q + 1) % W)
                            down(n, j, q, (U * u + q) % W)

                    turn(0, 0, 0)
                    up(0, 0, 0, 0, 0)
                    all_tiles(eng, tile)

        def cross_heads():
            scale = float(XD) ** -0.5
            f, r = Area(fa, F_SIZE), Area(ra, R_SIZE)
            qt, bvb, bob = f.take(DC, T), f.take(D), f.take(D)
            bqc, bkc, own = f.take(DC), f.take(DC), f.take(4)
            qblk = [f.take(DC, P) for _ in range(2)]
            stg = [f.take(DC, SE) for _ in range(2)]
            f2 = f.at
            staging = [f.take(DC, D) for _ in range(3)]
            lastT, vl = f.take(DC, B), f.take(DC, D)
            wk, wv, wo = ((r.take(DC, D), r.take(DC, D)) for _ in range(3))
            r2 = r.at
            wq = r.take(DC, D), r.take(DC, D)
            load, high, low, s_w = split_programs("xb", [
                (*wq, columns(d["L1_xattn_W_Q"])), (*wv, columns(d["L1_xattn_W_V"])),
                (*wk, columns(d["L1_xattn_W_K"])), (*wo, columns(d["L1_xattn_W_O"]))], staging)
            layer_norm("nd", ahead=((load, high, low), (0, 1, 2), (0,)))
            s_b, s_mm, s_out, s_vl = sem("xb_biases"), sem("xb_product"), sem("xb_taken"), sem("xb_last_v")
            s_own, s_zero = sem("xb_own_heads"), sem("xb_zeros")
            s_ld = [sem(f"xb_ctx{u}") for u in range(2)]
            jobs = [(e, h) for e in range(DC) for h in range(NHALF)]
            jobs.insert(len(jobs) // 2, None)
            NB = 4

            with nc.Block() as block:
                @block.sync
                def _(eng):
                    for dst, src in ((bqc, d["L1_xattn_b_Q"]),
                                     (bkc, d["L1_xattn_b_K"]),
                                     (bvb, d["L1_xattn_b_V"].partition_broadcast(P)),
                                     (bob, d["L1_xattn_b_O"].partition_broadcast(P)),
                                     (lastT, d["ctxLastT"])):
                        eng.dma_start(dst, src).then_inc(s_b, 16)
                    load(eng, (3,))
                    eng.wait_ge(s_zero, 1)
                    for u in range(2):
                        eng.dma_start(stg[u][:, :, 0:S], d["ctxT"][u]).then_inc(s_ld[u], 16)
                    eng.wait_ge(s_out, len(jobs) // 2 + 1)
                    eng.dma_start(vlast_dram.rearrange("b c d -> b (c d)"),
                                  vl[0:B].rearrange("b c d -> b (c d)")).then_inc(s_vl, 16)
                    eng.wait_ge(s_vl, 16)
                    eng.wait_ge(s_b, 80)

                @block.gpsimd
                def _(eng):
                    pool.memset(vl[0:B], 0.0)
                    for u in range(2):
                        ins = pool.memset(stg[u][:, :, S:SE], 0.0)
                    ins.then_inc(s_zero, 1)
                    pool.memset(own, 1.0).then_inc(s_own, 1)
                    eng.wait_ge(s_own, 1)
                    pool.affine_select(out=own, in_=own, compare_op=ALU.is_ge, fill=0.0, base=0,
                                       pattern=[[-XD, 4]], channel_multiplier=1).then_inc(s_own, 1)
                    eng.wait_ge(s_own, 2)
                    pool.affine_select(out=own, in_=own, compare_op=ALU.is_gt, fill=0.0, base=XD,
                                       pattern=[[XD, 4]], channel_multiplier=-1)
                    low(eng, (1, 2, 3))

                @block.scalar
                def _(eng):
                    high(eng, (1, 2, 3))

                @block.vector
                def _(eng):
                    eng.wait_ge(s_b, 80)
                    for j, job in enumerate(jobs):
                        eng.wait_ge(s_mm, j + 1)
                        if job is None:
                            eng.wait_ge(s_zero, 1)
                            for c in range(DC):
                                cols = slice(c * P, (c + 1) * P)
                                ins = dve.tensor_tensor(vl[0:B, c, cols], banks[0:B, 7, cols], bvb[0:B, cols], ALU.add)
                        else:
                            e, h = job
                            ins = dve.tensor_scalar(qt[:, e, h * HALF:(h + 1) * HALF], banks[:, j % NB, :],
                                                    bqc[:, e:e + 1], None, ALU.add)
                        ins.then_inc(s_out, 1)

                @block.tensor
                def _(eng):
                    eng.wait_ge(s_w[0], 1)
                    for j, job in enumerate(jobs):
                        if j >= NB:
                            eng.wait_ge(s_out, j - NB + 1)
                        if job is None:
                            eng.wait_ge(s_b, 80)
                            eng.wait_ge(s_w[1], 1)
                            for c in range(DC):
                                for part in range(2):
                                    ins = pe.matmul(banks[0:B, 7, :], lastT[:, c, :], wv[part][:, c, :].bitcast(F32),
                                                    start=c + part == 0, stop=c == DC - 1 and part == 1)
                        else:
                            e, h = job
                            cols, tok = slice(e * P, (e + 1) * P), slice(h * HALF, (h + 1) * HALF)
                            for c in range(DC):
                                ins = mm3(banks[:, j % NB, :], wq[0][:, c, cols], wq[1][:, c, cols], xh[:, c, tok],
                                          xl[:, c, tok], c == 0, c == DC - 1)
                        ins.then_inc(s_mm, 1)

            f, r = Area(fa, F_SIZE, f2), Area(ra, R_SIZE, r2)
            kt = [f.take(DC, SE) for _ in range(2)]
            v = [f.take(2, D) for _ in range(2)]
            vlast = [f.take(D) for _ in range(2)]
            pr = [f.take(DC, SE) for _ in range(2)]
            pt, ot = f.take(3, D), f.take(DC, P)
            mx, bias, rs, rinv = (f.take(2, DC) for _ in range(4))
            cx = [(r.take(DC, SE), r.take(DC, SE)) for _ in range(2)]
            oh, ol = r.take(DC, P), r.take(DC, P)
            s_vld = [sem(f"xb_vlast{u}") for u in range(2)]
            (s_ch, s_cl, s_kp, s_vp, s_k, s_v, s_qb, s_sc, s_bias, s_ex, s_rinv, s_pn, s_t, s_ta, s_td, s_pv,
             s_o, s_oh, s_ol, s_y, s_x, s_links) = (
                sem(f"xb_{n}") for n in (
                    "ctx_high", "ctx_low", "k_product", "v_product", "k_kept", "v_kept", "q_block", "scores", "bias",
                    "exp", "sums", "p_normed", "p_turned", "p_kept_a", "p_kept_d", "pv", "o_kept", "o_high", "o_low",
                    "out", "x_added", "links"))
            s_passed = sem("xb_passed")
            SC = 2
            T0, T1 = 6, 7

            with nc.Block() as block:
                @block.sync
                def _(eng):
                    def load_last(n, u):
                        eng.wait_ge(s_pv, n + 1)
                        eng.dma_start(vlast[u][0:DC, :], vlast_dram[n]).then_inc(s_vld[u], 16)

                    for u in range(2):
                        load_last(u, u)
                    with eng.Fori(0, B // 2 - 1) as i:
                        for u in range(2):
                            n = 2 * i + u + 2
                            eng.wait_ge(s_cl, n + 1)
                            eng.dma_start(stg[u][:, :, 0:S], d["ctxT"][n]).then_inc(s_ld[u], 16)
                            load_last(n, u)

                @block.gpsimd
                def _(eng):
                    eng.sem_inc(s_cl, LEAD)

                    def ctx_low(n, u):
                        eng.wait_ge(s_ch, n + 1)
                        pool.tensor_tensor(cx[u][1], stg[u], cx[u][0].bitcast(F32), ALU.subtract).then_inc(s_cl, 1)

                    def step(m, u, after):
                        eng.wait_ge(s_sc, m + 1)
                        shape = [P, DC, 4, NQ]
                        pool.tensor_tensor(qblk[u].rearrange("p c (h q) -> p c h q", h=4),
                                           qt[:, :, bass.ts(m, NQ)].unsqueeze(2).to_broadcast(shape),
                                           own.unsqueeze(1).unsqueeze(3).to_broadcast(shape), ALU.mult).then_inc(s_qb, 1)
                        if after:
                            ctx_low(m + 1, 1 - u)
                        eng.wait_ge(s_rinv, m + 1)
                        pool.tensor_tensor(pr[u][:, :, 0:S], pr[u][:, :, 0:S],
                                           rinv[:, u, :].unsqueeze(2).to_broadcast([P, DC, S]),
                                           ALU.mult).then_inc(s_pn, 1)

                    ctx_low(0, 0)
                    step(0, 0, True)
                    with pool.Fori(0, NT - 1) as g:
                        for j in range(SEQ):
                            step(SEQ * g + j + 1, (j + 1) % 2, True)
                    for m in range(B - SEQ + 1, B):
                        step(m, m % 2, m + 1 < B)

                @block.scalar
                def _(eng):
                    def ctx_high(half, n, u):
                        eng.wait_ge(s_ld[u], 16 * half + 16)
                        if not (isinstance(n, int) and n < LEAD):
                            eng.wait_ge(s_vp, 2 * n)
                        act.activation(cx[u][0], stg[u], ACT.Copy).then_inc(s_ch, 1)

                    def keep_k(m, u):
                        for e in range(DC):
                            eng.wait_ge(s_kp, DC * m + (e + 1))
                            if e == 0:
                                eng.wait_ge(s_sc, m + 1)
                            act.activation(kt[u][:, e, :], banks[:, e % 2, 0:SE], ACT.Identity,
                                           bias=bkc[:, e:e + 1]).then_inc(s_k, 1)

                    def exps(m, u):
                        eng.wait_ge(s_bias, m + 1)
                        for c in range(DC):
                            ins = act.activation(pr[u][:, c, 0:S], banks[:, SC + c, 0:S], ACT.Exp,
                                                 bias=bias[:, u, c:c + 1], scale=scale, accum_out=rs[:, u, c:c + 1])
                        ins.then_inc(s_ex, 1)

                    def keep_p(n):
                        eng.wait_ge(s_t, 3 * n + 1)
                        act.activation(pt[:, 0, :], banks[:, T0, :], ACT.Copy).then_inc(s_ta, 1)
                        eng.wait_ge(s_t, 3 * n + 3)
                        act.activation(pt[0:DC, 2, 0:P], banks[0:DC, 0, 0:P], ACT.Copy).then_inc(s_ta, 1)

                    def step(g, j, after, after2):
                        n = SEQ * g + j
                        if after:
                            keep_k(n + 1, (j + 1) % 2)
                        if after2:
                            ctx_high(2 * g + (j + 2) // 2, n + 2, j % 2)
                        keep_p(n)
                        if after:
                            exps(n + 1, (j + 1) % 2)

                    def tile_out(g):
                        eng.wait_ge(s_o, SEQ * g + (SEQ + 1))
                        eng.wait_ge(s_y, g + 1)
                        act.activation(oh, ot, ACT.Copy).then_inc(s_oh, 1)

                    eng.sem_inc(s_ta, LEAD)
                    ctx_high(0, 0, 0)
                    keep_k(0, 0)
                    ctx_high(0, 1, 1)
                    exps(0, 0)
                    with act.Fori(0, NT - 1) as g:
                        for j in range(SEQ):
                            step(g, j, True, True)
                        tile_out(g)
                    for j in range(SEQ):
                        step(NT - 1, j, j < SEQ - 1, j < SEQ - 2)
                    tile_out(NT - 1)

                @block.vector
                def _(eng):
                    links = Links(eng, s_links)

                    def keep_v(m, u):
                        for k in range(2):
                            eng.wait_ge(s_vp, 2 * m + (k + 1 + LEAD))
                            if k == 0:
                                eng.wait_ge(s_pv, m + 1)
                            dve.tensor_tensor(v[u][:, k, :], banks[:, k, :], bvb, ALU.add).then_inc(s_v, 1)

                    def tops(m, u):
                        eng.wait_ge(s_sc, m + 1 + LEAD)
                        links.link(dve.reduce_max(mx[:, u, :], banks[:, SC:SC + DC, 0:S], AX_X))
                        dve.tensor_scalar(bias[:, u, :], mx[:, u, :], -scale, None, ALU.mult).then_inc(s_bias, 1)

                    def sums(m, u):
                        eng.wait_ge(s_ex, m + 1)
                        dve.reciprocal(rinv[:, u, :], rs[:, u, :]).then_inc(s_rinv, 1)

                    def step(g, j, after):
                        n = SEQ * g + j
                        if after:
                            keep_v(n + 1, (j + 1) % 2)
                        eng.wait_ge(s_t, 3 * n + 2)
                        dve.tensor_copy(pt[:, 1, :], banks[:, T1, :]).then_inc(s_td, 1)
                        if after:
                            tops(n + 1, (j + 1) % 2)
                            sums(n + 1, (j + 1) % 2)
                        eng.wait_ge(s_pv, n + 1 + LEAD)
                        o = chunks(banks[:, T1, :])
                        for h in range(4):
                            rows = slice(XD * h, XD * h + XD)
                            ins = dve.tensor_copy(ot[rows, :, NQ * j:NQ * j + NQ], o[rows, :, rows])
                        ins.then_inc(s_o, 1)

                    def tile_out(g):
                        eng.wait_ge(s_oh, g + 1)
                        dve.tensor_tensor(ol, ot, oh.bitcast(F32), ALU.subtract).then_inc(s_ol, 1)
                        links.link(dve.tensor_tensor(x[:, g, :], x[:, g, :], bob, ALU.add))
                        eng.wait_ge(s_y, g + 2)
                        dve.tensor_tensor(x[:, g, :], banks[:, T0, :], x[:, g, :], ALU.add).then_inc(s_x, 1)
                        row_statistics(eng, s_x, g + 2, s_passed, g)

                    eng.sem_inc(s_x, 1)
                    eng.sem_inc(s_o, 1)
                    keep_v(0, 0)
                    tops(0, 0)
                    sums(0, 0)
                    with dve.Fori(0, NT - 1) as g:
                        links.enter(g, SEQ + 1)
                        for j in range(SEQ):
                            step(g, j, True)
                        tile_out(g)
                        links.leave(NT - 1)
                    for j in range(SEQ):
                        step(NT - 1, j, j < SEQ - 1)
                    tile_out(NT - 1)

                @block.tensor
                def _(eng):
                    eng.sem_inc(s_vp, 2)
                    eng.sem_inc(s_y, 1)
                    eng.sem_inc(s_sc, LEAD)
                    eng.sem_inc(s_pv, LEAD)

                    def keys_values(m, u, before=None):
                        eng.wait_ge(s_cl, m + 1 + LEAD)
                        if not (isinstance(m, int) and m == 0):
                            eng.wait_ge(s_v, 2 * m)
                            eng.wait_ge(s_ta, 2 * m)
                        for e in range(DC):
                            if e >= 2:
                                eng.wait_ge(s_k, DC * m + (e - 1))
                            cols = slice(e * P, (e + 1) * P)
                            for c in range(DC):
                                ins = mm3(banks[:, e % 2, 0:SE], wk[0][:, c, cols], wk[1][:, c, cols], cx[u][0][:, c, :],
                                          cx[u][1][:, c, :], c == 0, c == DC - 1)
                            ins.then_inc(s_kp, 1)
                        if before is not None:
                            tile_out(before)
                        for k in range(2):
                            eng.wait_ge(s_k, DC * m + (k + 3))
                            for c in range(DC):
                                rows = slice(k * P, (k + 1) * P)
                                ins = mm3(banks[:, k, :], cx[u][0][:, c, rows], cx[u][1][:, c, rows], wv[0][:, c, :],
                                          wv[1][:, c, :], c == 0, c == DC - 1)
                            ins.then_inc(s_vp, 1)

                    def scores(m, u):
                        eng.wait_ge(s_qb, m + 1)
                        eng.wait_ge(s_k, DC * m + DC)
                        if not (isinstance(m, int) and m == 0):
                            eng.wait_ge(s_ex, m)
                        for c in range(DC):
                            ins = pe.matmul(banks[:, SC + c, 0:S], qblk[u][:, c, :], kt[u][:, c, 0:S], start=True, stop=True)
                        ins.then_inc(s_sc, 1)

                    def turn(g, j, after):
                        n, u = SEQ * g + j, j % 2
                        eng.wait_ge(s_pn, n + 1)
                        eng.wait_ge(s_ta, 2 * n + 1)
                        eng.wait_ge(s_x, g + 1)
                        eng.wait_ge(s_o, n + 1)
                        for k in range(2):
                            for c in range(DC):
                                ins = pe.transpose(banks[:, (T0, T1)[k], c * P:(c + 1) * P],
                                                   pr[u][:, c, k * P:(k + 1) * P], ident[:])
                            ins.then_inc(s_t, 1)
                        if after:
                            eng.wait_ge(s_v, 2 * n + 3)
                        pe.transpose(banks[0:DC, 0, 0:P], pr[u][:, :, S - 1], ident[:]).then_inc(s_t, 1)

                    def p_v(g, j):
                        n, u = SEQ * g + j, j % 2
                        eng.wait_ge(s_ta, 2 * n + 2 + LEAD)
                        eng.wait_ge(s_td, n + 1)
                        eng.wait_ge(s_v, 2 * n + 2)
                        eng.wait_ge(s_vld[u], 32 * g + 16 * (j // 2 + 1))
                        for c in range(DC):
                            cols = slice(c * P, (c + 1) * P)
                            for k in range(2):
                                pe.matmul(banks[:, T1, cols], v[u][:, k, cols], pt[:, k, cols], start=k == 0, stop=False)
                            ins = pe.matmul(banks[:, T1, cols], vlast[u][0:DC, cols], pt[0:DC, 2, 0:P], start=False,
                                            stop=True)
                        ins.then_inc(s_pv, 1)

                    def step(g, j, after, before=None):
                        n = SEQ * g + j
                        if after:
                            keys_values(n + 1, (j + 1) % 2, before)
                        turn(g, j, after)
                        if after:
                            scores(n + 1, (j + 1) % 2)
                        p_v(g, j)

                    def tile_out(g):
                        eng.wait_ge(s_ol, g + 1)
                        for c in range(DC):
                            ins = mm3(banks[:, T0, :], oh[:, c, :], ol[:, c, :], wo[0][:, c, :], wo[1][:, c, :],
                                      c == 0, c == DC - 1)
                        ins.then_inc(s_y, 1)

                    keys_values(0, 0)
                    scores(0, 0)
                    for j in range(SEQ):
                        step(0, j, True)
                    with pe.Fori(0, NT - 2) as g:
                        for j in range(SEQ):
                            step(g + 1, j, True, g if j == 0 else None)
                    for j in range(SEQ):
                        step(NT - 1, j, j < SEQ - 1, NT - 2 if j == 0 else None)
                    tile_out(NT - 1)

        stored = out.rearrange("(t p) d -> p t d", p=P)
        for stage in d.get("stages", "ABCDEF"):
            if stage == "A":
                cross_one_head()
            elif stage == "B":
                self_attention("sa", False)
                free_semaphores()
            elif stage == "C":
                plan = Plan(0)
                routing("ra", plan, "nc")
                experts("ea", plan, d["L0_units"])
                free_semaphores()
            elif stage == "D":
                cross_heads()
            elif stage == "E":
                self_attention("sb", True)
                free_semaphores()
            else:
                plan = Plan(1)
                routing("rb", plan, "nf")
                experts("eb", plan, d["L1_units"], stored)
            made.add("statistics")
        if stage != "F":
            s_out = sem("x_stored")
            with nc.Block() as block:
                @block.sync
                def _(eng):
                    eng.dma_start(stored, x[:]).then_inc(s_out, 16)
                    eng.wait_ge(s_out, 16)


def layouts(i):
    def t(w):
        return np.swapaxes(w, -1, -2)

    def units(up1, up2, down):
        def up(w):
            return w.reshape(-1, P, DC, P).transpose(0, 3, 2, 1).reshape(-1, P, D)
        dn = t(down).reshape(-1, P, D)
        return np.ascontiguousarray(np.stack([up(up1), up(up2), dn], axis=2))

    ctx = i["ctx_1024"]
    a = {
        "x": i["x"].reshape(T, D),
        "ctx": ctx,
        "ctxT": t(ctx).reshape(B, DC, P, S).transpose(0, 2, 1, 3),
        "ctxLast": ctx[:, S - 1, :],
        "ctxLastT": ctx[:, S - 1, :].T.reshape(DC, P, B).transpose(1, 0, 2),
        "L0_xattn_WkT": t(i["L0_xattn_Wk"]),
        "L0_attn_w_qkvT": t(i["L0_attn_w_qkv"]),
        "L0_attn_w_outT": t(i["L0_attn_w_out"]),
        "L0_ffn_gateT": t(i["L0_ffn_gate_w"]),
        "L0_units": units(np.concatenate([i["L0_ffn_w1"], i["L0_ffn_ws1"][None]]),
                          np.concatenate([i["L0_ffn_w3"], i["L0_ffn_ws3"][None]]),
                          np.concatenate([i["L0_ffn_w2"], i["L0_ffn_ws2"][None]])),
        "L1_attn_w64": np.concatenate([i["L1_attn_wq"], i["L1_attn_wk"], i["L1_attn_wv"], i["L1_attn_wv"]], axis=1),
        "L1_attn_fcqk": np.concatenate([i["L1_attn_fcq_w"], i["L1_attn_fck_w"]]),
        "L1_attn_fcvv": np.concatenate([i["L1_attn_fcv_w"], i["L1_attn_fcv_w"]]),
        "L1_ffn_gateT": t(i["L1_ffn_gate_w"]),
        "L1_units": units(i["L1_ffn_w12"][:, :I1], i["L1_ffn_w12"][:, I1:], i["L1_ffn_w3"]),
    }
    for name in ("L0_xattn_Wq", "L0_xattn_bq", "L0_xattn_bk", "L0_xattn_Wv", "L0_xattn_bv", "L0_attn_ln_gamma",
                 "L0_attn_ln_beta", "L0_attn_b_out", "L0_ffn_gate_bias", "L1_xattn_W_Q", "L1_xattn_b_Q",
                 "L1_xattn_W_K", "L1_xattn_b_K", "L1_xattn_W_V", "L1_xattn_b_V", "L1_xattn_W_O", "L1_xattn_b_O",
                 "L1_attn_fcq_b", "L1_attn_fck_b", "L1_attn_fcv_b", "L1_attn_fco_w", "L1_attn_fco_b"):
        a[name] = i[name]
    for name in ("L0_xattn_bq", "L0_xattn_bk", "L1_xattn_b_Q", "L1_xattn_b_K", "L1_attn_fcq_b", "L1_attn_fck_b"):
        a[name] = i[name].reshape(-1, P).T
    return {k: np.ascontiguousarray(v) for k, v in a.items()}


def kernel(**inputs):
    from concourse import bacc
    from concourse.bass_utils import run_bass_kernel_spmd

    arrays = layouts({k: np.asarray(v) for k, v in inputs.items()})
    nc = bacc.Bacc("TRN2", target_bir_lowering=False, num_devices=1)
    d = {k: nc.dram_tensor(f"in_{k}", v.shape, mybir.dt.from_np(v.dtype), kind="ExternalInput").ap()
         for k, v in arrays.items()}
    out = nc.dram_tensor("out_x", (T, D), F32, kind="ExternalOutput").ap()
    build(nc, d, out)
    r = run_bass_kernel_spmd(nc, [{f"in_{k}": v for k, v in arrays.items()}], core_ids=[0])
    return r.results[0]["out_x"].reshape(B, NQ, D)
```
